# Optimizing a Trainium2 kernel written in Bass

```python
import numpy as np
import jax
import jax.numpy as jnp

def _softmax(x, axis=-1):
    return jax.nn.softmax(x, axis=axis)

def _gelu(x):
    return jax.nn.gelu(x, approximate=True)

def _silu(x):
    return jax.nn.silu(x)

def _sigmoid(x):
    return jax.nn.sigmoid(x)

def _layernorm(x, axis=-1, eps=1e-05):
    m = jnp.mean(x, axis=axis, keepdims=True)
    v = jnp.var(x, axis=axis, keepdims=True)
    return (x - m) / jnp.sqrt(v + eps)

def _scatter_add(tgt, idx, src, axis=0):
    return tgt.at[idx].add(src)

def _segment_sum(src, seg, n):
    return jax.ops.segment_sum(src, seg, n)
kernel_name = 'mk_decoder_preln_d1_seqx_r2_39491d'

def setup_inputs(seed: int=0):
    np.random.seed(seed)
    _w = jnp.asarray

    def _rec_inputs():
        import jax
        import jax.numpy as jnp
        _rk = jax.random.key(seed)
        x = -0.0002928 + 1 * jax.random.normal(jax.random.fold_in(_rk, 1), (16, 512, 512), jnp.float32)
        _lenS = 512 - jax.random.randint(jax.random.fold_in(_rk, 7), (16,), 0, max(1, 512 // 4) + 1, jnp.int32)
        _lenS2 = 512 - jax.random.randint(jax.random.fold_in(_rk, 8), (16,), 0, max(1, 512 // 4) + 1, jnp.int32)
        _ctx_1024P = jax.random.normal(jax.random.fold_in(_rk, 11), (16, 16, 512), jnp.float32)
        _ctx_1024c = jax.random.dirichlet(jax.random.fold_in(_rk, 511), 0.3 * jnp.ones((16,), jnp.float32), (16, 512))
        _ctx_1024t = jnp.einsum('bsk,bkd->bsd', _ctx_1024c, _ctx_1024P)
        _ctx_1024t = _ctx_1024t * jax.lax.rsqrt(jnp.mean(jnp.square(_ctx_1024t)) + 1e-12) * 0.953939
        ctx_1024 = 2.81802e-05 + 1.00001 * (_ctx_1024t + 0.3 * jax.random.normal(jax.random.fold_in(_rk, 611), (16, 512, 512), jnp.float32))
        _validS = jnp.arange(512)[None, :] < _lenS[:, None]
        _validS2 = jnp.arange(512)[None, :] < _lenS2[:, None]
        _causal = jnp.tril(jnp.ones((512, 512), dtype=bool))
        mask_BxS2_bk0 = jnp.logical_not(jnp.broadcast_to(_validS2[:, :], (16, 512)))
        return (x, ctx_1024, mask_BxS2_bk0)
    x, ctx_1024, mask_BxS2_bk0 = _rec_inputs()

    def _L0_attn_setup():
        import jax, jax.numpy as jnp
        import numpy as np
        DIM = 512
        HEADS = 16
        HEAD_DIM = DIM // HEADS
        B, S = (4, 2048)
        key = jax.random.key(seed)
        ks = jax.random.split(key, 8)
        sc = 1.0 / np.sqrt(DIM)
        return {'x': jax.random.normal(ks[0], (B, S, DIM), dtype=jnp.float32), 'Wq': jax.random.normal(ks[1], (DIM, DIM), dtype=jnp.float32) * sc, 'Wk': jax.random.normal(ks[2], (DIM, DIM), dtype=jnp.float32) * sc, 'Wv': jax.random.normal(ks[3], (DIM, DIM), dtype=jnp.float32) * sc, 'Wp': jax.random.normal(ks[4], (DIM, DIM), dtype=jnp.float32) * sc, 'bp': jnp.zeros((DIM,), dtype=jnp.float32), 'conv_w': jax.random.normal(ks[5], (DIM, 3), dtype=jnp.float32) * (1.0 / np.sqrt(3.0)), 'conv_b': jnp.zeros((DIM,), dtype=jnp.float32)}
    _L0_attn_all = _L0_attn_setup()
    _L0_attn_in = {k: v for k, v in _L0_attn_all.items() if k in ('Wq', 'Wk', 'Wv', 'Wp', 'bp', 'conv_w', 'conv_b')}
    del _L0_attn_all

    def _L0_xattn_setup():
        import jax, jax.numpy as jnp
        import numpy as np
        NUM_HEADS, NUM_KV, HEAD_DIM, WIDTH = (4, 1, 128, 512)
        MASK_FILL = -2.3819763e+38

        def _apply_rope(x, positions, max_wavelength=10000.0):
            d = x.shape[-1]
            freq_exp = 2.0 / d * jnp.arange(d // 2, dtype=jnp.float32)
            timescale = max_wavelength ** freq_exp
            radians = positions[..., None].astype(jnp.float32) / timescale
            radians = radians[..., None, :]
            sin, cos = (jnp.sin(radians), jnp.cos(radians))
            x1, x2 = jnp.split(x, 2, axis=-1)
            out = jnp.concatenate([x1 * cos - x2 * sin, x2 * cos + x1 * sin], axis=-1)
            return out.astype(x.dtype)

        def _rmsnorm(x, scale):
            var = jnp.mean(jnp.square(x.astype(jnp.float32)), axis=-1, keepdims=True)
            normed = x * jax.lax.rsqrt(var + 1e-06)
            return (normed * (1 + scale)).astype(x.dtype)
        key = jax.random.key(seed)
        ks = jax.random.split(key, 7)
        B, T, S = (8, 256, 1024)
        return {'x': jax.random.normal(ks[0], (B, T, WIDTH), jnp.float32), 'mem_seq': jax.random.normal(ks[1], (B, S, WIDTH), jnp.float32), 'mem_mask': jax.random.randint(ks[2], (B, S), 0, 2).astype(bool), 'rms_scale': jax.random.normal(ks[3], (WIDTH,), jnp.float32) * 0.02, 'q_w': jax.random.normal(ks[4], (NUM_HEADS, WIDTH, HEAD_DIM), jnp.float32) / np.sqrt(WIDTH), 'kv_w': jax.random.normal(ks[5], (2, NUM_KV, WIDTH, HEAD_DIM), jnp.float32) / np.sqrt(WIDTH), 'out_w': jax.random.normal(ks[6], (NUM_HEADS, HEAD_DIM, WIDTH), jnp.float32) / np.sqrt(NUM_HEADS * HEAD_DIM)}
    _L0_xattn_all = _L0_xattn_setup()
    _L0_xattn_in = {k: v for k, v in _L0_xattn_all.items() if k in ('rms_scale', 'q_w', 'kv_w', 'out_w')}
    del _L0_xattn_all

    def _L0_ffn_setup():
        import jax, jax.numpy as jnp
        import numpy as np
        from jax import lax
        T, B, I, M, O = (128, 64, 512, 512, 512)

        def _xavier(key, shape):
            fan_out, fan_in = shape
            limit = float(np.sqrt(6.0 / (fan_in + fan_out)))
            return jax.random.uniform(key, shape, jnp.float32, -limit, limit)
        key = jax.random.key(seed)
        ks = jax.random.split(key, 9)
        x = jax.random.normal(ks[0], (T, B, I), jnp.float32)
        return {'x': x, 'wf': _xavier(ks[1], (M, I)), 'uf': _xavier(ks[2], (M, M)), 'bf': jnp.zeros((M,), jnp.float32), 'wi': _xavier(ks[3], (M, I)), 'ui': _xavier(ks[4], (M, M)), 'bi': jnp.zeros((M,), jnp.float32), 'wc': _xavier(ks[5], (M, I)), 'uc': _xavier(ks[6], (M, M)), 'bc': jnp.zeros((M,), jnp.float32), 'wo': _xavier(ks[7], (O, I)), 'uo': _xavier(ks[8], (O, M)), 'bo': jnp.zeros((O,), jnp.float32), 'in_c': jnp.zeros((M,), jnp.float32)}
    _L0_ffn_all = _L0_ffn_setup()
    _L0_ffn_in = {k: v for k, v in _L0_ffn_all.items() if k in ('wf', 'uf', 'bf', 'wi', 'ui', 'bi', 'wc', 'uc', 'bc', 'wo', 'uo', 'bo', 'in_c')}
    del _L0_ffn_all
    return {'x': x, 'ctx_1024': ctx_1024, 'mask_BxS2_bk0': mask_BxS2_bk0, 'L0_attn_Wq': _L0_attn_in['Wq'], 'L0_attn_Wk': _L0_attn_in['Wk'], 'L0_attn_Wv': _L0_attn_in['Wv'], 'L0_attn_Wp': _L0_attn_in['Wp'], 'L0_attn_bp': _L0_attn_in['bp'], 'L0_attn_conv_w': _L0_attn_in['conv_w'], 'L0_attn_conv_b': _L0_attn_in['conv_b'], 'L0_xattn_rms_scale': _L0_xattn_in['rms_scale'], 'L0_xattn_q_w': _L0_xattn_in['q_w'], 'L0_xattn_kv_w': _L0_xattn_in['kv_w'], 'L0_xattn_out_w': _L0_xattn_in['out_w'], 'L0_ffn_wf': _L0_ffn_in['wf'], 'L0_ffn_uf': _L0_ffn_in['uf'], 'L0_ffn_bf': _L0_ffn_in['bf'], 'L0_ffn_wi': _L0_ffn_in['wi'], 'L0_ffn_ui': _L0_ffn_in['ui'], 'L0_ffn_bi': _L0_ffn_in['bi'], 'L0_ffn_wc': _L0_ffn_in['wc'], 'L0_ffn_uc': _L0_ffn_in['uc'], 'L0_ffn_bc': _L0_ffn_in['bc'], 'L0_ffn_wo': _L0_ffn_in['wo'], 'L0_ffn_uo': _L0_ffn_in['uo'], 'L0_ffn_bo': _L0_ffn_in['bo'], 'L0_ffn_in_c': _L0_ffn_in['in_c']}

def reference(x, ctx_1024, mask_BxS2_bk0, L0_attn_Wq, L0_attn_Wk, L0_attn_Wv, L0_attn_Wp, L0_attn_bp, L0_attn_conv_w, L0_attn_conv_b, L0_xattn_rms_scale, L0_xattn_q_w, L0_xattn_kv_w, L0_xattn_out_w, L0_ffn_wf, L0_ffn_uf, L0_ffn_bf, L0_ffn_wi, L0_ffn_ui, L0_ffn_bi, L0_ffn_wc, L0_ffn_uc, L0_ffn_bc, L0_ffn_wo, L0_ffn_uo, L0_ffn_bo, L0_ffn_in_c):
    import jax
    import jax.numpy as jnp

    def _L0_attn_ref(x, Wq, Wk, Wv, Wp, bp, conv_w, conv_b):
        import jax, jax.numpy as jnp
        import numpy as np
        DIM = 512
        HEADS = 16
        HEAD_DIM = DIM // HEADS
        B, S = (4, 2048)
        b, s, d = x.shape

        def split_heads(t):
            return t.reshape(b, s, HEADS, HEAD_DIM).transpose(0, 2, 1, 3)
        q = split_heads(x @ Wq.T)
        k = split_heads(x @ Wk.T)
        v = split_heads(x @ Wv.T)
        q = jax.nn.elu(q) + 1.0
        k = jax.nn.elu(k) + 1.0
        kv_state = jnp.einsum('bhnd,bhne->bhde', k, v)
        k_state = k.sum(axis=2)
        attn_out = jnp.einsum('bhnd,bhde->bhne', q, kv_state)
        denom = jnp.maximum(jnp.einsum('bhnd,bhd->bhn', q, k_state), 1e-06)[..., None]
        attn_out = (attn_out / denom).transpose(0, 2, 1, 3).reshape(b, s, d)
        xp = jnp.pad(x, ((0, 0), (1, 1), (0, 0)))
        local = xp[:, :-2, :] * conv_w[:, 0] + xp[:, 1:-1, :] * conv_w[:, 1] + xp[:, 2:, :] * conv_w[:, 2] + conv_b
        return (attn_out + local) @ Wp.T + bp

    def _L0_xattn_ref(x, mem_seq, mem_mask, rms_scale, q_w, kv_w, out_w):
        import jax, jax.numpy as jnp
        import numpy as np
        NUM_HEADS, NUM_KV, HEAD_DIM, WIDTH = (4, 1, 128, 512)
        MASK_FILL = -2.3819763e+38

        def _apply_rope(x, positions, max_wavelength=10000.0):
            d = x.shape[-1]
            freq_exp = 2.0 / d * jnp.arange(d // 2, dtype=jnp.float32)
            timescale = max_wavelength ** freq_exp
            radians = positions[..., None].astype(jnp.float32) / timescale
            radians = radians[..., None, :]
            sin, cos = (jnp.sin(radians), jnp.cos(radians))
            x1, x2 = jnp.split(x, 2, axis=-1)
            out = jnp.concatenate([x1 * cos - x2 * sin, x2 * cos + x1 * sin], axis=-1)
            return out.astype(x.dtype)

        def _rmsnorm(x, scale):
            var = jnp.mean(jnp.square(x.astype(jnp.float32)), axis=-1, keepdims=True)
            normed = x * jax.lax.rsqrt(var + 1e-06)
            return (normed * (1 + scale)).astype(x.dtype)
        B, S, _ = mem_seq.shape
        T = x.shape[1]
        G = NUM_HEADS // NUM_KV
        xn = _rmsnorm(x, rms_scale)
        mn = _rmsnorm(mem_seq, rms_scale)
        q = jnp.einsum('BTD,NDH->BTNH', xn, q_w)
        kv = jnp.einsum('BSD,cKDH->cBSKH', mn, kv_w)
        k, v = (kv[0], kv[1])
        q_pos = jnp.broadcast_to(jnp.arange(S, T + S), (B, T))
        k_pos = jnp.broadcast_to(jnp.arange(S), (B, S))
        q = _apply_rope(q, q_pos) * HEAD_DIM ** (-0.5)
        k = _apply_rope(k, k_pos)
        q = q.reshape(B, T, NUM_KV, G, HEAD_DIM)
        logits = jnp.einsum('BTKGH,BSKH->BKGTS', q, k, preferred_element_type=jnp.float32)
        masked = jnp.where(mem_mask[:, None, None, None, :], logits, MASK_FILL)
        probs = jax.nn.softmax(masked, axis=-1).astype(x.dtype)
        enc = jnp.einsum('BKGTS,BSKH->BTKGH', probs, v).reshape(B, T, NUM_HEADS, HEAD_DIM)
        return jnp.einsum('BTNH,NHD->BTD', enc, out_w)

    def _L0_ffn_ref(x, wf, uf, bf, wi, ui, bi, wc, uc, bc, wo, uo, bo, in_c):
        import jax, jax.numpy as jnp
        import numpy as np
        from jax import lax
        T, B, I, M, O = (128, 64, 512, 512, 512)

        def _xavier(key, shape):
            fan_out, fan_in = shape
            limit = float(np.sqrt(6.0 / (fan_in + fan_out)))
            return jax.random.uniform(key, shape, jnp.float32, -limit, limit)
        batch = x.shape[1]
        c0 = jnp.broadcast_to(in_c, (batch, in_c.shape[0]))

        def step(c, xt):
            ft = jax.nn.sigmoid(xt @ wf.T + c @ uf.T + bf)
            it = jax.nn.sigmoid(xt @ wi.T + c @ ui.T + bi)
            gt = jnp.tanh(xt @ wc.T + c @ uc.T + bc)
            c = ft * c + it * gt
            return (c, None)
        c_final, _ = lax.scan(step, c0, x)
        h = jnp.tanh(jnp.einsum('tbi,oi->tbo', x, wo) + c_final @ uo.T + bo)
        return h
    x = x + _L0_attn_ref(_layernorm(x, axis=-1), L0_attn_Wq, L0_attn_Wk, L0_attn_Wv, L0_attn_Wp, L0_attn_bp, L0_attn_conv_w, L0_attn_conv_b)
    x = x + _L0_xattn_ref(_layernorm(x, axis=-1), ctx_1024, mask_BxS2_bk0, L0_xattn_rms_scale, L0_xattn_q_w, L0_xattn_kv_w, L0_xattn_out_w)
    x = x + _L0_ffn_ref(_layernorm(x, axis=-1), L0_ffn_wf, L0_ffn_uf, L0_ffn_bf, L0_ffn_wi, L0_ffn_ui, L0_ffn_bi, L0_ffn_wc, L0_ffn_uc, L0_ffn_bc, L0_ffn_wo, L0_ffn_uo, L0_ffn_bo, L0_ffn_in_c)
    return x

_drawn_inputs = setup_inputs


def setup_inputs(seed=0):
    import zlib

    import numpy as np

    out = dict(_drawn_inputs(seed))
    spreads = {'L0_attn_bp': (0.0, 0.1),
     'L0_attn_conv_b': (0.0, 0.1),
     'L0_ffn_bf': (0.0, 0.8),
     'L0_ffn_bi': (0.0, 0.8),
     'L0_ffn_bc': (0.0, 0.1),
     'L0_ffn_bo': (0.0, 0.1),
     'L0_ffn_in_c': (0.0, 0.8)}
    factors = {'L0_attn_Wq': 8.0, 'L0_attn_Wk': 8.0, 'L0_xattn_rms_scale': 7.095}
    for name, (base, spread) in spreads.items():
        noise = np.random.default_rng([zlib.crc32(name.encode()), seed]).standard_normal(out[name].shape)
        drawn = base * np.exp(spread * noise) if base else spread * noise
        out[name] = jnp.asarray(drawn.astype(out[name].dtype))
    for name, factor in factors.items():
        out[name] = (out[name] * factor).astype(out[name].dtype)
    return out
```

```python
from contextlib import ExitStack

import numpy as np
import concourse.bass as bass
from concourse import mybir

F32 = mybir.dt.float32
F32R = mybir.dt.float32r
U8 = mybir.dt.uint8
ALU = mybir.AluOpType
ACT = mybir.ActivationFunctionType
P = 128


class Scope(ExitStack):

    def __init__(self, nc):
        super().__init__()
        self.nc, self.semaphores = nc, []

    def __exit__(self, *error):
        super().__exit__(*error)
        if self.semaphores and error[0] is None:
            self.nc.clear_and_free_semaphores(self.semaphores)
            self.nc.all_engine_barrier()


class Event:

    def __init__(self, ctx, nc, name, per=1, unit=1):
        self.sem, self.per, self.unit = nc.alloc_semaphore(name), per, unit
        ctx.semaphores.append(self.sem)

    def on(self, instruction):
        instruction.then_inc(self.sem, self.unit)

    def wait(self, engine, b, k=None):
        k = self.per - 1 if k is None else k
        if isinstance(b, int) and b < 0:
            return
        engine.wait_ge(self.sem, (b * self.per + k + 1) * self.unit)


class Ring:

    def __init__(self, banks, frees):
        self.banks, self.frees = banks, frees
        assert len(frees) % len(banks) == 0

    def take(self, engine, b, n):
        prev = n - len(self.banks)
        event, k = self.frees[prev]
        event.wait(engine, b if prev >= 0 else b - 1, k)
        return self.banks[n % len(self.banks)]


class Item:

    def __init__(self, b, par):
        self.b, self.par = b, par


def pipeline(engine, B, step, unroll=2):
    at = lambda base, i: Item(base + i, i % unroll)
    turns = (B - 3) // unroll
    step(Item(0, 0), None)
    step(at(0, 1), at(0, 0))
    with engine.Fori(0, turns) as j:
        for i in range(unroll):
            step(at(unroll * j, i + 2), at(unroll * j, i + 1))
    for b in range(unroll * turns + 2, B):
        step(at(0, b), at(0, b - 1))
    step(None, at(0, B - 1))


def following(new, B):
    return new is not None and not (isinstance(new.b, int) and new.b == B - 1)


class Split:

    def __init__(self, high, low):
        self.high, self.low = high, low

    def __getitem__(self, at):
        return Split(self.high[at], self.low[at])

    def high_f32(self):
        return self.high.bitcast(F32)


def product(pe, out, stationary, moving, first, last):
    pe.matmul(out, stationary.high, moving.high, start=first, stop=False)
    pe.matmul(out, stationary.high, moving.low, start=False, stop=False)
    return pe.matmul(out, stationary.low, moving.high, start=False, stop=last)


class Kernel:
    def __init__(self, nc, io, out, scratch1, scratch2):
        self.nc, self.io, self.out, self.x1, self.x2 = nc, io, out, scratch1, scratch2
        self.B, self.S, self.D = io["x"].shape
        self.C = self.D // P
        self.T = self.S // P

    def sb(self, ctx, name, shape, dtype=F32):
        return ctx.enter_context(self.nc.sbuf_tensor(name, shape, dtype))

    def split(self, ctx, name, shape):
        return Split(self.sb(ctx, name + "_hi", shape, F32R), self.sb(ctx, name + "_lo", shape, F32R))

    def banks(self, ctx, name, n):
        return [ctx.enter_context(self.nc.psum_tensor(f"{name}{i}", [P, 512], F32)) for i in range(n)]

    def load_weights(self, tag, jobs, rms_scale=None):
        nc, C, D = self.nc, self.C, self.D
        with Scope(self.nc) as ctx:
            sb = lambda n, s, d=F32: self.sb(ctx, f"{tag}_{n}", s, d)
            stage = [sb(f"stage{i}", [P, C, D]) for i in range(2)]
            scale = sb("scale", [P, C])
            banks = self.banks(ctx, f"{tag}_pw", 4)
            ev = lambda n, per=1, unit=1: Event(ctx, nc, f"{tag}_{n}", per, unit)
            loaded = [ev(f"loaded{i}", 1 if j[0] == "turn" else len(j[1]), 16) for i, j in enumerate(jobs)]
            scaled, turned, high, low = ev("scaled", C), ev("turned", C), ev("high", C), ev("low", C)
            scale_in, scale_one = ev("scale_in", 1, 16), ev("scale_one")
            block = ctx.enter_context(nc.Block())
            before = [sum(j[0] == jobs[i][0] for j in jobs[:i]) for i in range(len(jobs))]

            @block.sync
            def _(sp):
                if rms_scale is not None:
                    with nc.allow_non_contiguous_dma(reason="512 words once"):
                        scale_in.on(sp.dma_start(scale[:, :], rms_scale.rearrange("(c p) -> p c", p=P)))
                for i, (kind, parts, n, w) in enumerate(jobs):
                    low.wait(sp, i - 2)
                    if kind == "turn":
                        parts = [(parts.rearrange("(c p) n -> p c n", p=P), 0)]
                    for view, at in parts:
                        loaded[i].on(sp.dma_start(stage[i % 2][:, :, at:at + view.shape[2]], view))

            @block.tensor
            def _(pe):
                for i, (kind, parts, n, w) in enumerate(jobs):
                    if kind != "turn":
                        continue
                    loaded[i].wait(pe, 0)
                    for c in range(C):
                        if i >= 1:
                            low.wait(pe, i - 1, c)
                        for o in range(C):
                            mm = pe.transpose(banks[c][:, o * P:(o + 1) * P],
                                              stage[i % 2][:, o, c * P:(c + 1) * P], self.ident[:, :])
                        turned.on(mm)

            def source(i, c):
                kind, parts, n, w = jobs[i]
                return banks[c][:, 0:n] if kind == "turn" else stage[i % 2][:, c, 0:n]

            def ready(engine, i, c):
                if jobs[i][0] == "turn":
                    turned.wait(engine, before[i], c)
                elif jobs[i][0] == "scale":
                    scaled.wait(engine, before[i], c)
                else:
                    loaded[i].wait(engine, 0)

            @block.scalar
            def _(act):
                for i, (kind, parts, n, w) in enumerate(jobs):
                    for c in range(C):
                        ready(act, i, c)
                        high.on(act.activation(w.high[:, c, 0:n], source(i, c), ACT.Copy))

            @block.vector
            def _(dve):
                if rms_scale is not None:
                    scale_in.wait(dve, 0)
                    scale_one.on(dve.tensor_scalar(scale[:, :], scale[:, :], 1.0, None, ALU.add))
                    scale_one.wait(dve, 0)
                for i, (kind, parts, n, w) in enumerate(jobs):
                    if kind == "scale":
                        loaded[i].wait(dve, 0)
                        for c in range(C):
                            scaled.on(dve.tensor_scalar(stage[i % 2][:, c, 0:n], stage[i % 2][:, c, 0:n],
                                                        scale[:, c:c + 1], None, ALU.mult))
                    for c in range(C):
                        ready(dve, i, c)
                        high.wait(dve, i, c)
                        low.on(dve.tensor_tensor(w.low[:, c, 0:n], source(i, c),
                                                 w[:, c, 0:n].high_f32(), ALU.subtract))

    def norm_events(self, ctx, tag):
        e = lambda n, per=1, unit=1: Event(ctx, self.nc, f"{tag}_{n}", per, unit)

        class N:
            loaded = e("loaded", 1, 16)
            stats, moments, variance, rstd, normed = e("stats", self.T), e("moments", self.T), e("var"), e("rstd"), e("normed", self.T)
            carrier = self.sb(ctx, f"{tag}_carrier", [P, 1])
            st = self.sb(ctx, f"{tag}_st", [P, self.T, 6])
            mv = self.sb(ctx, f"{tag}_mv", [P, self.T, 2])
            var_eps = self.sb(ctx, f"{tag}_ve", [P, self.T])
            scale = self.sb(ctx, f"{tag}_sc", [P, self.T])
        return N

    def norm_stats(self, dve, N, b, x):
        N.loaded.wait(dve, b)
        for t in range(self.T):
            N.stats.on(dve.bn_stats(N.st[:, t, :], x[:, t, :]))
        N.stats.wait(dve, b)
        dve.memset(N.carrier[:, :], 0.0)
        for t in range(self.T):
            N.moments.on(dve.bn_aggr(N.mv[:, t, :], N.st[:, t, :]))
        N.moments.wait(dve, b)
        N.variance.on(dve.tensor_scalar(N.var_eps[:, :], N.mv[:, :, 1], 1e-5, None, ALU.add))

    def norm_power(self, pool, N, b):
        N.variance.wait(pool, b)
        N.normed.wait(pool, b - 1)
        N.rstd.on(pool.tensor_tensor(N.scale[:, :], N.var_eps[:, :], self.minus_half[:, 0:self.T], ALU.pow))

    def norm_apply(self, dve, N, b, x, scale, scale_event, out=None):
        scale_event.wait(dve, b)
        for t in range(self.T):
            N.normed.on(dve.tensor_scalar((out or x)[:, t, :], x[:, t, :], N.mv[:, t, 0:1], scale[:, t:t + 1],
                                          ALU.subtract, ALU.mult))

    def turn(self, pe, bank, src, c):
        for t in range(self.T):
            mm = pe.transpose(bank[:, t * P:(t + 1) * P], src[:, t, c * P:(c + 1) * P], self.ident[:, :])
        return mm

    def token_rows(self, dram, b):
        return dram[b, :, :].rearrange("(t p) d -> p t d", p=P)

    def constants(self, ctx):
        nc = self.nc
        self.ident = self.sb(ctx, "ident", [P, P])
        self.minus_half = self.sb(ctx, "minus_half", [P, 4])
        with Scope(self.nc) as c:
            zero = Event(c, nc, "ident_zero")
            block = c.enter_context(nc.Block())

            @block.gpsimd
            def _(pool):
                pool.memset(self.minus_half[:, :], -0.5)
                zero.on(pool.memset(self.ident[:, :], 0.0))
                zero.wait(pool, 0)
                pool.affine_select(out=self.ident[:, :], in_=self.ident[:, :], compare_op=ALU.not_equal,
                                   fill=1.0, base=0, pattern=[[-1, P]], channel_multiplier=1)

    def phase_a(self):
        nc, io, B, C, T, D, S = self.nc, self.io, self.B, self.C, self.T, self.D, self.S
        HEADS = 16
        HD = D // HEADS
        HC = P // HD
        KVW = P + HEADS
        with Scope(self.nc) as ctx:
            w = {n: self.split(ctx, f"a_{n}", [P, C, D]) for n in ("Wq", "Wk", "Wv", "Wp")}
            self.load_weights("aw", [("turn", io[f"L0_attn_{n}"], D, w[n]) for n in w])
            sb = lambda n, s, d=F32: self.sb(ctx, f"a_{n}", s, d)
            ev = lambda n, per=1, unit=1: Event(ctx, nc, f"a_{n}", per, unit)
            x = sb("x", [P, T, D])
            xT = self.split(ctx, "a_xT", [P, C, S])
            k = sb("k", [P, T, D])
            v1 = sb("v1", [P, T, C, P + 2])
            q = [self.split(ctx, f"a_q{i}", [P, C, S]) for i in range(2)]
            local = [sb(f"local{i}", [P, C, S]) for i in range(2)]
            kv = [self.split(ctx, f"a_kv{i}", [P, C * KVW + P - HEADS]) for i in range(2)]
            z = self.split(ctx, "a_z", [P, C, S])
            res = sb("res", [P, T, D])
            elu = sb("elu", [P, 2, D])
            kv_f = elu[:, :, :].rearrange("p a d -> p (a d)")[:, 0:C * KVW].rearrange("p (c e) -> p c e", c=C)
            rden = sb("rden", [HEADS, S])
            rden_s = self.split(ctx, "a_rdens", [HEADS, S])
            att = [sb(f"att{i}", [P, S]) for i in range(2)]
            head_rows = sb("head_rows", [HEADS, C, P], F32R)
            kv_mask = sb("kv_mask", [P, 2, P])
            head_mask = sb("head_mask", [P, C, HEADS])
            bp = sb("bp", [P, D])
            conv_w = sb("conv_w", [P, C, 3])
            conv_b = sb("conv_b", [P, C])
            N = self.norm_events(ctx, "a_ln")
            params = ev("params", 3, 16)
            built = ev("built", 11)
            xT_ps, xT_hi, xT_lo = ev("xT_ps", C), ev("xT_hi", C), ev("xT_lo", C)
            tap1, tap0, tap2 = ev("tap1", C), ev("tap0", C), ev("tap2", C)
            kq_ps, v_ps = ev("kq_ps", T + C), ev("v_ps", T)
            elu_neg, elu_exp, elu_out = ev("elu_neg", T + C), ev("elu_exp", T + C), ev("elu_out", T + C)
            q_hi, q_lo, v_sb = ev("q_hi", C), ev("q_lo", C), ev("v_sb", T)
            kv_ps, kv_part, kv_hi, kv_lo = ev("kv_ps", 2), ev("kv_part", 6), ev("kv_hi"), ev("kv_lo")
            den_ps, den_max, rden_f, rden_hi, rden_lo = ev("den_ps"), ev("den_max"), ev("rden_f"), ev("rden_hi"), ev("rden_lo")
            spread_ps, spread_sb, att_ps, att_sb = ev("spread_ps", C), ev("spread_sb", C), ev("att_ps", C), ev("att_sb", C)
            z_f, z_hi, z_lo = ev("z_f", C), ev("z_hi", C), ev("z_lo", C)
            out_ps, res_bp, x1_sb = ev("out_ps", T), ev("res_bp", T), ev("x1_sb", T)
            res_in, stored = ev("res_in", 1, 16), ev("stored", 1, 16)
            first = Ring(self.banks(ctx, "a_p", 3),
                         [(tap2, c) for c in range(C)] + [(elu_out, t) for t in range(T)]
                         + [(v_sb, t) for t in range(T)] + [(elu_out, T + c) for c in range(C)]
                         + [(kv_part, 2), (kv_part, 5)])
            second = Ring(self.banks(ctx, "a_r", 4),
                          [e for c in range(C) for e in ((spread_sb, c), (att_sb, c))] + [(x1_sb, t) for t in range(T)])
            den_bank = self.banks(ctx, "a_den", 1)[0]
            block = ctx.enter_context(nc.Block())

            @block.sync
            def _(sp):
                with nc.allow_non_contiguous_dma(reason="small parameters, once"):
                    params.on(sp.dma_start(conv_w[:, :, :], io["L0_attn_conv_w"].rearrange("(c p) k -> p c k", p=P)))
                    params.on(sp.dma_start(conv_b[:, :], io["L0_attn_conv_b"].rearrange("(c p) -> p c", p=P)))
                    params.on(sp.dma_start(bp[:, :], io["L0_attn_bp"].rearrange("(a n) -> a n", a=1).to_broadcast([P, D])))

                def load(b):
                    xT_ps.wait(sp, b - 1)
                    N.loaded.on(sp.dma_start(x[:, :, :], self.token_rows(io["x"], b)))
                load(0)

                def step(new, old):
                    if old:
                        stored.wait(sp, old.b - 1)
                        res_in.on(sp.dma_start(res[:, :, :], self.token_rows(io["x"], old.b)))
                    if following(new, B):
                        load(new.b + 1)
                    if old:
                        x1_sb.wait(sp, old.b)
                        stored.on(sp.dma_start(self.token_rows(self.x1, old.b), res[:, :, :]))
                pipeline(sp, B, step)
                stored.wait(sp, B - 1)

            @block.gpsimd
            def _(pool):
                keep = lambda ap, base, pattern, mult: pool.affine_select(
                    out=ap, in_=ap, compare_op=ALU.is_ge, fill=0.0, base=base, pattern=pattern, channel_multiplier=mult)
                built.on(pool.memset(kv_mask[:, :, :], 1.0))
                built.on(pool.memset(head_mask[:, :, :], 1.0))
                built.on(pool.memset(head_rows[:, :, :].bitcast(F32), 1.0))
                built.on(pool.memset(v1[:, :, :, :], 1.0))
                for i in range(2):
                    pool.memset(kv[i].high[:, :].bitcast(F32), 0.0)
                    last = pool.memset(kv[i].low[:, :].bitcast(F32), 0.0)
                built.on(last)
                built.wait(pool, 0, 4)
                km = kv_mask[:, :, :].rearrange("p a (h e) -> p a h e", h=HC)
                built.on(keep(km, 0, [[0, 2], [-HD, HC], [0, HD]], 1))
                built.on(keep(head_mask[:, :, :], 0, [[HC * HD, C], [-HD, HEADS]], 1))
                hr = head_rows[:, :, :].rearrange("h c (a e) -> h c a e", a=HC)
                built.on(keep(hr, 0, [[-HC, C], [-1, HC], [0, HD]], 1))
                built.wait(pool, 0, 7)
                built.on(keep(km, HD - 1, [[0, 2], [HD, HC], [0, HD]], -1))
                built.on(keep(head_mask[:, :, :], HD - 1, [[-HC * HD, C], [HD, HEADS]], -1))
                built.on(keep(hr, 0, [[HC, C], [1, HC], [0, HD]], -1))
                params.wait(pool, 0)
                self.norm_power(pool, N, 0)

                def step(new, old):
                    if old:
                        res_in.wait(pool, old.b)
                        for t in range(T):
                            res_bp.on(pool.tensor_tensor(res[:, t, :], res[:, t, :], bp[:, :], ALU.add))
                        for c in range(C):
                            att_sb.wait(pool, old.b, c)
                            z_f.on(pool.tensor_tensor(att[c % 2][:, :], att[c % 2][:, :], local[old.par][:, c, :], ALU.add))
                    if following(new, B):
                        self.norm_power(pool, N, new.b + 1)
                    if new:
                        for c in range(C):
                            q_hi.wait(pool, new.b, c)
                            q_lo.on(pool.tensor_tensor(q[new.par].low[:, c, :], elu[:, c % 2, :],
                                                       q[new.par][:, c, :].high_f32(), ALU.subtract))
                pipeline(pool, B, step)

            @block.scalar
            def _(act):
                params.wait(act, 0)
                built.wait(act, 0)

                def step(new, old):
                    def elu_front(u):
                        kq_ps.wait(act, new.b, u)
                        if u < 2:
                            kv_lo.wait(act, new.b - 1)
                        elif u - 2 < T:
                            elu_out.wait(act, new.b, u - 2)
                        else:
                            q_lo.wait(act, new.b, u - 2 - T)
                        bank = first.banks[(C + u if u < T else C + T + u) % 3]
                        elu_neg.on(act.activation(elu[:, u % 2, :], bank[:, :], ACT.Relu, scale=-1.0))
                        elu_neg.wait(act, new.b, u)
                        elu_exp.on(act.activation(elu[:, u % 2, :], elu[:, u % 2, :], ACT.Exp, scale=-1.0))

                    def q_high(c):
                        elu_out.wait(act, new.b, T + c)
                        q_hi.on(act.activation(q[new.par].high[:, c, :], elu[:, c % 2, :], ACT.Copy))

                    def spread_copy(c):
                        spread_ps.wait(act, old.b, c)
                        z_lo.wait(act, old.b if c >= 2 else old.b - 1, c - 2 if c >= 2 else C + c - 2)
                        spread_sb.on(act.activation(att[c % 2][:, :], second.banks[2 * c % 4][:, :], ACT.Copy))

                    def z_high(c):
                        z_f.wait(act, old.b, c)
                        if c == 0:
                            out_ps.wait(act, old.b - 1)
                        z_hi.on(act.activation(z.high[:, c, :], att[c % 2][:, :], ACT.Copy))

                    if new:
                        for c in range(C):
                            xT_ps.wait(act, new.b, c)
                            if c == 0:
                                kq_ps.wait(act, new.b - 1)
                            bank = first.banks[c % 3]
                            xT_hi.on(act.activation(xT.high[:, c, :], bank[:, :], ACT.Copy))
                            tap1.on(act.activation(local[new.par][:, c, :], bank[:, :], ACT.Identity,
                                                   bias=conv_b[:, c:c + 1], scale=conv_w[:, c, 1:2]))
                        for u in range(T):
                            elu_front(u)
                    if old:
                        rden_f.wait(act, old.b)
                        spread_ps.wait(act, old.b - 1)
                        rden_hi.on(act.activation(rden_s.high[:, :], rden[:, :], ACT.Copy))
                        for c in range(C):
                            spread_copy(c)
                            if c >= 1:
                                z_high(c - 1)
                        z_high(C - 1)
                    if new:
                        for t in range(T):
                            v_ps.wait(act, new.b, t)
                            if t == 0:
                                kv_ps.wait(act, new.b - 1)
                            v_sb.on(act.activation(v1[:, t, :, 0:P],
                                                   first.banks[(C + T + t) % 3][:, :].rearrange("p (c e) -> p c e", c=C), ACT.Copy))
                        for c in range(C):
                            elu_front(T + c)
                            if c >= 1:
                                q_high(c - 1)
                        q_high(C - 1)
                        for g in range(2):
                            kv_part.wait(act, new.b, 3 * g + 2)
                        kv_hi.on(act.activation(kv[new.par].high[:, 0:C * KVW].rearrange("p (c e) -> p c e", c=C),
                                                kv_f, ACT.Copy))
                pipeline(act, B, step)

            @block.vector
            def _(dve):
                params.wait(dve, 0)
                built.wait(dve, 0)
                self.norm_stats(dve, N, 0, x)
                self.norm_apply(dve, N, 0, x, N.scale, N.rstd)

                def step(new, old):
                    def elu_back(u):
                        elu_exp.wait(dve, new.b, u)
                        bank = first.banks[(C + u if u < T else C + T + u) % 3]
                        if u < T:
                            if u == 0:
                                kv_ps.wait(dve, new.b - 1)
                            dst = k[:, u, :]
                        else:
                            c = u - T
                            dst = elu[:, c % 2, :]
                        elu_out.on(dve.scalar_tensor_tensor(out=dst, in0=bank[:, :], scalar=0.0, in1=elu[:, u % 2, :],
                                                            op0=ALU.max, op1=ALU.add))

                    if new:
                        for c in range(C):
                            tap1.wait(dve, new.b, c)
                            bank, loc = first.banks[c % 3], local[new.par]
                            xT_lo.on(dve.tensor_tensor(xT.low[:, c, :], bank[:, :], xT[:, c, :].high_f32(), ALU.subtract))
                            tap0.on(dve.scalar_tensor_tensor(out=loc[:, c, 1:S], in0=bank[:, 0:S - 1], scalar=conv_w[:, c, 0:1],
                                                             in1=loc[:, c, 1:S], op0=ALU.mult, op1=ALU.add))
                            tap0.wait(dve, new.b, c)
                            tap2.on(dve.scalar_tensor_tensor(out=loc[:, c, 0:S - 1], in0=bank[:, 1:S], scalar=conv_w[:, c, 2:3],
                                                             in1=loc[:, c, 0:S - 1], op0=ALU.mult, op1=ALU.add))
                    if old:
                        den_ps.wait(dve, old.b)
                        den_max.on(dve.tensor_scalar(rden[:, :], den_bank[0:HEADS, :], 1e-6, None, ALU.max))
                        den_max.wait(dve, old.b)
                        rden_f.on(dve.reciprocal(rden[:, :], rden[:, :]))
                    if new:
                        for u in range(T):
                            elu_back(u)
                    if old:
                        rden_hi.wait(dve, old.b)
                        rden_lo.on(dve.tensor_tensor(rden_s.low[:, :], rden[:, :], rden_s[:, :].high_f32(), ALU.subtract))

                        def z_low(c):
                            z_hi.wait(dve, old.b, c)
                            z_lo.on(dve.tensor_tensor(z.low[:, c, :], att[c % 2][:, :], z[:, c, :].high_f32(), ALU.subtract))
                        for c in range(C):
                            spread_sb.wait(dve, old.b, c)
                            att_ps.wait(dve, old.b, c)
                            att_sb.on(dve.tensor_tensor(att[c % 2][:, :], second.banks[(2 * c + 1) % 4][:, :], att[c % 2][:, :], ALU.mult))
                            if c >= 1:
                                z_low(c - 1)
                        z_low(C - 1)
                    if following(new, B):
                        self.norm_stats(dve, N, new.b + 1, x)
                        self.norm_apply(dve, N, new.b + 1, x, N.scale, N.rstd)
                    if new:
                        for c in range(C):
                            elu_back(T + c)
                    if new:
                        q_lo.wait(dve, new.b)
                        for g in range(2):
                            kv_ps.wait(dve, new.b, g)
                            bank = first.banks[(2 * C + 2 * T + g) % 3][:, 0:2 * (P + 2)].rearrange("p (c e) -> p c e", c=2)
                            kv_part.on(dve.tensor_tensor(kv_f[:, 2 * g:2 * g + 2, 0:P], bank[:, :, 0:P], kv_mask[:, :, :], ALU.mult))
                            for i in range(2):
                                kv_part.on(dve.tensor_scalar(kv_f[:, 2 * g + i, P:KVW], head_mask[:, 2 * g + i, :],
                                                             bank[:, i, P:P + 1], None, ALU.mult))
                        kv_hi.wait(dve, new.b)
                        kv_part.wait(dve, new.b)
                        both = lambda ap: ap[:, 0:C * KVW].rearrange("p (c e) -> p c e", c=C)
                        kv_lo.on(dve.tensor_tensor(both(kv[new.par].low), kv_f, both(kv[new.par].high).bitcast(F32), ALU.subtract))
                    if old:
                        for t in range(T):
                            res_bp.wait(dve, old.b, t)
                            out_ps.wait(dve, old.b, t)
                            x1_sb.on(dve.tensor_tensor(res[:, t, :], second.banks[(2 * C + t) % 4][:, :], res[:, t, :], ALU.add))
                pipeline(dve, B, step)

            @block.tensor
            def _(pe):
                built.wait(pe, 0)

                def step(new, old):
                    if new:
                        for c in range(C):
                            bank = first.take(pe, new.b, c)
                            if c == 0:
                                N.normed.wait(pe, new.b)
                            xT_ps.on(self.turn(pe, bank, x, c))
                    if old:
                        rden_f.wait(pe, old.b - 1)
                        kv_lo.wait(pe, old.b)
                        for c in range(C):
                            q_lo.wait(pe, old.b, c)
                            mm = product(pe, den_bank[:, :], kv[old.par][:, c * KVW + P:c * KVW + 2 * P],
                                         q[old.par][:, c, :], c == 0, c == C - 1)
                        den_ps.on(mm)
                    if new:
                        for t in range(T):
                            bank = first.take(pe, new.b, C + t)
                            for c in range(C):
                                if t == 0:
                                    xT_lo.wait(pe, new.b, c)
                                mm = product(pe, bank[:, :], xT[:, c, t * P:(t + 1) * P], w["Wk"][:, c, :], c == 0, c == C - 1)
                            kq_ps.on(mm)
                    if old:
                        rden_lo.wait(pe, old.b)
                        for c in range(C):
                            bank = second.take(pe, old.b, 2 * c)
                            pe.matmul(bank[:, :], head_rows[:, c, :], rden_s.high[:, :], start=True, stop=False)
                            spread_ps.on(pe.matmul(bank[:, :], head_rows[:, c, :], rden_s.low[:, :], start=False, stop=True))
                            bank = second.take(pe, old.b, 2 * c + 1)
                            att_ps.on(product(pe, bank[:, :], kv[old.par][:, c * KVW:c * KVW + P], q[old.par][:, c, :], True, True))
                    if new:
                        for t in range(T):
                            bank = first.take(pe, new.b, C + T + t)
                            for c in range(C):
                                mm = product(pe, bank[:, :], xT[:, c, t * P:(t + 1) * P], w["Wv"][:, c, :], c == 0, c == C - 1)
                            v_ps.on(mm)
                    if new:
                        for o in range(C):
                            bank = first.take(pe, new.b, C + 2 * T + o)
                            for c in range(C):
                                mm = product(pe, bank[:, :], w["Wq"][:, c, o * P:(o + 1) * P], xT[:, c, :], c == 0, c == C - 1)
                            kq_ps.on(mm)
                    if new:
                        v_sb.wait(pe, new.b)
                        elu_out.wait(pe, new.b, T - 1)
                        for g in range(2):
                            bank = first.take(pe, new.b, 2 * C + 2 * T + g)
                            for i in range(2):
                                c = 2 * g + i
                                for t in range(T):
                                    mm = pe.matmul(bank[:, i * (P + 2):(i + 1) * (P + 2)], k[:, t, c * P:(c + 1) * P],
                                                   v1[:, t, c, :], start=(t == 0), stop=(t == T - 1))
                            kv_ps.on(mm)
                    if old:
                        for t in range(T):
                            bank = second.take(pe, old.b, 2 * C + t)
                            for c in range(C):
                                if t == 0:
                                    z_lo.wait(pe, old.b, c)
                                mm = product(pe, bank[:, :], z[:, c, t * P:(t + 1) * P], w["Wp"][:, c, :], c == 0, c == C - 1)
                            out_ps.on(mm)
                pipeline(pe, B, step)

    def phase_b(self):
        nc, io, B, C, T, D, S = self.nc, self.io, self.B, self.C, self.T, self.D, self.S
        H, _, HD = io["L0_xattn_q_w"].shape
        BIG = 2.0 ** 100
        with Scope(self.nc) as ctx:
            qw = self.split(ctx, "b_qw", [P, C, H * HD])
            kvw = self.split(ctx, "b_kvw", [P, C, 2 * HD])
            ow = self.split(ctx, "b_ow", [P, H, D])
            columns = lambda dram, n: [(dram[i, :, :].rearrange("(c p) h -> p c h", p=P), i * HD) for i in range(n)]
            self.load_weights("bw", [
                ("scale", columns(io["L0_xattn_q_w"], H), H * HD, qw),
                ("scale", columns(io["L0_xattn_kv_w"].rearrange("a k d h -> (a k) d h"), 2), 2 * HD, kvw),
                ("keep", [(io["L0_xattn_out_w"].rearrange("n h d -> h n d"), 0)], D, ow)],
                io["L0_xattn_rms_scale"])
            sb = lambda n, s, d=F32: self.sb(ctx, f"b_{n}", s, d)
            ev = lambda n, per=1, unit=1: Event(ctx, nc, f"b_{n}", per, unit)
            x = sb("x", [P, T, D])
            mem = sb("mem", [P, T, D])
            nT = self.split(ctx, "b_nT", [P, C, S])
            q = self.split(ctx, "b_q", [P, H, S])
            k = [self.split(ctx, f"b_k{i}", [P, S]) for i in range(2)]
            v = [self.split(ctx, f"b_v{i}", [P, T, HD]) for i in range(2)]
            p_f = sb("p_f", [P, T, S])
            p = self.split(ctx, "b_p", [P, T, S])
            psum = sb("psum", [P, S])
            psum_s = self.split(ctx, "b_psums", [P, S])
            enc_f = sb("enc_f", [P, H, S])
            enc = self.split(ctx, "b_enc", [P, H, S])
            res = sb("res", [P, T, D])
            cos_q, sin_q = sb("cos_q", [P, S]), sb("sin_q", [P, S])
            cos_k, sin_k = sb("cos_k", [P, T, HD]), sb("sin_k", [P, T, HD])
            rope_f = [sb(f"rope{i}", [P, S]) for i in range(2)]
            rope_swap = sb("rope_swap", [P, S])
            k_f = sb("k_f", [P, T, HD])
            mask_u8 = sb("mask_u8", [P, S], U8)
            mask_row = sb("mask_row", [P, S])
            unused = [sb(f"unused{i}", [P, S], mybir.dt.bfloat16) for i in range(4)]
            carrier = sb("carrier", [P, 4])
            unused_sq = [sb(f"unused_sq{i}", [P, D], mybir.dt.bfloat16) for i in range(2)]
            mask_any = sb("mask_any", [P, 1])
            p_scale, p_bias = sb("p_scale", [P, T]), sb("p_bias", [P, T])
            top = sb("top", [P, T, H])
            top_row = sb("top_row", [H, S], F32R)
            rsum = sb("rsum", [H, S])
            rsum_s = self.split(ctx, "b_rsums", [H, S])
            head_row = sb("head_row", [H, H, P], F32R)
            minus_row = sb("minus_row", [H, H, P], F32R)
            one_column = sb("one_column", [P, 2 * P], F32R)
            one = sb("one", [1, 1])
            sumsq, mem_ms, mem_scale = sb("sumsq", [P, T]), sb("mem_ms", [P, T]), sb("mem_scale", [P, T])
            one_in_d, rms_eps = sb("one_in_d", [P, T]), sb("rms_eps", [P, T])
            n_sq, n_rms, n_scale = sb("n_sq", [P, T]), sb("n_rms", [P, T]), sb("n_scale", [P, T])
            N = self.norm_events(ctx, "b_ln")
            params, built = ev("params", 4, 16), ev("built", 7)
            mem_in, sq, ms, mscale, mem_n = ev("mem_in", 1, 16), ev("sq", T), ev("ms", 2), ev("mscale"), ev("mem_n", T)
            nsteps, nscale = ev("nsteps", 4), ev("nscale")
            memT_ps, memT_hi, memT_lo = ev("memT_ps", C), ev("memT_hi", C), ev("memT_lo", C)
            kv_ps, v_hi, v_lo = ev("kv_ps", 2), ev("v_hi", 2), ev("v_lo", 2)
            k_cos, k_swap, k_rope = ev("k_cos", 2), ev("k_swap", 4), ev("k_rope", 2)
            kT_ps, k_hi, k_lo = ev("kT_ps"), ev("k_hi"), ev("k_lo")
            xT_ps, xT_hi, xT_lo = ev("xT_ps", C), ev("xT_hi", C), ev("xT_lo", C)
            q_ps, q_cos, q_swap, q_rope = ev("q_ps", H), ev("q_cos", H), ev("q_swap", 2 * H), ev("q_rope", H)
            q_hi, q_lo = ev("q_hi", H), ev("q_lo", H)
            mask_in, mask_f, mask_max, mask_ps, mask_sb = ev("mask_in", 1, 16), ev("mask_f"), ev("mask_max"), ev("mask_ps"), ev("mask_sb", 2)
            top_ps, top_sb, row_ps, row_sb = ev("top_ps", T * H), ev("top_sb", T * H), ev("row_ps"), ev("row_sb")
            st_ps, p_exp, p_hi, p_lo = ev("st_ps", H * T), ev("p_exp", H * T), ev("p_hi", H * T), ev("p_lo", H * T)
            add, add_hi, add_lo = ev("add", 3 * H), ev("add_hi", H), ev("add_lo", H)
            enc_ps, enc_sb, sum_ps = ev("enc_ps", H), ev("enc_sb", H), ev("sum_ps", H)
            rsum_f, rsum_hi, rsum_lo = ev("rsum_f"), ev("rsum_hi"), ev("rsum_lo")
            spread_ps, enc_n, enc_hi, enc_lo = ev("spread_ps", H), ev("enc_n", H), ev("enc_hi", H), ev("enc_lo", H)
            out_ps, x2_sb = ev("out_ps", T), ev("x2_sb", T)
            res_in, stored = ev("res_in", 1, 16), ev("stored", 1, 16)
            KV, KT, XT, Q = C, C + 2, C + 3, 2 * C + 3
            first = Ring(self.banks(ctx, "b_p", 3),
                         [(memT_lo, c) for c in range(C)] + [(k_swap, 1), (k_swap, 3)] + [(k_lo, 0)]
                         + [(xT_lo, c) for c in range(C)] + [(q_swap, 2 * h + 1) for h in range(H)])
            order = [("top", j) for j in range(T * H)]
            for h in range(H):
                order += [("st", h * T + i) for i in range(T)] + ([("enc", h - 1)] if h else [])
            order += [("enc", H - 1)] + [("spread", h) for h in range(H)] + [("out", t) for t in range(T)]
            reader = {"top": top_sb, "st": p_exp, "enc": enc_sb, "spread": enc_n, "out": x2_sb}
            second = Ring(self.banks(ctx, "b_r", 4), [(reader[kind], i) for kind, i in order])
            job = {o: n for n, o in enumerate(order)}
            bank_of = lambda kind, i: second.banks[job[kind, i] % 4]
            aux = self.banks(ctx, "b_aux", 1)[0]
            block = ctx.enter_context(nc.Block())

            @block.sync
            def _(sp):
                for tile, name in ((cos_q[:, :], "cos_q"), (sin_q[:, :], "sin_q"), (cos_k[:, :, :], "cos_k"), (sin_k[:, :, :], "sin_k")):
                    view = io[name] if name.endswith("q") else io[name].rearrange("(t p) h -> p t h", p=P)
                    params.on(sp.dma_start(tile, view))

                def load_mem(b):
                    memT_ps.wait(sp, b - 1)
                    mem_in.on(sp.dma_start(mem[:, :, :], self.token_rows(io["ctx_1024"], b)))

                def load_x(b):
                    xT_ps.wait(sp, b - 1)
                    N.loaded.on(sp.dma_start(x[:, :, :], self.token_rows(self.x1, b)))
                load_mem(0)
                load_x(0)

                def step(new, old):
                    if old:
                        stored.wait(sp, old.b - 1)
                        res_in.on(sp.dma_start(res[:, :, :], self.token_rows(self.x1, old.b)))
                    if following(new, B):
                        load_mem(new.b + 1)
                        load_x(new.b + 1)
                    if old:
                        x2_sb.wait(sp, old.b)
                        stored.on(sp.dma_start(self.token_rows(self.x2, old.b), res[:, :, :]))
                pipeline(sp, B, step)
                stored.wait(sp, B - 1)

            @block.gpsimd
            def _(pool):
                built.on(pool.memset(head_row[:, :, :].bitcast(F32), 0.0))
                built.on(pool.memset(minus_row[:, :, :].bitcast(F32), 0.0))
                built.on(pool.memset(one_column[:, :].bitcast(F32), 0.0))
                pool.memset(one_in_d[:, :], 1.0 / D)
                pool.memset(rms_eps[:, :], 1e-6)
                built.on(pool.memset(one[:, :], 1.0))
                built.wait(pool, 0, 3)
                for tile, value in ((head_row, 1.0), (minus_row, -1.0)):
                    built.on(pool.affine_select(out=tile[:, :, :], in_=tile[:, :, :], compare_op=ALU.not_equal, fill=value,
                                                base=0, pattern=[[-1, H], [0, P]], channel_multiplier=1))
                built.on(pool.memset(one_column[:, P - 1:P].bitcast(F32), 1.0))

                def mem_power(b):
                    sq.wait(pool, b)
                    ms.on(pool.tensor_tensor(mem_ms[:, :], sumsq[:, :], one_in_d[:, :], ALU.mult))
                    ms.wait(pool, b, 0)
                    ms.on(pool.tensor_tensor(mem_ms[:, :], mem_ms[:, :], rms_eps[:, :], ALU.add))
                    ms.wait(pool, b, 1)
                    mem_n.wait(pool, b - 1)
                    mscale.on(pool.tensor_tensor(mem_scale[:, :], mem_ms[:, :], self.minus_half[:, 0:T], ALU.pow))

                def x_power(b):
                    self.norm_power(pool, N, b)
                    own = lambda i, ins: (nsteps.on(ins), nsteps.wait(pool, b, i))
                    N.rstd.wait(pool, b)
                    own(0, pool.tensor_tensor(n_sq[:, :], N.scale[:, :], N.scale[:, :], ALU.mult))
                    own(1, pool.tensor_tensor(n_rms[:, :], n_sq[:, :], N.mv[:, :, 1], ALU.mult))
                    own(2, pool.tensor_tensor(n_sq[:, :], n_rms[:, :], rms_eps[:, :], ALU.add))
                    own(3, pool.tensor_tensor(n_rms[:, :], n_sq[:, :], self.minus_half[:, 0:T], ALU.pow))
                    nscale.on(pool.tensor_tensor(n_scale[:, :], n_rms[:, :], N.scale[:, :], ALU.mult))
                mem_power(0)
                x_power(0)

                def step(new, old):
                    if old:
                        for h in range(H):
                            add_lo.wait(pool, old.b if h else old.b - 1, (h - 1) % H)
                            for i in range(1, T):
                                p_exp.wait(pool, old.b, h * T + i)
                                add.on(pool.tensor_tensor(psum[:, :], p_f[:, 0, :] if i == 1 else psum[:, :], p_f[:, i, :], ALU.add))
                                add.wait(pool, old.b, 3 * h + i - 1)
                            add_hi.wait(pool, old.b, h)
                            add_lo.on(pool.tensor_tensor(psum_s.low[:, :], psum[:, :], psum_s[:, :].high_f32(), ALU.subtract))
                    if following(new, B):
                        mem_power(new.b + 1)
                    if new:
                        for h in range(H):
                            q_hi.wait(pool, new.b, h)
                            q_lo.on(pool.tensor_tensor(q.low[:, h, :], rope_f[h % 2][:, :], q[:, h, :].high_f32(), ALU.subtract))
                    if following(new, B):
                        x_power(new.b + 1)
                pipeline(pool, B, step)

            @block.scalar
            def _(act):
                def squares(b):
                    mem_in.wait(act, b)
                    ms.wait(act, b - 1)
                    for t in range(T):
                        sq.wait(act, b if t >= 2 else b - 1, (t - 2) % T)
                        sq.on(act.activation(unused_sq[t % 2][:, :], mem[:, t, :], ACT.Square, accum_out=sumsq[:, t:t + 1]))
                squares(0)
                built.wait(act, 0)

                def step(new, old):
                    def turned(ps, hi, c, bank, free):
                        ps.wait(act, new.b, c)
                        if c == 0:
                            free(act)
                        hi.on(act.activation(nT.high[:, c, :], bank[:, :], ACT.Copy))

                    def exp(j):
                        h, i = divmod(j, T)
                        st_ps.wait(act, old.b, j)
                        if h:
                            p_lo.wait(act, old.b, j - T)
                            add.wait(act, old.b, 3 * (h - 1) + max(i, 1) - 1)
                        else:
                            p_lo.wait(act, old.b - 1, j + (H - 1) * T)
                            add.wait(act, old.b - 1, 3 * (H - 1) + max(i, 1) - 1)
                        p_exp.on(act.activation(p_f[:, i, :], bank_of("st", j)[:, :], ACT.Exp,
                                                bias=p_bias[:, i:i + 1], scale=p_scale[:, i:i + 1]))

                    def p_high(j):
                        h, i = divmod(j, T)
                        enc_ps.wait(act, old.b if h else old.b - 1, (h - 1) % H)
                        p_exp.wait(act, old.b, j)
                        p_hi.on(act.activation(p.high[:, i, :], p_f[:, i, :], ACT.Copy))

                    def enc_copy(h):
                        enc_ps.wait(act, old.b, h)
                        enc_sb.on(act.activation(enc_f[:, h, :], bank_of("enc", h)[:, :], ACT.Copy))

                    def add_high(h):
                        add.wait(act, old.b, 3 * h + 2)
                        sum_ps.wait(act, old.b if h else old.b - 1, (h - 1) % H)
                        add_hi.on(act.activation(psum_s.high[:, :], psum[:, :], ACT.Copy))

                    if new:
                        for c in range(C):
                            turned(memT_ps, memT_hi, c, first.banks[c % 3], lambda e: q_ps.wait(e, new.b - 1))
                        for g in range(2):
                            kv_ps.wait(act, new.b, g)
                            v_hi.on(act.activation(v[new.par].high[:, 2 * g:2 * g + 2, :],
                                                   first.banks[(KV + g) % 3][:, :].rearrange("p (t n) -> p t n", t=2)[:, :, HD:2 * HD],
                                                   ACT.Copy))
                        mask_f.wait(act, new.b - 1)
                        mask_in.on(act.dma_start(mask_u8[:, :], io["mask_BxS2_bk0"][new.b, :].rearrange("(a s) -> a s", a=1).to_broadcast([P, S])))
                    if old:
                        mask_sb.wait(act, old.b)
                    for h in range(H):
                        if old:
                            for i in range(T):
                                exp(h * T + i)
                                if i:
                                    p_high(h * T + i - 1)
                            p_high(h * T + T - 1)
                            if h:
                                enc_copy(h - 1)
                                add_high(h - 1)
                        if new and h == 0:
                            kT_ps.wait(act, new.b)
                            k_hi.on(act.activation(k[new.par].high[:, :], first.banks[KT % 3][:, :], ACT.Copy))
                        if new:
                            turned(xT_ps, xT_hi, h, first.banks[(XT + h) % 3], lambda e: kv_ps.wait(e, new.b))
                    if old:
                        enc_copy(H - 1)
                        add_high(H - 1)
                    if following(new, B):
                        squares(new.b + 1)
                    if new:
                        if old:
                            st_ps.wait(act, old.b)
                        for h in range(2):
                            q_rope.wait(act, new.b, h)
                            q_hi.on(act.activation(q.high[:, h, :], rope_f[h % 2][:, :], ACT.Copy))
                    if old:
                        rsum_f.wait(act, old.b)
                        spread_ps.wait(act, old.b - 1)
                        rsum_hi.on(act.activation(rsum_s.high[:, :], rsum[:, :], ACT.Copy))
                    if new:
                        for h in range(2, H):
                            q_rope.wait(act, new.b, h)
                            q_hi.on(act.activation(q.high[:, h, :], rope_f[h % 2][:, :], ACT.Copy))
                    if old:
                        for h in range(H):
                            enc_n.wait(act, old.b, h)
                            if h == 0:
                                out_ps.wait(act, old.b - 1)
                            enc_hi.on(act.activation(enc.high[:, h, :], enc_f[:, h, :], ACT.Copy))
                pipeline(act, B, step)

            @block.vector
            def _(dve):
                def mem_apply(b):
                    mscale.wait(dve, b)
                    for t in range(T):
                        mem_n.on(dve.tensor_scalar(mem[:, t, :], mem[:, t, :], mem_scale[:, t:t + 1], None, ALU.mult))

                def x_norm(b):
                    self.norm_stats(dve, N, b, x)
                    self.norm_apply(dve, N, b, x, n_scale, nscale)
                mem_apply(0)
                x_norm(0)
                params.wait(dve, 0)
                built.wait(dve, 0)

                def step(new, old):
                    def turned(hi, lo, c, bank):
                        hi.wait(dve, new.b, c)
                        lo.on(dve.tensor_tensor(nT.low[:, c, :], bank[:, :], nT[:, c, :].high_f32(), ALU.subtract))

                    def top_logits(j):
                        top_sb.wait(dve, old.b if j >= 4 else old.b - 1, (j - 3) % (T * H))
                        top_ps.wait(dve, old.b, j + 1)
                        dve.memset(carrier[:, j // 2 % 4:j // 2 % 4 + 1], 0.0)
                        for i in (j, j + 1):
                            t, h = divmod(i, H)
                            top_sb.on(dve.tensor_tensor_reduce(out=unused[i % 4][:, :], in0=bank_of("top", i)[:, :], in1=mask_row[:, :],
                                                               scale=1.0, scalar=-3e38, op0=ALU.add, op1=ALU.max,
                                                               accum_out=top[:, t, h:h + 1]))

                    def keys(g):
                        v_hi.wait(dve, new.b, g)
                        bank = first.banks[(KV + g) % 3][:, :].rearrange("p (t n) -> p t n", t=2)
                        tiles, half = slice(2 * g, 2 * g + 2), HD // 2
                        v_lo.on(dve.tensor_tensor(v[new.par].low[:, tiles, :], bank[:, :, HD:2 * HD], v[new.par][:, tiles, :].high_f32(), ALU.subtract))
                        swap = rope_swap[:, g * 2 * HD:(g + 1) * 2 * HD].rearrange("p (t n) -> p t n", t=2)
                        k_cos.on(dve.tensor_tensor(k_f[:, tiles, :], bank[:, :, 0:HD], cos_k[:, tiles, :], ALU.mult))
                        q_rope.wait(dve, new.b - 1)
                        k_swap.on(dve.tensor_tensor(swap[:, :, 0:half], bank[:, :, half:HD], sin_k[:, tiles, 0:half], ALU.mult))
                        k_swap.on(dve.tensor_tensor(swap[:, :, half:HD], bank[:, :, 0:half], sin_k[:, tiles, half:HD], ALU.mult))
                        k_cos.wait(dve, new.b, g)
                        k_swap.wait(dve, new.b, 2 * g + 1)
                        k_rope.on(dve.tensor_tensor(k_f[:, tiles, :], k_f[:, tiles, :], swap, ALU.add))

                    def p_low(j):
                        h, i = divmod(j, T)
                        p_hi.wait(dve, old.b, j)
                        p_lo.on(dve.tensor_tensor(p.low[:, i, :], p_f[:, i, :], p[:, i, :].high_f32(), ALU.subtract))

                    def query(h):
                        q_ps.wait(dve, new.b, h)
                        bank, half = first.banks[(Q + h) % 3], HD // 2
                        q_lo.wait(dve, new.b if h >= 2 else new.b - 1, (h - 2) % H)
                        q_cos.on(dve.tensor_tensor(rope_f[h % 2][:, :], bank[:, :], cos_q[:, :], ALU.mult))
                        if h:
                            q_rope.wait(dve, new.b, h - 1)
                        else:
                            k_rope.wait(dve, new.b)
                        q_swap.on(dve.tensor_tensor(rope_swap[0:half, :], bank[half:P, :], sin_q[half:P, :], ALU.mult))
                        q_swap.on(dve.tensor_tensor(rope_swap[half:P, :], bank[0:half, :], sin_q[0:half, :], ALU.mult))
                        q_cos.wait(dve, new.b, h)
                        q_swap.wait(dve, new.b, 2 * h + 1)
                        q_rope.on(dve.tensor_tensor(rope_f[h % 2][:, :], rope_f[h % 2][:, :], rope_swap[:, :], ALU.add))

                    def enc_low(h):
                        enc_hi.wait(dve, old.b, h)
                        enc_lo.on(dve.tensor_tensor(enc.low[:, h, :], enc_f[:, h, :], enc[:, h, :].high_f32(), ALU.subtract))

                    if old:
                        mask_in.wait(dve, old.b)
                        mask_f.on(dve.tensor_scalar(mask_row[:, :], mask_u8[:, :], -1.0, BIG, ALU.add, ALU.mult))
                        mask_f.wait(dve, old.b)
                        mask_max.on(dve.tensor_reduce(mask_any[:, :], mask_row[:, :], mybir.AxisListType.X, ALU.max))
                        mask_ps.wait(dve, old.b)
                        mask_max.wait(dve, old.b)
                        p_exp.wait(dve, old.b - 1)
                        mask_sb.on(dve.tensor_scalar(p_scale[:, :], aux[:, 0:T], 1.0 / BIG, 1.0, ALU.mult, ALU.add))
                        mask_sb.on(dve.tensor_scalar(p_bias[:, :], aux[:, 0:T], mask_any[:, 0:1], None, ALU.subtract))
                    for c in range(C):
                        if new:
                            turned(memT_hi, memT_lo, c, first.banks[c % 3])
                        if old:
                            for i in range(0, H, 2):
                                top_logits(c * H + i)
                    if old:
                        row_ps.wait(dve, old.b)
                        row_sb.on(dve.tensor_copy(top_row[:, :], aux[0:H, :]))
                    if new:
                        for g in range(2):
                            keys(g)
                    for h in range(H):
                        if old:
                            for i in range(T):
                                p_low(h * T + i)
                        if new and h == 0:
                            k_hi.wait(dve, new.b)
                            k_lo.on(dve.tensor_tensor(k[new.par].low[:, :], first.banks[KT % 3][:, :], k[new.par][:, :].high_f32(), ALU.subtract))
                        if new:
                            turned(xT_hi, xT_lo, h, first.banks[(XT + h) % 3])
                    if new:
                        for h in range(2):
                            query(h)
                    if old:
                        sum_ps.wait(dve, old.b)
                        rsum_f.on(dve.reciprocal(rsum[:, :], aux[0:H, :]))
                        rsum_hi.wait(dve, old.b)
                        rsum_lo.on(dve.tensor_tensor(rsum_s.low[:, :], rsum[:, :], rsum_s[:, :].high_f32(), ALU.subtract))
                    if new:
                        for h in range(2, H):
                            query(h)
                    if old:
                        for h in range(H):
                            spread_ps.wait(dve, old.b, h)
                            enc_n.on(dve.tensor_tensor(enc_f[:, h, :], bank_of("spread", h)[:, :], enc_f[:, h, :], ALU.mult))
                            if h:
                                enc_low(h - 1)
                        enc_low(H - 1)
                    if following(new, B):
                        mem_apply(new.b + 1)
                        x_norm(new.b + 1)
                    if old:
                        res_in.wait(dve, old.b)
                        for t in range(T):
                            out_ps.wait(dve, old.b, t)
                            x2_sb.on(dve.tensor_tensor(res[:, t, :], bank_of("out", t)[:, :], res[:, t, :], ALU.add))
                pipeline(dve, B, step)

            @block.tensor
            def _(pe):
                built.wait(pe, 0)

                def step(new, old):
                    if old:
                        mask_f.wait(pe, old.b)
                        rsum_f.wait(pe, old.b - 1)
                        for i in range(T):
                            mm = pe.matmul(aux[:, i:i + 1], mask_row[0:1, i * P:(i + 1) * P], one[:, :], start=True, stop=True)
                        mask_ps.on(mm)
                    for c in range(C):
                        if new:
                            bank = first.take(pe, new.b, c)
                            if c == 0:
                                mem_n.wait(pe, new.b)
                            memT_ps.on(self.turn(pe, bank, mem, c))
                        if old:
                            for h in range(H):
                                j = c * H + h
                                bank = second.take(pe, old.b, job["top", j])
                                if c == 0:
                                    q_lo.wait(pe, old.b, h)
                                top_ps.on(pe.matmul(bank[:, :], q.high[:, h, c * P:(c + 1) * P], k[old.par].high[:, :], start=True, stop=True))
                    if new:
                        for g in range(2):
                            bank = first.take(pe, new.b, KV + g)
                            for i in range(2):
                                t = 2 * g + i
                                for c in range(C):
                                    if t == 0:
                                        memT_lo.wait(pe, new.b, c)
                                    mm = product(pe, bank[:, i * 2 * HD:(i + 1) * 2 * HD], nT[:, c, t * P:(t + 1) * P], kvw[:, c, :], c == 0, c == C - 1)
                            kv_ps.on(mm)
                    if old:
                        top_sb.wait(pe, old.b)
                        mask_sb.wait(pe, old.b)
                        for t in range(T):
                            mm = pe.matmul(aux[0:H, t * P:(t + 1) * P], top[:, t, :], self.ident[:, :], start=True, stop=True)
                        row_ps.on(mm)

                    def encode(h):
                        bank = second.take(pe, old.b, job["enc", h])
                        for i in range(T):
                            p_lo.wait(pe, old.b, h * T + i)
                            mm = product(pe, bank[:, :], v[old.par][:, i, :], p[:, i, :], i == 0, i == T - 1)
                        enc_ps.on(mm)

                    def total(h):
                        add_lo.wait(pe, old.b, h)
                        lhs = one_column[:, P - 1 - h:2 * P - 1 - h]
                        pe.matmul(aux[:, :], lhs, psum_s.high[:, :], start=(h == 0), stop=False)
                        sum_ps.on(pe.matmul(aux[:, :], lhs, psum_s.low[:, :], start=False, stop=(h == H - 1)))

                    for h in range(H):
                        if old:
                            for i in range(T):
                                j = h * T + i
                                bank = second.take(pe, old.b, job["st", j])
                                if j == 0:
                                    row_sb.wait(pe, old.b)
                                pe.matmul(bank[:, :], minus_row[:, h, :], top_row[:, :], start=True, stop=False)
                                st_ps.on(product(pe, bank[:, :], k[old.par][:, i * P:(i + 1) * P], q[:, h, :], False, True))
                        if new and h == 0:
                            bank = first.take(pe, new.b, KT)
                            k_rope.wait(pe, new.b)
                            for t in range(T):
                                mm = pe.transpose(bank[:, t * P:(t + 1) * P], k_f[:, t, :], self.ident[:, :])
                            kT_ps.on(mm)
                        if new:
                            bank = first.take(pe, new.b, XT + h)
                            if h == 0:
                                N.normed.wait(pe, new.b)
                            xT_ps.on(self.turn(pe, bank, x, h))
                        if old and h:
                            encode(h - 1)
                            if h >= 2:
                                total(h - 2)
                    if old:
                        encode(H - 1)
                        total(H - 2)

                    def queries(h):
                        bank = first.take(pe, new.b, Q + h)
                        for c in range(C):
                            if h == 0:
                                xT_lo.wait(pe, new.b, c)
                            mm = product(pe, bank[:, :], qw[:, c, h * HD:(h + 1) * HD], nT[:, c, :], c == 0, c == C - 1)
                        q_ps.on(mm)

                    def spread(h):
                        bank = second.take(pe, old.b, job["spread", h])
                        if h == 0:
                            rsum_lo.wait(pe, old.b)
                        pe.matmul(bank[:, :], head_row[:, h, :], rsum_s.high[:, :], start=True, stop=False)
                        spread_ps.on(pe.matmul(bank[:, :], head_row[:, h, :], rsum_s.low[:, :], start=False, stop=True))
                    if new:
                        queries(0)
                    if old:
                        total(H - 1)
                    if new:
                        queries(1)
                        queries(2)
                    if old:
                        for h in range(H):
                            spread(h)
                    if new:
                        queries(3)
                    if old:
                        for t in range(T):
                            bank = second.take(pe, old.b, job["out", t])
                            for h in range(H):
                                if t == 0:
                                    enc_lo.wait(pe, old.b, h)
                                mm = product(pe, bank[:, :], enc[:, h, t * P:(t + 1) * P], ow[:, h, :], h == 0, h == H - 1)
                            out_ps.on(mm)
                pipeline(pe, B, step)

    def phase_c(self, state):
        nc, io, B, C, T, D, S = self.nc, self.io, self.B, self.C, self.T, self.D, self.S
        GATES = "icf"
        with Scope(self.nc) as ctx:
            w = {g: self.split(ctx, f"c_w{g}", [P, C, D]) for g in GATES}
            u = {g: self.split(ctx, f"c_u{g}", [P, C, D]) for g in GATES}
            self.load_weights("cw", [("turn", io[f"L0_ffn_{k}{g}"], D, t[g]) for g in GATES for k, t in (("w", w), ("u", u))])
            sb = lambda n, s, d=F32: self.sb(ctx, f"c_{n}", s, d)
            ev = lambda n, per=1, unit=1: Event(ctx, nc, f"c_{n}", per, unit)
            x = sb("x", [P, T, D])
            nT = [self.split(ctx, f"c_nT{i}", [P, C, S]) for i in range(2)]
            c_f = sb("c_f", [P, C, S])
            gate = sb("gate", [P, 2, 3, S])
            bias = sb("bias", [P, 3, C])
            c_in = sb("c_in", [P, C])
            N = self.norm_events(ctx, "c_ln")
            params, zero, start_f, start_hi, start = ev("params", 4, 16), ev("zero"), ev("start_f", C), ev("start_hi"), ev("start")
            xT_ps, xT_hi, xT_lo = ev("xT_ps", C), ev("xT_hi", C), ev("xT_lo", C)
            gate_ps, gate_sb = ev("gate_ps", 3 * C), ev("gate_sb", 3 * C)
            ig, fc, c_new, c_hi, c_lo = ev("ig", C), ev("fc", C), ev("c_new", C), ev("c_hi", C), ev("c_lo", C)
            turning = Ring(self.banks(ctx, "c_t", 2), [(xT_lo, c) for c in range(C)])
            gating = Ring(self.banks(ctx, "c_g", 6), [(gate_sb, n) for n in range(3 * C)])
            block = ctx.enter_context(nc.Block())

            @block.sync
            def _(sp):
                with nc.allow_non_contiguous_dma(reason="small parameters, once"):
                    for i, g in enumerate(GATES):
                        params.on(sp.dma_start(bias[:, i, :], io[f"L0_ffn_b{g}"].rearrange("(c p) -> p c", p=P)))
                    params.on(sp.dma_start(c_in[:, :], io["L0_ffn_in_c"].rearrange("(c p) -> p c", p=P)))

                def load(b):
                    xT_ps.wait(sp, b - 1)
                    N.loaded.on(sp.dma_start(x[:, :, :], self.token_rows(self.x2, b)))
                load(0)

                def step(new, old):
                    if following(new, B):
                        load(new.b + 1)
                pipeline(sp, B, step)

            @block.gpsimd
            def _(pool):
                self.norm_power(pool, N, 0)

                def step(new, old):
                    if following(new, B):
                        self.norm_power(pool, N, new.b + 1)
                pipeline(pool, B, step)

            @block.scalar
            def _(act):
                start_f.wait(act, 0)
                start_hi.on(act.activation(state[1].high[:, :, :], c_f[:, :, :], ACT.Copy))
                params.wait(act, 0)

                def step(new, old):
                    def split_new(j):
                        c_new.wait(act, old.b, j)
                        c_hi.on(act.activation(state[old.par].high[:, j, :], c_f[:, j, :], ACT.Copy))
                    if new:
                        for c in range(C):
                            xT_ps.wait(act, new.b, c)
                            xT_hi.on(act.activation(nT[new.par].high[:, c, :], turning.banks[c % 2][:, :], ACT.Copy))
                    if old:
                        for j in range(C):
                            for i, g in enumerate(GATES):
                                gate_ps.wait(act, old.b, 3 * j + i)
                                if i == 0:
                                    c_new.wait(act, old.b if j >= 2 else old.b - 1, (j - 2) % C)
                                gate_sb.on(act.activation(gate[:, j % 2, i, :], gating.banks[(3 * j + i) % 6][:, :],
                                                          ACT.Tanh if g == "c" else ACT.Sigmoid, bias=bias[:, i, j:j + 1]))
                                if j and i == 0:
                                    split_new(j - 1)
                        split_new(C - 1)
                pipeline(act, B, step)

            @block.vector
            def _(dve):
                zero.on(dve.memset(c_f[:, :, :], 0.0))
                zero.wait(dve, 0)
                params.wait(dve, 0)
                for c in range(C):
                    start_f.on(dve.tensor_scalar(c_f[:, c, :], c_f[:, c, :], c_in[:, c:c + 1], None, ALU.add))
                start_hi.wait(dve, 0)
                start.on(dve.tensor_tensor(state[1].low[:, :, :], c_f[:, :, :], state[1][:, :, :].high_f32(), ALU.subtract))

                def norm(b):
                    self.norm_stats(dve, N, b, x)
                    self.norm_apply(dve, N, b, x, N.scale, N.rstd)
                norm(0)

                def step(new, old):
                    if new:
                        for c in range(C):
                            xT_hi.wait(dve, new.b, c)
                            xT_lo.on(dve.tensor_tensor(nT[new.par].low[:, c, :], turning.banks[c % 2][:, :],
                                                       nT[new.par][:, c, :].high_f32(), ALU.subtract))

                    def update(j):
                        slot = gate[:, j % 2, :, :]
                        gate_sb.wait(dve, old.b, 3 * j + 1)
                        ig.on(dve.tensor_tensor(slot[:, 0, :], slot[:, 0, :], slot[:, 1, :], ALU.mult))
                        gate_sb.wait(dve, old.b, 3 * j + 2)
                        fc.on(dve.tensor_tensor(slot[:, 2, :], slot[:, 2, :], c_f[:, j, :], ALU.mult))
                        ig.wait(dve, old.b, j)
                        fc.wait(dve, old.b, j)
                        c_new.on(dve.tensor_tensor(c_f[:, j, :], slot[:, 0, :], slot[:, 2, :], ALU.add))

                    def split_new(j):
                        c_hi.wait(dve, old.b, j)
                        c_lo.on(dve.tensor_tensor(state[old.par].low[:, j, :], c_f[:, j, :], state[old.par][:, j, :].high_f32(), ALU.subtract))
                    if old:
                        update(0)
                        update(1)
                        split_new(0)
                    if following(new, B):
                        norm(new.b + 1)
                    if old:
                        for j in range(2, C):
                            update(j)
                            split_new(j - 1)
                        split_new(C - 1)
                pipeline(dve, B, step)

            @block.tensor
            def _(pe):
                start.wait(pe, 0)

                def step(new, old):
                    def part(j, weights, source, first):
                        for i, g in enumerate(GATES):
                            n = 3 * j + i
                            bank = gating.take(pe, old.b, n) if first else gating.banks[n % 6]
                            for c in range(C):
                                mm = product(pe, bank[:, :], weights[g][:, c, j * P:(j + 1) * P], source[:, c, :],
                                             first and c == 0, not first and c == C - 1)
                            if not first:
                                gate_ps.on(mm)
                    if old:
                        xT_lo.wait(pe, old.b)
                        part(0, w, nT[old.par], True)
                    if new:
                        N.normed.wait(pe, new.b)
                        for c in range(C):
                            xT_ps.on(self.turn(pe, turning.take(pe, new.b, c), x, c))
                    if old:
                        c_lo.wait(pe, old.b - 1)
                        part(0, u, state[1 - old.par], False)
                        for j in range(1, C):
                            part(j, w, nT[old.par], True)
                            part(j, u, state[1 - old.par], False)
                pipeline(pe, B, step)

    def phase_d(self, c_last):
        nc, io, B, C, T, D, S = self.nc, self.io, self.B, self.C, self.T, self.D, self.S
        X = 3
        with Scope(self.nc) as ctx:
            wo, uo = (self.split(ctx, f"d_{n}", [P, C, D]) for n in ("wo", "uo"))
            self.load_weights("dw", [("turn", io[f"L0_ffn_{n}"], D, t) for n, t in (("uo", uo), ("wo", wo))])
            sb = lambda n, s, d=F32: self.sb(ctx, f"d_{n}", s, d)
            ev = lambda n, per=1, unit=1: Event(ctx, nc, f"d_{n}", per, unit)
            x = [sb(f"x{i}", [P, T, D]) for i in range(X)]
            n = sb("n", [P, T, D])
            nT = [self.split(ctx, f"d_nT{i}", [P, C, S]) for i in range(X)]
            base = sb("base", [P, T, D])
            bo = sb("bo", [P, D])
            y = sb("y", [P, 2, D])
            N = self.norm_events(ctx, "d_ln")
            stored = ev("stored", 1, 16)
            bo_in, base_ps, base_sb = ev("bo_in", 1, 16), ev("base_ps", T), ev("base_sb", T)
            xT_ps, xT_hi, xT_lo = ev("xT_ps", C), ev("xT_hi", C), ev("xT_lo", C)
            y_ps, y_sb, y_tanh, out_sb = ev("y_ps", T), ev("y_sb", T), ev("y_tanh", T), ev("out_sb", T)
            turning = Ring(self.banks(ctx, "d_t", 4), [(xT_lo, c) for c in range(C)])
            output = Ring(self.banks(ctx, "d_y", 4), [(y_sb, t) for t in range(T)])
            block = ctx.enter_context(nc.Block())

            @block.sync
            def _(sp):
                bo_in.on(sp.dma_start(bo[:, :], io["L0_ffn_bo"].rearrange("(a n) -> a n", a=1).to_broadcast([P, D])))
                N.loaded.on(sp.dma_start(x[0][:, :, :], self.token_rows(self.x2, 0)))

                def step(new, old):
                    if following(new, B):
                        stored.wait(sp, new.b - 2)
                        N.loaded.wait(sp, new.b)
                        N.loaded.on(sp.dma_start(x[(new.par + 1) % X][:, :, :], self.token_rows(self.x2, new.b + 1)))
                    if old:
                        out_sb.wait(sp, old.b)
                        stored.on(sp.dma_start(self.token_rows(self.out, old.b), x[old.par][:, :, :]))
                pipeline(sp, B, step, X)
                stored.wait(sp, B - 1)

            @block.gpsimd
            def _(pool):
                self.norm_power(pool, N, 0)

                def step(new, old):
                    if old:
                        for t in range(T):
                            y_tanh.wait(pool, old.b, t)
                            out_sb.on(pool.tensor_tensor(x[old.par][:, t, :], x[old.par][:, t, :], y[:, t % 2, :], ALU.add))
                    if following(new, B):
                        self.norm_power(pool, N, new.b + 1)
                pipeline(pool, B, step, X)

            @block.scalar
            def _(act):
                def step(new, old):
                    for c in range(C):
                        if new:
                            xT_ps.wait(act, new.b, c)
                            xT_hi.on(act.activation(nT[new.par].high[:, c, :], turning.banks[c][:, :], ACT.Copy))
                    for t in range(T):
                        if old:
                            y_sb.wait(act, old.b, t)
                            y_tanh.on(act.activation(y[:, t % 2, :], y[:, t % 2, :], ACT.Tanh))
                pipeline(act, B, step, X)

            @block.vector
            def _(dve):
                bo_in.wait(dve, 0)
                for t in range(T):
                    base_ps.wait(dve, 0, t)
                    base_sb.on(dve.tensor_tensor(base[:, t, :], output.banks[t][:, :], bo[:, :], ALU.add))
                base_sb.wait(dve, 0)

                def norm(b, tile):
                    self.norm_stats(dve, N, b, tile)
                    xT_ps.wait(dve, b - 1)
                    self.norm_apply(dve, N, b, tile, N.scale, N.rstd, n)
                norm(0, x[0])

                def step(new, old):
                    if new:
                        for c in range(C):
                            xT_hi.wait(dve, new.b, c)
                            xT_lo.on(dve.tensor_tensor(nT[new.par].low[:, c, :], turning.banks[c][:, :],
                                                       nT[new.par][:, c, :].high_f32(), ALU.subtract))
                    if old:
                        for t in range(T):
                            y_ps.wait(dve, old.b, t)
                            out_sb.wait(dve, old.b if t >= 2 else old.b - 1, (t - 2) % T)
                            y_sb.on(dve.tensor_tensor(y[:, t % 2, :], output.banks[t][:, :], base[:, t, :], ALU.add))
                    if following(new, B):
                        norm(new.b + 1, x[(new.par + 1) % X])
                pipeline(dve, B, step, X)

            @block.tensor
            def _(pe):
                for t in range(T):
                    for c in range(C):
                        mm = product(pe, output.banks[t][:, :], c_last[:, c, t * P:(t + 1) * P], uo[:, c, :], c == 0, c == C - 1)
                    base_ps.on(mm)

                def step(new, old):
                    if new:
                        N.normed.wait(pe, new.b)
                        for c in range(C):
                            xT_ps.on(self.turn(pe, turning.take(pe, new.b, c), n, c))
                    if old:
                        for t in range(T):
                            if isinstance(old.b, int) and old.b == 0:
                                base_sb.wait(pe, 0, t)
                            bank = output.take(pe, old.b, t)
                            for c in range(C):
                                if t == 0:
                                    xT_lo.wait(pe, old.b, c)
                                mm = product(pe, bank[:, :], nT[old.par][:, c, t * P:(t + 1) * P], wo[:, c, :], c == 0, c == C - 1)
                            y_ps.on(mm)
                pipeline(pe, B, step, X)

    def run(self):
        with Scope(self.nc) as ctx:
            self.constants(ctx)
            self.phase_a()
            self.phase_b()
            self.phase_cd(ctx)

    def phase_cd(self, ctx):
        state = [self.split(ctx, f"state{i}", [P, self.C, self.S]) for i in range(2)]
        self.phase_c(state)
        self.phase_d(state[(self.B - 1) % 2])


def tables(T, S, H):
    f32 = np.float32
    timescale = f32(10000.0) ** (f32(2.0 / H) * np.arange(H // 2, dtype=f32))
    angle = lambda start, n: (np.arange(start, start + n, dtype=f32)[:, None] / timescale).astype(f32)
    aq, ak, scale = angle(S, T).T, angle(0, S), f32(H ** -0.5)
    two = np.concatenate
    return {"cos_q": two([np.cos(aq), np.cos(aq)]) * scale, "sin_q": two([np.sin(aq), -np.sin(aq)]) * scale,
            "cos_k": two([np.cos(ak), np.cos(ak)], 1), "sin_k": two([-np.sin(ak), np.sin(ak)], 1)}


_INS = ["x", "ctx_1024", "mask_BxS2_bk0", "L0_attn_Wq", "L0_attn_Wk", "L0_attn_Wv", "L0_attn_Wp", "L0_attn_bp",
        "L0_attn_conv_w", "L0_attn_conv_b", "L0_xattn_rms_scale", "L0_xattn_q_w", "L0_xattn_kv_w", "L0_xattn_out_w",
        "L0_ffn_wf", "L0_ffn_uf", "L0_ffn_bf", "L0_ffn_wi", "L0_ffn_ui", "L0_ffn_bi", "L0_ffn_wc", "L0_ffn_uc",
        "L0_ffn_bc", "L0_ffn_wo", "L0_ffn_uo", "L0_ffn_bo", "L0_ffn_in_c"]


def kernel(**inputs):
    import concourse.bacc as bacc
    from concourse.bass_utils import run_bass_kernel_spmd

    nc = bacc.Bacc("TRN2", target_bir_lowering=False, num_devices=1)
    arrays = {f"in_{n}": np.ascontiguousarray(inputs[n]) for n in _INS}
    B, S, D = inputs["x"].shape
    arrays.update({f"in_{n}": np.ascontiguousarray(t, np.float32)
                   for n, t in tables(S, inputs["ctx_1024"].shape[1], inputs["L0_xattn_q_w"].shape[2]).items()})
    io = {n[3:]: nc.dram_tensor(n, a.shape, mybir.dt.from_np(a.dtype), kind="ExternalInput").ap() for n, a in arrays.items()}
    out = nc.dram_tensor("out", (B, S, D), F32, kind="ExternalOutput").ap()
    x1, x2 = (nc.dram_tensor(n, (B, S, D), F32, kind="Internal").ap() for n in ("x1", "x2"))
    Kernel(nc, io, out, x1, x2).run()
    return run_bass_kernel_spmd(nc, [arrays], core_ids=[0]).results[0]["out"]
```

```python
from contextlib import ExitStack

import numpy as np
import concourse.bass as bass
from concourse import mybir

F32 = mybir.dt.float32
F32R = mybir.dt.float32r
U8 = mybir.dt.uint8
ALU = mybir.AluOpType
ACT = mybir.ActivationFunctionType
P = 128


class Scope(ExitStack):

    def __init__(self, nc):
        super().__init__()
        self.nc, self.semaphores = nc, []

    def __exit__(self, *error):
        super().__exit__(*error)
        if self.semaphores and error[0] is None:
            self.nc.clear_and_free_semaphores(self.semaphores)
            self.nc.all_engine_barrier()


class Event:

    def __init__(self, ctx, nc, name, per=1, unit=1):
        self.sem, self.per, self.unit = nc.alloc_semaphore(name), per, unit
        ctx.semaphores.append(self.sem)

    def on(self, instruction):
        instruction.then_inc(self.sem, self.unit)

    def wait(self, engine, b, k=None):
        k = self.per - 1 if k is None else k
        if isinstance(b, int) and b < 0:
            return
        engine.wait_ge(self.sem, (b * self.per + k + 1) * self.unit)


class Ring:

    def __init__(self, banks, frees, batches):
        self.banks, self.frees, self.batches = banks, [f if len(f) == 3 else (*f, 0) for f in frees], batches
        assert len(frees) % len(banks) == 0

    def take(self, engine, s, n):
        for back in range(len(self.banks), 2 * len(self.frees), len(self.banks)):
            steps, prev = divmod(n - back, len(self.frees))
            event, k, lag = self.frees[prev]
            b = s + (steps - lag)
            if not isinstance(b, int) or 0 <= b < self.batches:
                event.wait(engine, b, k)
                break
        return self.banks[n % len(self.banks)]


class Item:

    def __init__(self, b, par):
        self.b, self.par = b, par


def pipeline(engine, B, step, unroll=2):
    at = lambda base, i: Item(base + i, i % unroll)
    turns = (B - 3) // unroll
    step(Item(0, 0), None)
    step(at(0, 1), at(0, 0))
    with engine.Fori(0, turns) as j:
        for i in range(unroll):
            step(at(unroll * j, i + 2), at(unroll * j, i + 1))
    for b in range(unroll * turns + 2, B):
        step(at(0, b), at(0, b - 1))
    step(None, at(0, B - 1))


def following(new, B):
    return new is not None and not (isinstance(new.b, int) and new.b == B - 1)


class Split:

    def __init__(self, high, low):
        self.high, self.low = high, low

    def __getitem__(self, at):
        return Split(self.high[at], self.low[at])

    def high_f32(self):
        return self.high.bitcast(F32)


def product(pe, out, stationary, moving, first, last):
    pe.matmul(out, stationary.high, moving.high, start=first, stop=False)
    pe.matmul(out, stationary.high, moving.low, start=False, stop=False)
    return pe.matmul(out, stationary.low, moving.high, start=False, stop=last)


class Kernel:
    def __init__(self, nc, io, out, scratch1, scratch2):
        self.nc, self.io, self.out, self.x1, self.x2 = nc, io, out, scratch1, scratch2
        self.B, self.S, self.D = io["x"].shape
        self.C = self.D // P
        self.T = self.S // P

    def sb(self, ctx, name, shape, dtype=F32):
        return ctx.enter_context(self.nc.sbuf_tensor(name, shape, dtype))

    def split(self, ctx, name, shape):
        return Split(self.sb(ctx, name + "_hi", shape, F32R), self.sb(ctx, name + "_lo", shape, F32R))

    def banks(self, ctx, name, n):
        return [ctx.enter_context(self.nc.psum_tensor(f"{name}{i}", [P, 512], F32)) for i in range(n)]

    def load_weights(self, tag, jobs, rms_scale=None):
        nc, C, D = self.nc, self.C, self.D
        with Scope(self.nc) as ctx:
            sb = lambda n, s, d=F32: self.sb(ctx, f"{tag}_{n}", s, d)
            stage = [sb(f"stage{i}", [P, C, D]) for i in range(2)]
            scale = sb("scale", [P, C])
            banks = self.banks(ctx, f"{tag}_pw", 4)
            ev = lambda n, per=1, unit=1: Event(ctx, nc, f"{tag}_{n}", per, unit)
            loaded = [ev(f"loaded{i}", 1 if j[0] == "turn" else len(j[1]), 16) for i, j in enumerate(jobs)]
            scaled, turned, high, low = ev("scaled", C), ev("turned", C), ev("high", C), ev("low", C)
            scale_in, scale_one = ev("scale_in", 1, 16), ev("scale_one")
            block = ctx.enter_context(nc.Block())
            before = [sum(j[0] == jobs[i][0] for j in jobs[:i]) for i in range(len(jobs))]

            @block.sync
            def _(sp):
                if rms_scale is not None:
                    with nc.allow_non_contiguous_dma(reason="512 words once"):
                        scale_in.on(sp.dma_start(scale[:, :], rms_scale.rearrange("(c p) -> p c", p=P)))
                for i, (kind, parts, n, w) in enumerate(jobs):
                    low.wait(sp, i - 2)
                    if kind == "turn":
                        parts = [(parts.rearrange("(c p) n -> p c n", p=P), 0)]
                    for view, at in parts:
                        loaded[i].on(sp.dma_start(stage[i % 2][:, :, at:at + view.shape[2]], view))

            @block.tensor
            def _(pe):
                for i, (kind, parts, n, w) in enumerate(jobs):
                    if kind != "turn":
                        continue
                    loaded[i].wait(pe, 0)
                    for c in range(C):
                        if i >= 1:
                            low.wait(pe, i - 1, c)
                        for o in range(C):
                            mm = pe.transpose(banks[c][:, o * P:(o + 1) * P],
                                              stage[i % 2][:, o, c * P:(c + 1) * P], self.ident[:, :])
                        turned.on(mm)

            def source(i, c):
                kind, parts, n, w = jobs[i]
                return banks[c][:, 0:n] if kind == "turn" else stage[i % 2][:, c, 0:n]

            def ready(engine, i, c):
                if jobs[i][0] == "turn":
                    turned.wait(engine, before[i], c)
                elif jobs[i][0] == "scale":
                    scaled.wait(engine, before[i], c)
                else:
                    loaded[i].wait(engine, 0)

            @block.scalar
            def _(act):
                for i, (kind, parts, n, w) in enumerate(jobs):
                    for c in range(C):
                        ready(act, i, c)
                        high.on(act.activation(w.high[:, c, 0:n], source(i, c), ACT.Copy))

            @block.vector
            def _(dve):
                if rms_scale is not None:
                    scale_in.wait(dve, 0)
                    scale_one.on(dve.tensor_scalar(scale[:, :], scale[:, :], 1.0, None, ALU.add))
                    scale_one.wait(dve, 0)
                for i, (kind, parts, n, w) in enumerate(jobs):
                    if kind == "scale":
                        loaded[i].wait(dve, 0)
                        for c in range(C):
                            scaled.on(dve.tensor_scalar(stage[i % 2][:, c, 0:n], stage[i % 2][:, c, 0:n],
                                                        scale[:, c:c + 1], None, ALU.mult))
                    for c in range(C):
                        ready(dve, i, c)
                        high.wait(dve, i, c)
                        low.on(dve.tensor_tensor(w.low[:, c, 0:n], source(i, c),
                                                 w[:, c, 0:n].high_f32(), ALU.subtract))

    def norm_events(self, ctx, tag):
        e = lambda n, per=1, unit=1: Event(ctx, self.nc, f"{tag}_{n}", per, unit)

        class N:
            loaded = e("loaded", 1, 16)
            stats, moments, variance, rstd, normed = e("stats", self.T), e("moments", self.T), e("var"), e("rstd"), e("normed", self.T)
            carrier = self.sb(ctx, f"{tag}_carrier", [P, 1])
            st = self.sb(ctx, f"{tag}_st", [P, self.T, 6])
            mv = self.sb(ctx, f"{tag}_mv", [P, self.T, 2])
            var_eps = self.sb(ctx, f"{tag}_ve", [P, self.T])
            scale = self.sb(ctx, f"{tag}_sc", [P, self.T])
        return N

    def norm_stats(self, dve, N, b, x):
        N.loaded.wait(dve, b)
        for t in range(self.T):
            N.stats.on(dve.bn_stats(N.st[:, t, :], x[:, t, :]))
        N.stats.wait(dve, b)
        dve.memset(N.carrier[:, :], 0.0)
        for t in range(self.T):
            N.moments.on(dve.bn_aggr(N.mv[:, t, :], N.st[:, t, :]))
        N.moments.wait(dve, b)
        N.variance.on(dve.tensor_scalar(N.var_eps[:, :], N.mv[:, :, 1], 1e-5, None, ALU.add))

    def norm_power(self, pool, N, b):
        N.variance.wait(pool, b)
        N.normed.wait(pool, b - 1)
        N.rstd.on(pool.tensor_tensor(N.scale[:, :], N.var_eps[:, :], self.minus_half[:, 0:self.T], ALU.pow))

    def norm_apply(self, dve, N, b, x, scale, scale_event, out=None):
        scale_event.wait(dve, b)
        for t in range(self.T):
            N.normed.on(dve.tensor_scalar((out or x)[:, t, :], x[:, t, :], N.mv[:, t, 0:1], scale[:, t:t + 1],
                                          ALU.subtract, ALU.mult))

    def turn(self, pe, bank, src, c):
        for t in range(self.T):
            mm = pe.transpose(bank[:, t * P:(t + 1) * P], src[:, t, c * P:(c + 1) * P], self.ident[:, :])
        return mm

    def token_rows(self, dram, b):
        return dram[b, :, :].rearrange("(t p) d -> p t d", p=P)

    def constants(self, ctx):
        nc = self.nc
        self.ident = self.sb(ctx, "ident", [P, P])
        self.minus_half = self.sb(ctx, "minus_half", [P, 4])
        with Scope(self.nc) as c:
            zero = Event(c, nc, "ident_zero")
            block = c.enter_context(nc.Block())

            @block.gpsimd
            def _(pool):
                pool.memset(self.minus_half[:, :], -0.5)
                zero.on(pool.memset(self.ident[:, :], 0.0))
                zero.wait(pool, 0)
                pool.affine_select(out=self.ident[:, :], in_=self.ident[:, :], compare_op=ALU.not_equal,
                                   fill=1.0, base=0, pattern=[[-1, P]], channel_multiplier=1)

    def phase_a(self):
        nc, io, B, C, T, D, S = self.nc, self.io, self.B, self.C, self.T, self.D, self.S
        HEADS = 16
        HD = D // HEADS
        HC = P // HD
        KVW = P + HEADS
        with Scope(self.nc) as ctx:
            w = {n: self.split(ctx, f"a_{n}", [P, C, D]) for n in ("Wq", "Wk", "Wv", "Wp")}
            self.load_weights("aw", [("turn", io[f"L0_attn_{n}"], D, w[n]) for n in w])
            sb = lambda n, s, d=F32: self.sb(ctx, f"a_{n}", s, d)
            ev = lambda n, per=1, unit=1: Event(ctx, nc, f"a_{n}", per, unit)
            x = sb("x", [P, T, D])
            xT = self.split(ctx, "a_xT", [P, C, S])
            k = sb("k", [P, T, D])
            v1 = sb("v1", [P, T, C, P + 2])
            q = [self.split(ctx, f"a_q{i}", [P, C, S]) for i in range(2)]
            local = [sb(f"local{i}", [P, C, S]) for i in range(2)]
            kv = [self.split(ctx, f"a_kv{i}", [P, C * KVW + P - HEADS]) for i in range(2)]
            z = self.split(ctx, "a_z", [P, C, S])
            res = sb("res", [P, T, D])
            elu = sb("elu", [P, 2, D])
            kv_f = elu[:, :, :].rearrange("p a d -> p (a d)")[:, 0:C * KVW].rearrange("p (c e) -> p c e", c=C)
            rden = sb("rden", [HEADS, S])
            rden_s = self.split(ctx, "a_rdens", [HEADS, S])
            att = [sb(f"att{i}", [P, S]) for i in range(2)]
            head_rows = sb("head_rows", [HEADS, C, P], F32R)
            kv_mask = sb("kv_mask", [P, 2, P])
            head_mask = sb("head_mask", [P, C, HEADS])
            bp = sb("bp", [P, D])
            conv_w = sb("conv_w", [P, C, 3])
            conv_b = sb("conv_b", [P, C])
            N = self.norm_events(ctx, "a_ln")
            params = ev("params", 3, 16)
            built = ev("built", 11)
            xT_ps, xT_hi, xT_lo = ev("xT_ps", C), ev("xT_hi", C), ev("xT_lo", C)
            tap1, tap0, tap2 = ev("tap1", C), ev("tap0", C), ev("tap2", C)
            kq_ps, v_ps = ev("kq_ps", T + C), ev("v_ps", T)
            elu_neg, elu_exp, elu_out = ev("elu_neg", T + C), ev("elu_exp", T + C), ev("elu_out", T + C)
            q_hi, q_lo, v_sb = ev("q_hi", C), ev("q_lo", C), ev("v_sb", T)
            kv_ps, kv_part, kv_hi, kv_lo = ev("kv_ps", 2), ev("kv_part", 6), ev("kv_hi"), ev("kv_lo")
            den_ps, den_max, rden_f, rden_hi, rden_lo = ev("den_ps"), ev("den_max"), ev("rden_f"), ev("rden_hi"), ev("rden_lo")
            spread_ps, spread_sb, att_ps, att_sb = ev("spread_ps", C), ev("spread_sb", C), ev("att_ps", C), ev("att_sb", C)
            z_f, z_hi, z_lo = ev("z_f", C), ev("z_hi", C), ev("z_lo", C)
            out_ps, res_bp, x1_sb = ev("out_ps", T), ev("res_bp", T), ev("x1_sb", T)
            res_in, stored = ev("res_in", 1, 16), ev("stored", 1, 16)
            first = Ring(self.banks(ctx, "a_p", 3),
                         [(tap2, c) for c in range(C)] + [(elu_out, t) for t in range(T)]
                         + [(v_sb, t) for t in range(T)] + [(elu_out, T + c) for c in range(C)]
                         + [(kv_part, 2), (kv_part, 5)], B)
            second = Ring(self.banks(ctx, "a_r", 4),
                          [e for c in range(C) for e in ((spread_sb, c), (att_sb, c))] + [(x1_sb, t) for t in range(T)], B)
            den_bank = self.banks(ctx, "a_den", 1)[0]
            block = ctx.enter_context(nc.Block())

            @block.sync
            def _(sp):
                with nc.allow_non_contiguous_dma(reason="small parameters, once"):
                    params.on(sp.dma_start(conv_w[:, :, :], io["L0_attn_conv_w"].rearrange("(c p) k -> p c k", p=P)))
                    params.on(sp.dma_start(conv_b[:, :], io["L0_attn_conv_b"].rearrange("(c p) -> p c", p=P)))
                    params.on(sp.dma_start(bp[:, :], io["L0_attn_bp"].rearrange("(a n) -> a n", a=1).to_broadcast([P, D])))

                def load(b):
                    xT_ps.wait(sp, b - 1)
                    N.loaded.on(sp.dma_start(x[:, :, :], self.token_rows(io["x"], b)))
                load(0)

                def step(new, old):
                    if old:
                        stored.wait(sp, old.b - 1)
                        res_in.on(sp.dma_start(res[:, :, :], self.token_rows(io["x"], old.b)))
                    if following(new, B):
                        load(new.b + 1)
                    if old:
                        x1_sb.wait(sp, old.b)
                        stored.on(sp.dma_start(self.token_rows(self.x1, old.b), res[:, :, :]))
                pipeline(sp, B, step)
                stored.wait(sp, B - 1)

            @block.gpsimd
            def _(pool):
                keep = lambda ap, base, pattern, mult: pool.affine_select(
                    out=ap, in_=ap, compare_op=ALU.is_ge, fill=0.0, base=base, pattern=pattern, channel_multiplier=mult)
                built.on(pool.memset(kv_mask[:, :, :], 1.0))
                built.on(pool.memset(head_mask[:, :, :], 1.0))
                built.on(pool.memset(head_rows[:, :, :].bitcast(F32), 1.0))
                built.on(pool.memset(v1[:, :, :, :], 1.0))
                for i in range(2):
                    pool.memset(kv[i].high[:, :].bitcast(F32), 0.0)
                    last = pool.memset(kv[i].low[:, :].bitcast(F32), 0.0)
                built.on(last)
                built.wait(pool, 0, 4)
                km = kv_mask[:, :, :].rearrange("p a (h e) -> p a h e", h=HC)
                built.on(keep(km, 0, [[0, 2], [-HD, HC], [0, HD]], 1))
                built.on(keep(head_mask[:, :, :], 0, [[HC * HD, C], [-HD, HEADS]], 1))
                hr = head_rows[:, :, :].rearrange("h c (a e) -> h c a e", a=HC)
                built.on(keep(hr, 0, [[-HC, C], [-1, HC], [0, HD]], 1))
                built.wait(pool, 0, 7)
                built.on(keep(km, HD - 1, [[0, 2], [HD, HC], [0, HD]], -1))
                built.on(keep(head_mask[:, :, :], HD - 1, [[-HC * HD, C], [HD, HEADS]], -1))
                built.on(keep(hr, 0, [[HC, C], [1, HC], [0, HD]], -1))
                params.wait(pool, 0)
                self.norm_power(pool, N, 0)

                def step(new, old):
                    if old:
                        res_in.wait(pool, old.b)
                        for t in range(T):
                            res_bp.on(pool.tensor_tensor(res[:, t, :], res[:, t, :], bp[:, :], ALU.add))
                        for c in range(C):
                            att_sb.wait(pool, old.b, c)
                            z_f.on(pool.tensor_tensor(att[c % 2][:, :], att[c % 2][:, :], local[old.par][:, c, :], ALU.add))
                    if following(new, B):
                        self.norm_power(pool, N, new.b + 1)
                    if new:
                        for c in range(C):
                            q_hi.wait(pool, new.b, c)
                            q_lo.on(pool.tensor_tensor(q[new.par].low[:, c, :], elu[:, c % 2, :],
                                                       q[new.par][:, c, :].high_f32(), ALU.subtract))
                pipeline(pool, B, step)

            @block.scalar
            def _(act):
                params.wait(act, 0)
                built.wait(act, 0)

                def step(new, old):
                    def elu_front(u):
                        kq_ps.wait(act, new.b, u)
                        if u < 2:
                            kv_lo.wait(act, new.b - 1)
                        elif u - 2 < T:
                            elu_out.wait(act, new.b, u - 2)
                        else:
                            q_lo.wait(act, new.b, u - 2 - T)
                        bank = first.banks[(C + u if u < T else C + T + u) % 3]
                        elu_neg.on(act.activation(elu[:, u % 2, :], bank[:, :], ACT.Relu, scale=-1.0))
                        elu_neg.wait(act, new.b, u)
                        elu_exp.on(act.activation(elu[:, u % 2, :], elu[:, u % 2, :], ACT.Exp, scale=-1.0))

                    def q_high(c):
                        elu_out.wait(act, new.b, T + c)
                        q_hi.on(act.activation(q[new.par].high[:, c, :], elu[:, c % 2, :], ACT.Copy))

                    def spread_copy(c):
                        spread_ps.wait(act, old.b, c)
                        z_lo.wait(act, old.b if c >= 2 else old.b - 1, c - 2 if c >= 2 else C + c - 2)
                        spread_sb.on(act.activation(att[c % 2][:, :], second.banks[2 * c % 4][:, :], ACT.Copy))

                    def z_high(c):
                        z_f.wait(act, old.b, c)
                        if c == 0:
                            out_ps.wait(act, old.b - 1)
                        z_hi.on(act.activation(z.high[:, c, :], att[c % 2][:, :], ACT.Copy))

                    if new:
                        for c in range(C):
                            xT_ps.wait(act, new.b, c)
                            if c == 0:
                                kq_ps.wait(act, new.b - 1)
                            bank = first.banks[c % 3]
                            xT_hi.on(act.activation(xT.high[:, c, :], bank[:, :], ACT.Copy))
                            tap1.on(act.activation(local[new.par][:, c, :], bank[:, :], ACT.Identity,
                                                   bias=conv_b[:, c:c + 1], scale=conv_w[:, c, 1:2]))
                        for u in range(T):
                            elu_front(u)
                    if old:
                        rden_f.wait(act, old.b)
                        spread_ps.wait(act, old.b - 1)
                        rden_hi.on(act.activation(rden_s.high[:, :], rden[:, :], ACT.Copy))
                        for c in range(C):
                            spread_copy(c)
                            if c >= 1:
                                z_high(c - 1)
                        z_high(C - 1)
                    if new:
                        for t in range(T):
                            v_ps.wait(act, new.b, t)
                            if t == 0:
                                kv_ps.wait(act, new.b - 1)
                            v_sb.on(act.activation(v1[:, t, :, 0:P],
                                                   first.banks[(C + T + t) % 3][:, :].rearrange("p (c e) -> p c e", c=C), ACT.Copy))
                        for c in range(C):
                            elu_front(T + c)
                            if c >= 1:
                                q_high(c - 1)
                        q_high(C - 1)
                        for g in range(2):
                            kv_part.wait(act, new.b, 3 * g + 2)
                        kv_hi.on(act.activation(kv[new.par].high[:, 0:C * KVW].rearrange("p (c e) -> p c e", c=C),
                                                kv_f, ACT.Copy))
                pipeline(act, B, step)

            @block.vector
            def _(dve):
                params.wait(dve, 0)
                built.wait(dve, 0)
                self.norm_stats(dve, N, 0, x)
                self.norm_apply(dve, N, 0, x, N.scale, N.rstd)

                def step(new, old):
                    def elu_back(u):
                        elu_exp.wait(dve, new.b, u)
                        bank = first.banks[(C + u if u < T else C + T + u) % 3]
                        if u < T:
                            if u == 0:
                                kv_ps.wait(dve, new.b - 1)
                            dst = k[:, u, :]
                        else:
                            c = u - T
                            dst = elu[:, c % 2, :]
                        elu_out.on(dve.scalar_tensor_tensor(out=dst, in0=bank[:, :], scalar=0.0, in1=elu[:, u % 2, :],
                                                            op0=ALU.max, op1=ALU.add))

                    if new:
                        for c in range(C):
                            tap1.wait(dve, new.b, c)
                            bank, loc = first.banks[c % 3], local[new.par]
                            xT_lo.on(dve.tensor_tensor(xT.low[:, c, :], bank[:, :], xT[:, c, :].high_f32(), ALU.subtract))
                            tap0.on(dve.scalar_tensor_tensor(out=loc[:, c, 1:S], in0=bank[:, 0:S - 1], scalar=conv_w[:, c, 0:1],
                                                             in1=loc[:, c, 1:S], op0=ALU.mult, op1=ALU.add))
                            tap0.wait(dve, new.b, c)
                            tap2.on(dve.scalar_tensor_tensor(out=loc[:, c, 0:S - 1], in0=bank[:, 1:S], scalar=conv_w[:, c, 2:3],
                                                             in1=loc[:, c, 0:S - 1], op0=ALU.mult, op1=ALU.add))
                    if old:
                        den_ps.wait(dve, old.b)
                        den_max.on(dve.tensor_scalar(rden[:, :], den_bank[0:HEADS, :], 1e-6, None, ALU.max))
                        den_max.wait(dve, old.b)
                        rden_f.on(dve.reciprocal(rden[:, :], rden[:, :]))
                    if new:
                        for u in range(T):
                            elu_back(u)
                    if old:
                        rden_hi.wait(dve, old.b)
                        rden_lo.on(dve.tensor_tensor(rden_s.low[:, :], rden[:, :], rden_s[:, :].high_f32(), ALU.subtract))

                        def z_low(c):
                            z_hi.wait(dve, old.b, c)
                            z_lo.on(dve.tensor_tensor(z.low[:, c, :], att[c % 2][:, :], z[:, c, :].high_f32(), ALU.subtract))
                        for c in range(C):
                            spread_sb.wait(dve, old.b, c)
                            att_ps.wait(dve, old.b, c)
                            att_sb.on(dve.tensor_tensor(att[c % 2][:, :], second.banks[(2 * c + 1) % 4][:, :], att[c % 2][:, :], ALU.mult))
                            if c >= 1:
                                z_low(c - 1)
                        z_low(C - 1)
                    if following(new, B):
                        self.norm_stats(dve, N, new.b + 1, x)
                        self.norm_apply(dve, N, new.b + 1, x, N.scale, N.rstd)
                    if new:
                        for c in range(C):
                            elu_back(T + c)
                    if new:
                        q_lo.wait(dve, new.b)
                        for g in range(2):
                            kv_ps.wait(dve, new.b, g)
                            bank = first.banks[(2 * C + 2 * T + g) % 3][:, 0:2 * (P + 2)].rearrange("p (c e) -> p c e", c=2)
                            kv_part.on(dve.tensor_tensor(kv_f[:, 2 * g:2 * g + 2, 0:P], bank[:, :, 0:P], kv_mask[:, :, :], ALU.mult))
                            for i in range(2):
                                kv_part.on(dve.tensor_scalar(kv_f[:, 2 * g + i, P:KVW], head_mask[:, 2 * g + i, :],
                                                             bank[:, i, P:P + 1], None, ALU.mult))
                        kv_hi.wait(dve, new.b)
                        kv_part.wait(dve, new.b)
                        both = lambda ap: ap[:, 0:C * KVW].rearrange("p (c e) -> p c e", c=C)
                        kv_lo.on(dve.tensor_tensor(both(kv[new.par].low), kv_f, both(kv[new.par].high).bitcast(F32), ALU.subtract))
                    if old:
                        for t in range(T):
                            res_bp.wait(dve, old.b, t)
                            out_ps.wait(dve, old.b, t)
                            x1_sb.on(dve.tensor_tensor(res[:, t, :], second.banks[(2 * C + t) % 4][:, :], res[:, t, :], ALU.add))
                pipeline(dve, B, step)

            @block.tensor
            def _(pe):
                built.wait(pe, 0)

                def step(new, old):
                    if new:
                        for c in range(C):
                            bank = first.take(pe, new.b, c)
                            if c == 0:
                                N.normed.wait(pe, new.b)
                            xT_ps.on(self.turn(pe, bank, x, c))
                    if old:
                        rden_f.wait(pe, old.b - 1)
                        kv_lo.wait(pe, old.b)
                        for c in range(C):
                            q_lo.wait(pe, old.b, c)
                            mm = product(pe, den_bank[:, :], kv[old.par][:, c * KVW + P:c * KVW + 2 * P],
                                         q[old.par][:, c, :], c == 0, c == C - 1)
                        den_ps.on(mm)
                    if new:
                        for t in range(T):
                            bank = first.take(pe, new.b, C + t)
                            for c in range(C):
                                if t == 0:
                                    xT_lo.wait(pe, new.b, c)
                                mm = product(pe, bank[:, :], xT[:, c, t * P:(t + 1) * P], w["Wk"][:, c, :], c == 0, c == C - 1)
                            kq_ps.on(mm)
                    if old:
                        rden_lo.wait(pe, old.b)
                        for c in range(C):
                            bank = second.take(pe, old.b, 2 * c)
                            pe.matmul(bank[:, :], head_rows[:, c, :], rden_s.high[:, :], start=True, stop=False)
                            spread_ps.on(pe.matmul(bank[:, :], head_rows[:, c, :], rden_s.low[:, :], start=False, stop=True))
                            bank = second.take(pe, old.b, 2 * c + 1)
                            att_ps.on(product(pe, bank[:, :], kv[old.par][:, c * KVW:c * KVW + P], q[old.par][:, c, :], True, True))
                    if new:
                        for t in range(T):
                            bank = first.take(pe, new.b, C + T + t)
                            for c in range(C):
                                mm = product(pe, bank[:, :], xT[:, c, t * P:(t + 1) * P], w["Wv"][:, c, :], c == 0, c == C - 1)
                            v_ps.on(mm)
                    if new:
                        for o in range(C):
                            bank = first.take(pe, new.b, C + 2 * T + o)
                            for c in range(C):
                                mm = product(pe, bank[:, :], w["Wq"][:, c, o * P:(o + 1) * P], xT[:, c, :], c == 0, c == C - 1)
                            kq_ps.on(mm)
                    if new:
                        v_sb.wait(pe, new.b)
                        elu_out.wait(pe, new.b, T - 1)
                        for g in range(2):
                            bank = first.take(pe, new.b, 2 * C + 2 * T + g)
                            for i in range(2):
                                c = 2 * g + i
                                for t in range(T):
                                    mm = pe.matmul(bank[:, i * (P + 2):(i + 1) * (P + 2)], k[:, t, c * P:(c + 1) * P],
                                                   v1[:, t, c, :], start=(t == 0), stop=(t == T - 1))
                            kv_ps.on(mm)
                    if old:
                        for t in range(T):
                            bank = second.take(pe, old.b, 2 * C + t)
                            for c in range(C):
                                if t == 0:
                                    z_lo.wait(pe, old.b, c)
                                mm = product(pe, bank[:, :], z[:, c, t * P:(t + 1) * P], w["Wp"][:, c, :], c == 0, c == C - 1)
                            out_ps.on(mm)
                pipeline(pe, B, step)

    def phase_b(self):
        nc, io, B, C, T, D, S = self.nc, self.io, self.B, self.C, self.T, self.D, self.S
        H, _, HD = io["L0_xattn_q_w"].shape
        BIG = 2.0 ** 100
        with Scope(self.nc) as ctx:
            qw = self.split(ctx, "b_qw", [P, C, H * HD])
            kvw = self.split(ctx, "b_kvw", [P, C, 2 * HD])
            ow = self.split(ctx, "b_ow", [P, H, D])
            columns = lambda dram, n: [(dram[i, :, :].rearrange("(c p) h -> p c h", p=P), i * HD) for i in range(n)]
            self.load_weights("bw", [
                ("scale", columns(io["L0_xattn_q_w"], H), H * HD, qw),
                ("scale", columns(io["L0_xattn_kv_w"].rearrange("a k d h -> (a k) d h"), 2), 2 * HD, kvw),
                ("keep", [(io["L0_xattn_out_w"].rearrange("n h d -> h n d"), 0)], D, ow)],
                io["L0_xattn_rms_scale"])
            sb = lambda n, s, d=F32: self.sb(ctx, f"b_{n}", s, d)
            ev = lambda n, per=1, unit=1: Event(ctx, nc, f"b_{n}", per, unit)
            x = sb("x", [P, T, D])
            mem = sb("mem", [P, T, D])
            nT = self.split(ctx, "b_nT", [P, C, S])
            q = self.split(ctx, "b_q", [P, H, S])
            k = [self.split(ctx, f"b_k{i}", [P, S]) for i in range(2)]
            v = [self.split(ctx, f"b_v{i}", [P, T, HD]) for i in range(2)]
            p_f = sb("p_f", [P, T, S])
            p = self.split(ctx, "b_p", [P, T, S])
            psum = sb("psum", [P, S])
            enc_f = sb("enc_f", [P, H, S])
            enc = self.split(ctx, "b_enc", [P, H, S])
            res = sb("res", [P, T, D])
            cos_q, sin_q = sb("cos_q", [P, S]), sb("sin_q", [P, S])
            cos_k, sin_k = sb("cos_k", [P, T, HD]), sb("sin_k", [P, T, HD])
            rope_f = [sb(f"rope{i}", [P, S]) for i in range(2)]
            rope_swap = sb("rope_swap", [P, S])
            k_f = sb("k_f", [P, T, HD])
            mask_u8 = sb("mask_u8", [P, S], U8)
            mask_row = sb("mask_row", [P, S])
            unused = [sb(f"unused{i}", [P, S], mybir.dt.bfloat16) for i in range(4)]
            carrier = sb("carrier", [P, 4])
            unused_sq = [sb(f"unused_sq{i}", [P, D], mybir.dt.bfloat16) for i in range(2)]
            mask_any = sb("mask_any", [P, 1])
            p_scale, p_bias = sb("p_scale", [P, T]), sb("p_bias", [P, T])
            top = sb("top", [P, T, H])
            top_row = sb("top_row", [H, S], F32R)
            rsum = sb("rsum", [P, T, H])
            rsum_s = self.split(ctx, "b_rsums", [H, S])
            head_row = sb("head_row", [H, H, P], F32R)
            minus_row = sb("minus_row", [H, H, P], F32R)
            ones = sb("ones", [P, 1])
            sumsq, mem_ms, mem_scale = sb("sumsq", [P, T]), sb("mem_ms", [P, T]), sb("mem_scale", [P, T])
            one_in_d, rms_eps = sb("one_in_d", [P, T]), sb("rms_eps", [P, T])
            n_sq, n_rms, n_scale = sb("n_sq", [P, T]), sb("n_rms", [P, T]), sb("n_scale", [P, T])
            N = self.norm_events(ctx, "b_ln")
            params, built = ev("params", 4, 16), ev("built", 5)
            mem_in, sq, ms, mscale, mem_n = ev("mem_in", 1, 16), ev("sq", T), ev("ms", 2), ev("mscale"), ev("mem_n", T)
            nsteps, nscale = ev("nsteps", 4), ev("nscale")
            memT_ps, memT_hi, memT_lo = ev("memT_ps", C), ev("memT_hi", C), ev("memT_lo", C)
            kv_ps, v_hi, v_lo = ev("kv_ps", 2), ev("v_hi", 2), ev("v_lo", 2)
            k_cos, k_swap, k_rope = ev("k_cos", 2), ev("k_swap", 4), ev("k_rope", 2)
            kT_ps, k_hi, k_lo = ev("kT_ps"), ev("k_hi"), ev("k_lo")
            xT_ps, xT_hi, xT_lo = ev("xT_ps", C), ev("xT_hi", C), ev("xT_lo", C)
            q_ps, q_cos, q_swap, q_rope = ev("q_ps", H), ev("q_cos", H), ev("q_swap", 2 * H), ev("q_rope", H)
            q_hi, q_lo = ev("q_hi", H), ev("q_lo", H)
            mask_in, mask_f, mask_max, mask_ps, mask_sb = ev("mask_in", 1, 16), ev("mask_f"), ev("mask_max"), ev("mask_ps"), ev("mask_sb", 2)
            top_ps, top_sb, row_ps, row_sb = ev("top_ps", T * H), ev("top_sb", T * H), ev("row_ps"), ev("row_sb")
            st_ps, p_exp, p_hi, p_lo = ev("st_ps", H * T), ev("p_exp", H * T), ev("p_hi", H * T), ev("p_lo", H * T)
            add = ev("add", 3 * H)
            enc_ps, enc_sb, sum_ps = ev("enc_ps", H * T), ev("enc_sb", H), ev("sum_ps", H)
            rsum_f, rrow_ps, rsum_hi, rsum_lo = ev("rsum_f"), ev("rrow_ps"), ev("rsum_hi"), ev("rsum_lo")
            spread_ps, enc_n, enc_hi, enc_lo = ev("spread_ps", H), ev("enc_n", H), ev("enc_hi", H), ev("enc_lo", H)
            out_ps, x2_sb = ev("out_ps", T), ev("x2_sb", T)
            res_in, stored = ev("res_in", 1, 16), ev("stored", 1, 16)
            KV, XT, KT, Q = C, C + 2, 2 * C + 2, 2 * C + 3
            first = Ring(self.banks(ctx, "b_p", 3),
                         [(memT_lo, c) for c in range(C)] + [(k_swap, 1), (k_swap, 3)] + [(xT_lo, c) for c in range(C)]
                         + [(k_lo, 0)] + [(q_swap, 2 * h + 1) for h in range(H)], B)
            order = [("st", i) for i in range(2 * T)]
            for h in range(1, H):
                st = [("st", (h + 1) * T + i) for i in range(T)] if h < H - 1 else []
                top_2 = [[("top", (h - 1) * T + i), ("top", (h - 1) * T + i + 1)] for i in (0, 2)]
                order += st[:3] + ([] if st else [("rrow", 0)]) + top_2[0] + st[3:] + top_2[1]
            order += [("spread", h) for h in range(H)] + [("out", 0), ("out", 1)] + [("top", (H - 1) * T + i) for i in range(T)]
            order += [("out", 2), ("row", 0), ("out", 3)]
            reader = {"top": (top_sb, 0), "row": (row_sb, 0), "st": (p_exp, 1), "rrow": (rsum_lo, 1), "spread": (enc_n, 1), "out": (x2_sb, 1)}
            second = Ring(self.banks(ctx, "b_r", 3), [(reader[kind][0], i, reader[kind][1]) for kind, i in order], B)
            job = {o: n for n, o in enumerate(order)}
            bank_of = lambda kind, i: second.banks[job[kind, i] % 3]
            enc_bank = self.banks(ctx, "b_enc", 1)[0]
            aux = self.banks(ctx, "b_aux", 1)[0]
            MASK = T * H
            block = ctx.enter_context(nc.Block())

            @block.sync
            def _(sp):
                for tile, name in ((cos_q[:, :], "cos_q"), (sin_q[:, :], "sin_q"), (cos_k[:, :, :], "cos_k"), (sin_k[:, :, :], "sin_k")):
                    view = io[name] if name.endswith("q") else io[name].rearrange("(t p) h -> p t h", p=P)
                    params.on(sp.dma_start(tile, view))

                def load_mem(b):
                    memT_ps.wait(sp, b - 1)
                    mem_in.on(sp.dma_start(mem[:, :, :], self.token_rows(io["ctx_1024"], b)))

                def load_x(b):
                    xT_ps.wait(sp, b - 1)
                    N.loaded.on(sp.dma_start(x[:, :, :], self.token_rows(self.x1, b)))
                load_mem(0)
                load_x(0)

                def step(new, old):
                    if old:
                        stored.wait(sp, old.b - 1)
                        res_in.on(sp.dma_start(res[:, :, :], self.token_rows(self.x1, old.b)))
                    if following(new, B):
                        load_mem(new.b + 1)
                        load_x(new.b + 1)
                    if old:
                        x2_sb.wait(sp, old.b)
                        stored.on(sp.dma_start(self.token_rows(self.x2, old.b), res[:, :, :]))
                pipeline(sp, B, step)
                stored.wait(sp, B - 1)

            @block.gpsimd
            def _(pool):
                built.on(pool.memset(head_row[:, :, :].bitcast(F32), 0.0))
                built.on(pool.memset(minus_row[:, :, :].bitcast(F32), 0.0))
                pool.memset(one_in_d[:, :], 1.0 / D)
                pool.memset(rms_eps[:, :], 1e-6)
                built.on(pool.memset(ones[:, :], 1.0))
                built.wait(pool, 0, 2)
                for tile, value in ((head_row, 1.0), (minus_row, -1.0)):
                    built.on(pool.affine_select(out=tile[:, :, :], in_=tile[:, :, :], compare_op=ALU.not_equal, fill=value,
                                                base=0, pattern=[[-1, H], [0, P]], channel_multiplier=1))

                def mem_power(b):
                    sq.wait(pool, b)
                    ms.on(pool.tensor_tensor(mem_ms[:, :], sumsq[:, :], one_in_d[:, :], ALU.mult))
                    ms.wait(pool, b, 0)
                    ms.on(pool.tensor_tensor(mem_ms[:, :], mem_ms[:, :], rms_eps[:, :], ALU.add))
                    ms.wait(pool, b, 1)
                    mem_n.wait(pool, b - 1)
                    mscale.on(pool.tensor_tensor(mem_scale[:, :], mem_ms[:, :], self.minus_half[:, 0:T], ALU.pow))

                def x_power(b):
                    self.norm_power(pool, N, b)
                    own = lambda i, ins: (nsteps.on(ins), nsteps.wait(pool, b, i))
                    N.rstd.wait(pool, b)
                    own(0, pool.tensor_tensor(n_sq[:, :], N.scale[:, :], N.scale[:, :], ALU.mult))
                    own(1, pool.tensor_tensor(n_rms[:, :], n_sq[:, :], N.mv[:, :, 1], ALU.mult))
                    own(2, pool.tensor_tensor(n_sq[:, :], n_rms[:, :], rms_eps[:, :], ALU.add))
                    own(3, pool.tensor_tensor(n_rms[:, :], n_sq[:, :], self.minus_half[:, 0:T], ALU.pow))
                    nscale.on(pool.tensor_tensor(n_scale[:, :], n_rms[:, :], N.scale[:, :], ALU.mult))
                mem_power(0)
                x_power(0)

                def step(new, old):
                    def adds(h):
                        sum_ps.wait(pool, old.b if h else old.b - 1, (h - 1) % H)
                        for i in range(1, T):
                            p_exp.wait(pool, old.b, h * T + i)
                            add.on(pool.tensor_tensor(psum[:, :], p_f[:, 0, :] if i == 1 else psum[:, :], p_f[:, i, :], ALU.add))
                            if i < T - 1:
                                add.wait(pool, old.b, 3 * h + i - 1)

                    def query_low(h):
                        q_hi.wait(pool, new.b, h)
                        q_lo.on(pool.tensor_tensor(q.low[:, h, :], rope_f[h % 2][:, :], q[:, h, :].high_f32(), ALU.subtract))

                    if old:
                        adds(0)
                        adds(1)
                    if new:
                        query_low(0)
                    if old:
                        adds(2)
                    if following(new, B):
                        mem_power(new.b + 1)
                    if new:
                        query_low(1)
                    if following(new, B):
                        x_power(new.b + 1)
                    if old:
                        adds(3)
                    if new:
                        query_low(2)
                        query_low(3)
                pipeline(pool, B, step)

            @block.scalar
            def _(act):
                def squares(b):
                    mem_in.wait(act, b)
                    ms.wait(act, b - 1)
                    for t in range(T):
                        sq.wait(act, b if t >= 2 else b - 1, (t - 2) % T)
                        sq.on(act.activation(unused_sq[t % 2][:, :], mem[:, t, :], ACT.Square, accum_out=sumsq[:, t:t + 1]))
                def mem_apply(b):
                    mscale.wait(act, b)
                    sq.wait(act, b)
                    for t in range(T):
                        mem_n.on(act.activation(mem[:, t, :], mem[:, t, :], ACT.Copy, scale=mem_scale[:, t:t + 1]))

                def load_mask(b):
                    mask_f.wait(act, b - 1)
                    mask_in.on(act.dma_start(mask_u8[:, :], io["mask_BxS2_bk0"][b, :].rearrange("(a s) -> a s", a=1).to_broadcast([P, S])))
                squares(0)
                load_mask(0)
                mem_apply(0)
                built.wait(act, 0)

                def step(new, old):
                    def turned(ps, hi, c, bank, free):
                        ps.wait(act, new.b, c)
                        if c == 0:
                            free(act)
                        hi.on(act.activation(nT.high[:, c, :], bank[:, :], ACT.Copy))

                    def exp(j):
                        h, i = divmod(j, T)
                        st_ps.wait(act, old.b, j)
                        if h:
                            p_lo.wait(act, old.b, j - T)
                            add.wait(act, old.b, 3 * (h - 1) + max(i, 1) - 1)
                        else:
                            p_lo.wait(act, old.b - 1, j + (H - 1) * T)
                            add.wait(act, old.b - 1, 3 * (H - 1) + max(i, 1) - 1)
                        p_exp.on(act.activation(p_f[:, i, :], bank_of("st", j)[:, :], ACT.Exp,
                                                bias=p_bias[:, i:i + 1], scale=p_scale[:, i:i + 1]))

                    def p_high(j):
                        h, i = divmod(j, T)
                        enc_ps.wait(act, old.b if h else old.b - 1, (h - 1) % H * T + i)
                        p_exp.wait(act, old.b, j)
                        p_hi.on(act.activation(p.high[:, i, :], p_f[:, i, :], ACT.Copy))

                    def enc_copy(h):
                        enc_ps.wait(act, old.b, h * T + T - 1)
                        enc_sb.on(act.activation(enc_f[:, h, :], enc_bank[:, :], ACT.Copy))

                    def query_high(h):
                        if old:
                            st_ps.wait(act, old.b, h * T + T - 1)
                        q_rope.wait(act, new.b, h)
                        q_hi.on(act.activation(q.high[:, h, :], rope_f[h % 2][:, :], ACT.Copy))

                    def memory_high(c):
                        turned(memT_ps, memT_hi, c, first.banks[c % 3], lambda e: q_ps.wait(e, new.b - 1))

                    if old:
                        mask_sb.wait(act, old.b)
                    if new:
                        memory_high(0)
                        memory_high(1)
                    for i in range(T):
                        if old:
                            exp(i)
                        if new and i < 2:
                            memory_high(i + 2)
                        if old:
                            p_high(i)
                    if new:
                        for g in range(2):
                            kv_ps.wait(act, new.b, g)
                            v_hi.on(act.activation(v[new.par].high[:, 2 * g:2 * g + 2, :],
                                                   first.banks[(KV + g) % 3][:, :].rearrange("p (t n) -> p t n", t=2)[:, :, HD:2 * HD],
                                                   ACT.Copy))
                    for i in range(T):
                        if old:
                            exp(T + i)
                            p_high(T + i)
                        if new:
                            turned(xT_ps, xT_hi, i, first.banks[(XT + i) % 3], lambda e: kv_ps.wait(e, new.b))
                    if new:
                        kT_ps.wait(act, new.b)
                        k_hi.on(act.activation(k[new.par].high[:, :], first.banks[KT % 3][:, :], ACT.Copy))
                    if following(new, B):
                        load_mask(new.b + 1)
                    for h in range(1, H):
                        if old:
                            enc_copy(h - 1)
                        for i in range(T):
                            if old and h < H - 1:
                                exp((h + 1) * T + i)
                                p_high((h + 1) * T + i)
                            if new and i == 1:
                                query_high(h - 1)
                        if following(new, B):
                            if h == 1:
                                squares(new.b + 1)
                            if h == 2:
                                mem_apply(new.b + 1)
                    if old:
                        rrow_ps.wait(act, old.b)
                        spread_ps.wait(act, old.b - 1)
                        rsum_hi.on(act.activation(rsum_s.high[:, :], bank_of("rrow", 0)[0:H, :], ACT.Copy))
                        enc_copy(H - 1)
                        for h in range(H):
                            enc_n.wait(act, old.b, h)
                            if h == 0:
                                out_ps.wait(act, old.b - 1)
                            enc_hi.on(act.activation(enc.high[:, h, :], enc_f[:, h, :], ACT.Copy))
                    if new:
                        query_high(H - 1)
                pipeline(act, B, step)

            @block.vector
            def _(dve):
                self.norm_stats(dve, N, 0, x)
                self.norm_apply(dve, N, 0, x, n_scale, nscale)
                params.wait(dve, 0)
                built.wait(dve, 0)

                def step(new, old):
                    def turned(hi, lo, c, bank):
                        hi.wait(dve, new.b, c)
                        lo.on(dve.tensor_tensor(nT.low[:, c, :], bank[:, :], nT[:, c, :].high_f32(), ALU.subtract))

                    def top_logits(j):
                        top_sb.wait(dve, new.b if j >= 4 else new.b - 1, (j - 3) % (T * H))
                        top_ps.wait(dve, new.b, j + 1)
                        dve.memset(carrier[:, j // 2 % 4:j // 2 % 4 + 1], 0.0)
                        for i in (j, j + 1):
                            h, t = divmod(i, T)
                            top_sb.on(dve.tensor_tensor_reduce(out=unused[i % 4][:, :], in0=bank_of("top", i)[:, :], in1=mask_row[:, :],
                                                               scale=1.0, scalar=-3e38, op0=ALU.add, op1=ALU.max,
                                                               accum_out=top[:, t, h:h + 1]))

                    def keys(g):
                        v_hi.wait(dve, new.b, g)
                        bank = first.banks[(KV + g) % 3][:, :].rearrange("p (t n) -> p t n", t=2)
                        tiles, half = slice(2 * g, 2 * g + 2), HD // 2
                        v_lo.on(dve.tensor_tensor(v[new.par].low[:, tiles, :], bank[:, :, HD:2 * HD], v[new.par][:, tiles, :].high_f32(), ALU.subtract))
                        swap = rope_swap[:, g * 2 * HD:(g + 1) * 2 * HD].rearrange("p (t n) -> p t n", t=2)
                        k_cos.on(dve.tensor_tensor(k_f[:, tiles, :], bank[:, :, 0:HD], cos_k[:, tiles, :], ALU.mult))
                        q_rope.wait(dve, new.b - 1)
                        k_swap.on(dve.tensor_tensor(swap[:, :, 0:half], bank[:, :, half:HD], sin_k[:, tiles, 0:half], ALU.mult))
                        k_swap.on(dve.tensor_tensor(swap[:, :, half:HD], bank[:, :, 0:half], sin_k[:, tiles, half:HD], ALU.mult))
                        k_cos.wait(dve, new.b, g)
                        k_swap.wait(dve, new.b, 2 * g + 1)
                        k_rope.on(dve.tensor_tensor(k_f[:, tiles, :], k_f[:, tiles, :], swap, ALU.add))

                    def p_low(j):
                        h, i = divmod(j, T)
                        p_hi.wait(dve, old.b, j)
                        p_lo.on(dve.tensor_tensor(p.low[:, i, :], p_f[:, i, :], p[:, i, :].high_f32(), ALU.subtract))

                    def query(h):
                        q_ps.wait(dve, new.b, h)
                        bank, half = first.banks[(Q + h) % 3], HD // 2
                        q_lo.wait(dve, new.b if h >= 2 else new.b - 1, (h - 2) % H)
                        q_cos.on(dve.tensor_tensor(rope_f[h % 2][:, :], bank[:, :], cos_q[:, :], ALU.mult))
                        if h:
                            q_rope.wait(dve, new.b, h - 1)
                        else:
                            k_rope.wait(dve, new.b)
                        q_swap.on(dve.tensor_tensor(rope_swap[0:half, :], bank[half:P, :], sin_q[half:P, :], ALU.mult))
                        q_swap.on(dve.tensor_tensor(rope_swap[half:P, :], bank[0:half, :], sin_q[0:half, :], ALU.mult))
                        q_cos.wait(dve, new.b, h)
                        q_swap.wait(dve, new.b, 2 * h + 1)
                        q_rope.on(dve.tensor_tensor(rope_f[h % 2][:, :], rope_f[h % 2][:, :], rope_swap[:, :], ALU.add))

                    def enc_low(h):
                        enc_hi.wait(dve, old.b, h)
                        enc_lo.on(dve.tensor_tensor(enc.low[:, h, :], enc_f[:, h, :], enc[:, h, :].high_f32(), ALU.subtract))

                    def memory_low(c):
                        turned(memT_hi, memT_lo, c, first.banks[c % 3])

                    def enc_norm(h):
                        spread_ps.wait(dve, old.b, h)
                        enc_sb.wait(dve, old.b, h)
                        enc_n.on(dve.tensor_tensor(enc_f[:, h, :], bank_of("spread", h)[:, :], enc_f[:, h, :], ALU.mult))

                    def residual(t):
                        out_ps.wait(dve, old.b, t)
                        x2_sb.on(dve.tensor_tensor(res[:, t, :], bank_of("out", t)[:, :], res[:, t, :], ALU.add))

                    if new:
                        memory_low(0)
                        memory_low(1)
                    for i in range(T):
                        if new and i < 2:
                            memory_low(i + 2)
                        if old:
                            p_low(i)
                    if new:
                        for g in range(2):
                            keys(g)
                    for i in range(T):
                        if old:
                            p_low(T + i)
                        if new:
                            turned(xT_hi, xT_lo, i, first.banks[(XT + i) % 3])
                    if new:
                        k_hi.wait(dve, new.b)
                        k_lo.on(dve.tensor_tensor(k[new.par].low[:, :], first.banks[KT % 3][:, :], k[new.par][:, :].high_f32(), ALU.subtract))
                        mask_in.wait(dve, new.b)
                        top_sb.wait(dve, new.b - 1)
                        mask_max.wait(dve, new.b - 1)
                        mask_ps.wait(dve, new.b - 1)
                        mask_f.on(dve.tensor_scalar(mask_row[:, :], mask_u8[:, :], -1.0, BIG, ALU.add, ALU.mult))
                        mask_f.wait(dve, new.b)
                        mask_sb.wait(dve, new.b - 1)
                        mask_max.on(dve.tensor_reduce(mask_any[:, :], mask_row[:, :], mybir.AxisListType.X, ALU.max))
                        query(0)
                    for h in range(1, H):
                        for i in range(T):
                            if old and h < H - 1:
                                p_low((h + 1) * T + i)
                            if old and h == H - 1 and i == 0:
                                sum_ps.wait(dve, old.b)
                                if new:
                                    mask_ps.wait(dve, new.b)
                                rsum_f.on(dve.reciprocal(rsum[:, :, :], aux[:, 0:T * H].rearrange("p (t h) -> p t h", t=T)))
                            if new and h == H - 1 and i == 0:
                                mask_ps.wait(dve, new.b)
                                mask_max.wait(dve, new.b)
                                if old:
                                    p_exp.wait(dve, old.b)
                                mask_sb.on(dve.tensor_scalar(p_scale[:, :], aux[:, MASK:MASK + T], 1.0 / BIG, 1.0, ALU.mult, ALU.add))
                                mask_sb.on(dve.tensor_scalar(p_bias[:, :], aux[:, MASK:MASK + T], mask_any[:, 0:1], None, ALU.subtract))
                            if new and h < H - 1 and i == 1:
                                query(h)
                            if old and h == H - 1 and i == T - 1:
                                rsum_hi.wait(dve, old.b)
                                rsum_lo.on(dve.tensor_tensor(rsum_s.low[:, :], bank_of("rrow", 0)[0:H, :], rsum_s[:, :].high_f32(), ALU.subtract))
                            if new and i >= 2:
                                top_logits((h - 1) * T + 2 * (i - 2))
                        if following(new, B):
                            if h == 1:
                                self.norm_stats(dve, N, new.b + 1, x)
                            if h == 2:
                                self.norm_apply(dve, N, new.b + 1, x, n_scale, nscale)
                    if old:
                        enc_norm(0)
                        for h in range(1, H):
                            enc_norm(h)
                            enc_low(h - 1)
                        enc_low(H - 1)
                        res_in.wait(dve, old.b)
                    if new:
                        query(H - 1)
                    if old:
                        residual(0)
                        residual(1)
                    if new:
                        top_logits((H - 1) * T)
                        top_logits((H - 1) * T + 2)
                    if old:
                        residual(2)
                    if new:
                        row_ps.wait(dve, new.b)
                        row_sb.on(dve.tensor_copy(top_row[:, :], bank_of("row", 0)[0:H, :]))
                    if old:
                        residual(3)
                pipeline(dve, B, step)

            @block.tensor
            def _(pe):
                built.wait(pe, 0)

                def step(new, old):
                    s = new.b if new else old.b + 1
                    take = lambda kind, i: second.take(pe, s, job[kind, i])

                    def turn_memory(c):
                        bank = first.take(pe, s, c)
                        if c == 0:
                            mem_n.wait(pe, new.b)
                        memT_ps.on(self.turn(pe, bank, mem, c))

                    def turn_x(c):
                        bank = first.take(pe, s, XT + c)
                        if c == 0:
                            N.normed.wait(pe, new.b)
                        xT_ps.on(self.turn(pe, bank, x, c))

                    def keys_values(g):
                        bank = first.take(pe, s, KV + g)
                        for i in range(2):
                            t = 2 * g + i
                            for c in range(C):
                                if t == 0:
                                    memT_lo.wait(pe, new.b, c)
                                mm = product(pe, bank[:, i * 2 * HD:(i + 1) * 2 * HD], nT[:, c, t * P:(t + 1) * P], kvw[:, c, :], c == 0, c == C - 1)
                        kv_ps.on(mm)

                    def turn_keys():
                        bank = first.take(pe, s, KT)
                        k_rope.wait(pe, new.b)
                        for t in range(T):
                            mm = pe.transpose(bank[:, t * P:(t + 1) * P], k_f[:, t, :], self.ident[:, :])
                        kT_ps.on(mm)

                    def queries(h):
                        bank = first.take(pe, s, Q + h)
                        for c in range(C):
                            if h == 0:
                                xT_lo.wait(pe, new.b, c)
                            mm = product(pe, bank[:, :], qw[:, c, h * HD:(h + 1) * HD], nT[:, c, :], c == 0, c == C - 1)
                        q_ps.on(mm)

                    def top_logits(h, tiles):
                        for t in tiles:
                            bank = take("top", h * T + t)
                            q_hi.wait(pe, new.b, h)
                            k_hi.wait(pe, new.b)
                            top_ps.on(pe.matmul(bank[:, :], q.high[:, h, t * P:(t + 1) * P], k[new.par].high[:, :], start=True, stop=True))

                    def logits(h, i):
                        j = h * T + i
                        bank = take("st", j)
                        if j == 0:
                            row_sb.wait(pe, old.b)
                            k_lo.wait(pe, old.b)
                        if i == 0:
                            q_lo.wait(pe, old.b, h)
                        pe.matmul(bank[:, :], minus_row[:, h, :], top_row[:, :], start=True, stop=False)
                        st_ps.on(product(pe, bank[:, :], k[old.par][:, i * P:(i + 1) * P], q[:, h, :], False, True))

                    def encode(h, i):
                        if i == 0:
                            enc_sb.wait(pe, old.b if h else old.b - 1, (h - 1) % H)
                            v_lo.wait(pe, old.b)
                        p_lo.wait(pe, old.b, h * T + i)
                        enc_ps.on(product(pe, enc_bank[:, :], v[old.par][:, i, :], p[:, i, :], i == 0, i == T - 1))

                    def total(h):
                        if h == 0:
                            rsum_f.wait(pe, old.b - 1)
                            mask_sb.wait(pe, old.b)
                        add.wait(pe, old.b, 3 * h + 2)
                        for t in range(T):
                            mm = pe.matmul(aux[:, t * H + h:t * H + h + 1], psum[:, t * P:(t + 1) * P], ones[:, :], start=True, stop=True)
                        sum_ps.on(mm)

                    def spread(h):
                        bank = take("spread", h)
                        if h == 0:
                            rsum_lo.wait(pe, old.b)
                        pe.matmul(bank[:, :], head_row[:, h, :], rsum_s.high[:, :], start=True, stop=False)
                        spread_ps.on(pe.matmul(bank[:, :], head_row[:, h, :], rsum_s.low[:, :], start=False, stop=True))

                    def out(t):
                        bank = take("out", t)
                        for h in range(H):
                            if t == 0:
                                enc_lo.wait(pe, old.b, h)
                            mm = product(pe, bank[:, :], enc[:, h, t * P:(t + 1) * P], ow[:, h, :], h == 0, h == H - 1)
                        out_ps.on(mm)

                    if new:
                        turn_memory(0)
                        turn_memory(1)
                    for i in range(T):
                        if old:
                            logits(0, i)
                        if new and i < 2:
                            turn_memory(i + 2)
                    if new:
                        keys_values(0)
                        keys_values(1)
                    for i in range(T):
                        if old:
                            logits(1, i)
                            encode(0, i)
                            if i == 1:
                                total(0)
                        if new:
                            turn_x(i)
                    if new:
                        turn_keys()
                        queries(0)
                    for h in range(1, H):
                        last = h == H - 1
                        if last and old:
                            total(h)
                        if last and new:
                            mask_f.wait(pe, new.b)
                            mask_sb.wait(pe, new.b - 1)
                            for i in range(T):
                                mm = pe.matmul(aux[:, MASK + i:MASK + i + 1], mask_row[0:1, i * P:(i + 1) * P], ones[0:1, :], start=True, stop=True)
                            mask_ps.on(mm)
                        for i in range(T):
                            if old and not last:
                                logits(h + 1, i)
                            if old:
                                encode(h, i)
                            if i == 1 and not last:
                                if old:
                                    total(h)
                                if new:
                                    queries(h)
                            if i == 1 and last and old:
                                bank = take("rrow", 0)
                                rsum_f.wait(pe, old.b)
                                for t in range(T):
                                    mm = pe.matmul(bank[0:H, t * P:(t + 1) * P], rsum[:, t, :], self.ident[:, :], start=True, stop=True)
                                rrow_ps.on(mm)
                            if new and i >= 2:
                                top_logits(h - 1, (2 * i - 4, 2 * i - 3))
                    if old:
                        for h in range(H):
                            spread(h)
                    if new:
                        queries(H - 1)
                    if old:
                        out(0)
                        out(1)
                    if new:
                        top_logits(H - 1, range(T))
                    if old:
                        out(2)
                    if new:
                        bank = take("row", 0)
                        top_sb.wait(pe, new.b)
                        for t in range(T):
                            mm = pe.matmul(bank[0:H, t * P:(t + 1) * P], top[:, t, :], self.ident[:, :], start=True, stop=True)
                        row_ps.on(mm)
                    if old:
                        out(3)
                pipeline(pe, B, step)

    def phase_c(self, state):
        nc, io, B, C, T, D, S = self.nc, self.io, self.B, self.C, self.T, self.D, self.S
        GATES = "icf"
        with Scope(self.nc) as ctx:
            w = {g: self.split(ctx, f"c_w{g}", [P, C, D]) for g in GATES}
            u = {g: self.split(ctx, f"c_u{g}", [P, C, D]) for g in GATES}
            self.load_weights("cw", [("turn", io[f"L0_ffn_{k}{g}"], D, t[g]) for g in GATES for k, t in (("w", w), ("u", u))])
            sb = lambda n, s, d=F32: self.sb(ctx, f"c_{n}", s, d)
            ev = lambda n, per=1, unit=1: Event(ctx, nc, f"c_{n}", per, unit)
            x = sb("x", [P, T, D])
            nT = [self.split(ctx, f"c_nT{i}", [P, C, S]) for i in range(2)]
            c_f = sb("c_f", [P, C, S])
            gate = sb("gate", [P, 2, 3, S])
            bias = sb("bias", [P, 3, C])
            c_in = sb("c_in", [P, C])
            N = self.norm_events(ctx, "c_ln")
            params, zero, start_f, start_hi, start = ev("params", 4, 16), ev("zero"), ev("start_f", C), ev("start_hi"), ev("start")
            xT_ps, xT_hi, xT_lo = ev("xT_ps", C), ev("xT_hi", C), ev("xT_lo", C)
            gate_ps, gate_sb = ev("gate_ps", 3 * C), ev("gate_sb", 3 * C)
            ig, fc, c_new, c_hi, c_lo = ev("ig", C), ev("fc", C), ev("c_new", C), ev("c_hi", C), ev("c_lo", C)
            turning = Ring(self.banks(ctx, "c_t", 2), [(xT_lo, c) for c in range(C)], self.B)
            gating = Ring(self.banks(ctx, "c_g", 6), [(gate_sb, n) for n in range(3 * C)], self.B)
            block = ctx.enter_context(nc.Block())

            @block.sync
            def _(sp):
                with nc.allow_non_contiguous_dma(reason="small parameters, once"):
                    for i, g in enumerate(GATES):
                        params.on(sp.dma_start(bias[:, i, :], io[f"L0_ffn_b{g}"].rearrange("(c p) -> p c", p=P)))
                    params.on(sp.dma_start(c_in[:, :], io["L0_ffn_in_c"].rearrange("(c p) -> p c", p=P)))

                def load(b):
                    xT_ps.wait(sp, b - 1)
                    N.loaded.on(sp.dma_start(x[:, :, :], self.token_rows(self.x2, b)))
                load(0)

                def step(new, old):
                    if following(new, B):
                        load(new.b + 1)
                pipeline(sp, B, step)

            @block.gpsimd
            def _(pool):
                self.norm_power(pool, N, 0)

                def step(new, old):
                    if following(new, B):
                        self.norm_power(pool, N, new.b + 1)
                pipeline(pool, B, step)

            @block.scalar
            def _(act):
                start_f.wait(act, 0)
                start_hi.on(act.activation(state[1].high[:, :, :], c_f[:, :, :], ACT.Copy))
                params.wait(act, 0)

                def step(new, old):
                    def split_new(j):
                        c_new.wait(act, old.b, j)
                        c_hi.on(act.activation(state[old.par].high[:, j, :], c_f[:, j, :], ACT.Copy))
                    if new:
                        for c in range(C):
                            xT_ps.wait(act, new.b, c)
                            xT_hi.on(act.activation(nT[new.par].high[:, c, :], turning.banks[c % 2][:, :], ACT.Copy))
                    if old:
                        for j in range(C):
                            for i, g in enumerate(GATES):
                                gate_ps.wait(act, old.b, 3 * j + i)
                                if i == 0:
                                    c_new.wait(act, old.b if j >= 2 else old.b - 1, (j - 2) % C)
                                gate_sb.on(act.activation(gate[:, j % 2, i, :], gating.banks[(3 * j + i) % 6][:, :],
                                                          ACT.Tanh if g == "c" else ACT.Sigmoid, bias=bias[:, i, j:j + 1]))
                                if j and i == 0:
                                    split_new(j - 1)
                        split_new(C - 1)
                pipeline(act, B, step)

            @block.vector
            def _(dve):
                zero.on(dve.memset(c_f[:, :, :], 0.0))
                zero.wait(dve, 0)
                params.wait(dve, 0)
                for c in range(C):
                    start_f.on(dve.tensor_scalar(c_f[:, c, :], c_f[:, c, :], c_in[:, c:c + 1], None, ALU.add))
                start_hi.wait(dve, 0)
                start.on(dve.tensor_tensor(state[1].low[:, :, :], c_f[:, :, :], state[1][:, :, :].high_f32(), ALU.subtract))

                def norm(b):
                    self.norm_stats(dve, N, b, x)
                    self.norm_apply(dve, N, b, x, N.scale, N.rstd)
                norm(0)

                def step(new, old):
                    if new:
                        for c in range(C):
                            xT_hi.wait(dve, new.b, c)
                            xT_lo.on(dve.tensor_tensor(nT[new.par].low[:, c, :], turning.banks[c % 2][:, :],
                                                       nT[new.par][:, c, :].high_f32(), ALU.subtract))

                    def update(j):
                        slot = gate[:, j % 2, :, :]
                        gate_sb.wait(dve, old.b, 3 * j + 1)
                        ig.on(dve.tensor_tensor(slot[:, 0, :], slot[:, 0, :], slot[:, 1, :], ALU.mult))
                        gate_sb.wait(dve, old.b, 3 * j + 2)
                        fc.on(dve.tensor_tensor(slot[:, 2, :], slot[:, 2, :], c_f[:, j, :], ALU.mult))
                        ig.wait(dve, old.b, j)
                        fc.wait(dve, old.b, j)
                        c_new.on(dve.tensor_tensor(c_f[:, j, :], slot[:, 0, :], slot[:, 2, :], ALU.add))

                    def split_new(j):
                        c_hi.wait(dve, old.b, j)
                        c_lo.on(dve.tensor_tensor(state[old.par].low[:, j, :], c_f[:, j, :], state[old.par][:, j, :].high_f32(), ALU.subtract))
                    if old:
                        update(0)
                        update(1)
                        split_new(0)
                    if following(new, B):
                        norm(new.b + 1)
                    if old:
                        for j in range(2, C):
                            update(j)
                            split_new(j - 1)
                        split_new(C - 1)
                pipeline(dve, B, step)

            @block.tensor
            def _(pe):
                start.wait(pe, 0)

                def step(new, old):
                    def part(j, weights, source, first):
                        for i, g in enumerate(GATES):
                            n = 3 * j + i
                            bank = gating.take(pe, old.b, n) if first else gating.banks[n % 6]
                            for c in range(C):
                                mm = product(pe, bank[:, :], weights[g][:, c, j * P:(j + 1) * P], source[:, c, :],
                                             first and c == 0, not first and c == C - 1)
                            if not first:
                                gate_ps.on(mm)
                    if old:
                        xT_lo.wait(pe, old.b)
                        part(0, w, nT[old.par], True)
                    if new:
                        N.normed.wait(pe, new.b)
                        for c in range(C):
                            xT_ps.on(self.turn(pe, turning.take(pe, new.b, c), x, c))
                    if old:
                        c_lo.wait(pe, old.b - 1)
                        part(0, u, state[1 - old.par], False)
                        for j in range(1, C):
                            part(j, w, nT[old.par], True)
                            part(j, u, state[1 - old.par], False)
                pipeline(pe, B, step)

    def phase_d(self, c_last):
        nc, io, B, C, T, D, S = self.nc, self.io, self.B, self.C, self.T, self.D, self.S
        X = 3
        with Scope(self.nc) as ctx:
            wo, uo = (self.split(ctx, f"d_{n}", [P, C, D]) for n in ("wo", "uo"))
            self.load_weights("dw", [("turn", io[f"L0_ffn_{n}"], D, t) for n, t in (("uo", uo), ("wo", wo))])
            sb = lambda n, s, d=F32: self.sb(ctx, f"d_{n}", s, d)
            ev = lambda n, per=1, unit=1: Event(ctx, nc, f"d_{n}", per, unit)
            x = [sb(f"x{i}", [P, T, D]) for i in range(X)]
            n = sb("n", [P, T, D])
            nT = [self.split(ctx, f"d_nT{i}", [P, C, S]) for i in range(X)]
            base = sb("base", [P, T, D])
            bo = sb("bo", [P, D])
            y = sb("y", [P, 2, D])
            N = self.norm_events(ctx, "d_ln")
            stored = ev("stored", 1, 16)
            bo_in, base_ps, base_sb = ev("bo_in", 1, 16), ev("base_ps", T), ev("base_sb", T)
            xT_ps, xT_hi, xT_lo = ev("xT_ps", C), ev("xT_hi", C), ev("xT_lo", C)
            y_ps, y_sb, y_tanh, out_sb = ev("y_ps", T), ev("y_sb", T), ev("y_tanh", T), ev("out_sb", T)
            turning = Ring(self.banks(ctx, "d_t", 4), [(xT_lo, c) for c in range(C)], self.B)
            output = Ring(self.banks(ctx, "d_y", 4), [(y_sb, t) for t in range(T)], self.B)
            block = ctx.enter_context(nc.Block())

            @block.sync
            def _(sp):
                bo_in.on(sp.dma_start(bo[:, :], io["L0_ffn_bo"].rearrange("(a n) -> a n", a=1).to_broadcast([P, D])))
                N.loaded.on(sp.dma_start(x[0][:, :, :], self.token_rows(self.x2, 0)))

                def step(new, old):
                    if following(new, B):
                        stored.wait(sp, new.b - 2)
                        N.loaded.wait(sp, new.b)
                        N.loaded.on(sp.dma_start(x[(new.par + 1) % X][:, :, :], self.token_rows(self.x2, new.b + 1)))
                    if old:
                        out_sb.wait(sp, old.b)
                        stored.on(sp.dma_start(self.token_rows(self.out, old.b), x[old.par][:, :, :]))
                pipeline(sp, B, step, X)
                stored.wait(sp, B - 1)

            @block.gpsimd
            def _(pool):
                self.norm_power(pool, N, 0)

                def step(new, old):
                    if old:
                        for t in range(T):
                            y_tanh.wait(pool, old.b, t)
                            out_sb.on(pool.tensor_tensor(x[old.par][:, t, :], x[old.par][:, t, :], y[:, t % 2, :], ALU.add))
                    if following(new, B):
                        self.norm_power(pool, N, new.b + 1)
                pipeline(pool, B, step, X)

            @block.scalar
            def _(act):
                def step(new, old):
                    for c in range(C):
                        if new:
                            xT_ps.wait(act, new.b, c)
                            xT_hi.on(act.activation(nT[new.par].high[:, c, :], turning.banks[c][:, :], ACT.Copy))
                    for t in range(T):
                        if old:
                            y_sb.wait(act, old.b, t)
                            y_tanh.on(act.activation(y[:, t % 2, :], y[:, t % 2, :], ACT.Tanh))
                pipeline(act, B, step, X)

            @block.vector
            def _(dve):
                bo_in.wait(dve, 0)
                for t in range(T):
                    base_ps.wait(dve, 0, t)
                    base_sb.on(dve.tensor_tensor(base[:, t, :], output.banks[t][:, :], bo[:, :], ALU.add))
                base_sb.wait(dve, 0)

                def norm(b, tile):
                    self.norm_stats(dve, N, b, tile)
                    xT_ps.wait(dve, b - 1)
                    self.norm_apply(dve, N, b, tile, N.scale, N.rstd, n)
                norm(0, x[0])

                def step(new, old):
                    if new:
                        for c in range(C):
                            xT_hi.wait(dve, new.b, c)
                            xT_lo.on(dve.tensor_tensor(nT[new.par].low[:, c, :], turning.banks[c][:, :],
                                                       nT[new.par][:, c, :].high_f32(), ALU.subtract))
                    if old:
                        for t in range(T):
                            y_ps.wait(dve, old.b, t)
                            out_sb.wait(dve, old.b if t >= 2 else old.b - 1, (t - 2) % T)
                            y_sb.on(dve.tensor_tensor(y[:, t % 2, :], output.banks[t][:, :], base[:, t, :], ALU.add))
                    if following(new, B):
                        norm(new.b + 1, x[(new.par + 1) % X])
                pipeline(dve, B, step, X)

            @block.tensor
            def _(pe):
                for t in range(T):
                    for c in range(C):
                        mm = product(pe, output.banks[t][:, :], c_last[:, c, t * P:(t + 1) * P], uo[:, c, :], c == 0, c == C - 1)
                    base_ps.on(mm)

                def step(new, old):
                    if new:
                        N.normed.wait(pe, new.b)
                        for c in range(C):
                            xT_ps.on(self.turn(pe, turning.take(pe, new.b, c), n, c))
                    if old:
                        for t in range(T):
                            if isinstance(old.b, int) and old.b == 0:
                                base_sb.wait(pe, 0, t)
                            bank = output.take(pe, old.b, t)
                            for c in range(C):
                                if t == 0:
                                    xT_lo.wait(pe, old.b, c)
                                mm = product(pe, bank[:, :], nT[old.par][:, c, t * P:(t + 1) * P], wo[:, c, :], c == 0, c == C - 1)
                            y_ps.on(mm)
                pipeline(pe, B, step, X)

    def run(self):
        with Scope(self.nc) as ctx:
            self.constants(ctx)
            self.phase_a()
            self.phase_b()
            self.phase_cd(ctx)

    def phase_cd(self, ctx):
        state = [self.split(ctx, f"state{i}", [P, self.C, self.S]) for i in range(2)]
        self.phase_c(state)
        self.phase_d(state[(self.B - 1) % 2])


def tables(T, S, H):
    f32 = np.float32
    timescale = f32(10000.0) ** (f32(2.0 / H) * np.arange(H // 2, dtype=f32))
    angle = lambda start, n: (np.arange(start, start + n, dtype=f32)[:, None] / timescale).astype(f32)
    aq, ak, scale = angle(S, T).T, angle(0, S), f32(H ** -0.5)
    two = np.concatenate
    return {"cos_q": two([np.cos(aq), np.cos(aq)]) * scale, "sin_q": two([np.sin(aq), -np.sin(aq)]) * scale,
            "cos_k": two([np.cos(ak), np.cos(ak)], 1), "sin_k": two([-np.sin(ak), np.sin(ak)], 1)}


_INS = ["x", "ctx_1024", "mask_BxS2_bk0", "L0_attn_Wq", "L0_attn_Wk", "L0_attn_Wv", "L0_attn_Wp", "L0_attn_bp",
        "L0_attn_conv_w", "L0_attn_conv_b", "L0_xattn_rms_scale", "L0_xattn_q_w", "L0_xattn_kv_w", "L0_xattn_out_w",
        "L0_ffn_wf", "L0_ffn_uf", "L0_ffn_bf", "L0_ffn_wi", "L0_ffn_ui", "L0_ffn_bi", "L0_ffn_wc", "L0_ffn_uc",
        "L0_ffn_bc", "L0_ffn_wo", "L0_ffn_uo", "L0_ffn_bo", "L0_ffn_in_c"]


def kernel(**inputs):
    import concourse.bacc as bacc
    from concourse.bass_utils import run_bass_kernel_spmd

    nc = bacc.Bacc("TRN2", target_bir_lowering=False, num_devices=1)
    arrays = {f"in_{n}": np.ascontiguousarray(inputs[n]) for n in _INS}
    B, S, D = inputs["x"].shape
    arrays.update({f"in_{n}": np.ascontiguousarray(t, np.float32)
                   for n, t in tables(S, inputs["ctx_1024"].shape[1], inputs["L0_xattn_q_w"].shape[2]).items()})
    io = {n[3:]: nc.dram_tensor(n, a.shape, mybir.dt.from_np(a.dtype), kind="ExternalInput").ap() for n, a in arrays.items()}
    out = nc.dram_tensor("out", (B, S, D), F32, kind="ExternalOutput").ap()
    x1, x2 = (nc.dram_tensor(n, (B, S, D), F32, kind="Internal").ap() for n in ("x1", "x2"))
    Kernel(nc, io, out, x1, x2).run()
    return run_bass_kernel_spmd(nc, [arrays], core_ids=[0]).results[0]["out"]
```

```python
from contextlib import ExitStack

import numpy as np
import concourse.bass as bass
from concourse import mybir

F32 = mybir.dt.float32
F32R = mybir.dt.float32r
U8 = mybir.dt.uint8
ALU = mybir.AluOpType
ACT = mybir.ActivationFunctionType
P = 128


class Scope(ExitStack):

    def __init__(self, nc):
        super().__init__()
        self.nc, self.semaphores = nc, []

    def __exit__(self, *error):
        super().__exit__(*error)
        if self.semaphores and error[0] is None:
            self.nc.clear_and_free_semaphores(self.semaphores)
            self.nc.all_engine_barrier()


class Event:

    def __init__(self, ctx, nc, name, per=1, unit=1):
        self.sem, self.per, self.unit = nc.alloc_semaphore(name), per, unit
        ctx.semaphores.append(self.sem)

    def on(self, instruction):
        instruction.then_inc(self.sem, self.unit)

    def wait(self, engine, b, k=None):
        k = self.per - 1 if k is None else k
        if isinstance(b, int) and b < 0:
            return
        engine.wait_ge(self.sem, (b * self.per + k + 1) * self.unit)


class Ring:

    def __init__(self, banks, frees, batches):
        self.banks, self.frees, self.batches = banks, [f if len(f) == 3 else (*f, 0) for f in frees], batches
        assert len(frees) % len(banks) == 0

    def take(self, engine, s, n):
        for back in range(len(self.banks), 2 * len(self.frees), len(self.banks)):
            steps, prev = divmod(n - back, len(self.frees))
            event, k, lag = self.frees[prev]
            b = s + (steps - lag)
            if not isinstance(b, int) or 0 <= b < self.batches:
                event.wait(engine, b, k)
                break
        return self.banks[n % len(self.banks)]


class Item:

    def __init__(self, b, par):
        self.b, self.par = b, par


def pipeline(engine, B, step, unroll=2, ahead=1):
    at = lambda base, i: Item(base + i, i % unroll)
    turns = (B - 2 - ahead) // unroll
    step(Item(0, 0), None)
    step(at(0, 1), at(0, 0))
    with engine.Fori(0, turns) as j:
        for i in range(unroll):
            step(at(unroll * j, i + 2), at(unroll * j, i + 1))
    for b in range(unroll * turns + 2, B):
        step(at(0, b), at(0, b - 1))
    step(None, at(0, B - 1))


def following(new, B, ahead=1):
    return new is not None and not (isinstance(new.b, int) and new.b + ahead >= B)


class Split:

    def __init__(self, high, low):
        self.high, self.low = high, low

    def __getitem__(self, at):
        return Split(self.high[at], self.low[at])

    def high_f32(self):
        return self.high.bitcast(F32)


def product(pe, out, stationary, moving, first, last):
    pe.matmul(out, stationary.high, moving.high, start=first, stop=False)
    pe.matmul(out, stationary.high, moving.low, start=False, stop=False)
    return pe.matmul(out, stationary.low, moving.high, start=False, stop=last)


class Kernel:
    def __init__(self, nc, io, out, scratch1, scratch2):
        self.nc, self.io, self.out, self.x1, self.x2 = nc, io, out, scratch1, scratch2
        self.B, self.S, self.D = io["x"].shape
        self.C = self.D // P
        self.T = self.S // P

    def sb(self, ctx, name, shape, dtype=F32):
        return ctx.enter_context(self.nc.sbuf_tensor(name, shape, dtype))

    def split(self, ctx, name, shape):
        return Split(self.sb(ctx, name + "_hi", shape, F32R), self.sb(ctx, name + "_lo", shape, F32R))

    def banks(self, ctx, name, n):
        return [ctx.enter_context(self.nc.psum_tensor(f"{name}{i}", [P, 512], F32)) for i in range(n)]

    def load_weights(self, tag, jobs, stage, first, rms_scale=None):
        nc, C, D = self.nc, self.C, self.D
        with Scope(self.nc) as ctx:
            sb = lambda n, s, d=F32: self.sb(ctx, f"{tag}_{n}", s, d)
            scale = sb("scale", [P, C])
            banks = self.banks(ctx, f"{tag}_pw", 4)
            ev = lambda n, per=1, unit=1: Event(ctx, nc, f"{tag}_{n}", per, unit)
            loaded = [ev(f"loaded{i}", 1 if j[0] == "turn" else len(j[1]), 16) for i, j in enumerate(jobs)]
            scaled, turned, high, low = ev("scaled", C), ev("turned", C), ev("high", C), ev("low", C)
            scale_in, scale_one = ev("scale_in", 1, 16), ev("scale_one")
            block = ctx.enter_context(nc.Block())
            before = [sum(j[0] == jobs[i][0] for j in jobs[:i]) for i in range(len(jobs))]

            @block.gpsimd
            def _(pool):
                first.get("pool", lambda e: None)(pool)

            @block.sync
            def _(sp):
                first["sp"](sp)
                if rms_scale is not None:
                    with nc.allow_non_contiguous_dma(reason="512 words once"):
                        scale_in.on(sp.dma_start(scale[:, :], rms_scale.rearrange("(c p) -> p c", p=P)))
                for i, (kind, parts, n, w) in enumerate(jobs):
                    low.wait(sp, i - len(stage))
                    if kind == "turn":
                        parts = [(parts.rearrange("(c p) n -> p c n", p=P), 0)]
                    for view, at in parts:
                        loaded[i].on(sp.dma_start(stage[i % len(stage)][:, :, at:at + view.shape[2]], view))

            @block.tensor
            def _(pe):
                for i, (kind, parts, n, w) in enumerate(jobs):
                    if kind != "turn":
                        continue
                    loaded[i].wait(pe, 0)
                    for c in range(C):
                        if i >= 1:
                            low.wait(pe, i - 1, c)
                        for o in range(C):
                            mm = pe.transpose(banks[c][:, o * P:(o + 1) * P],
                                              stage[i % len(stage)][:, o, c * P:(c + 1) * P], self.ident[:, :])
                        turned.on(mm)

            def source(i, c):
                kind, parts, n, w = jobs[i]
                return banks[c][:, 0:n] if kind == "turn" else stage[i % len(stage)][:, c, 0:n]

            def ready(engine, i, c):
                if jobs[i][0] == "turn":
                    turned.wait(engine, before[i], c)
                elif jobs[i][0] == "scale":
                    scaled.wait(engine, before[i], c)
                else:
                    loaded[i].wait(engine, 0)

            @block.scalar
            def _(act):
                first.get("act", lambda e: None)(act)
                for i, (kind, parts, n, w) in enumerate(jobs):
                    for c in range(C):
                        ready(act, i, c)
                        high.on(act.activation(w.high[:, c, 0:n], source(i, c), ACT.Copy))

            @block.vector
            def _(dve):
                first["dve"](dve)
                if rms_scale is not None:
                    scale_in.wait(dve, 0)
                    scale_one.on(dve.tensor_scalar(scale[:, :], scale[:, :], 1.0, None, ALU.add))
                    scale_one.wait(dve, 0)
                for i, (kind, parts, n, w) in enumerate(jobs):
                    if kind == "scale":
                        loaded[i].wait(dve, 0)
                        for c in range(C):
                            scaled.on(dve.tensor_scalar(stage[i % len(stage)][:, c, 0:n], stage[i % len(stage)][:, c, 0:n],
                                                        scale[:, c:c + 1], None, ALU.mult))
                    for c in range(C):
                        ready(dve, i, c)
                        high.wait(dve, i, c)
                        low.on(dve.tensor_tensor(w.low[:, c, 0:n], source(i, c),
                                                 w[:, c, 0:n].high_f32(), ALU.subtract))

    def norm_events(self, ctx, tag):
        e = lambda n, per=1, unit=1: Event(ctx, self.nc, f"{tag}_{n}", per, unit)

        class N:
            loaded = e("loaded", 1, 16)
            stats, moments, variance, rstd, normed = e("stats", self.T), e("moments", self.T), e("var"), e("rstd"), e("normed", self.T)
            carrier = self.sb(ctx, f"{tag}_carrier", [P, 1])
            st = self.sb(ctx, f"{tag}_st", [P, self.T, 6])
            mv = self.sb(ctx, f"{tag}_mv", [P, self.T, 2])
            var_eps = self.sb(ctx, f"{tag}_ve", [P, self.T])
            scale = self.sb(ctx, f"{tag}_sc", [P, self.T])
        return N

    def norm_stats(self, dve, N, b, x):
        for t in range(self.T):
            self.norm_tile(dve, N, b, x, t)
        self.norm_variance(dve, N, b)

    def norm_tile(self, dve, N, b, x, t):
        if t == 0:
            N.loaded.wait(dve, b)
        N.stats.on(dve.bn_stats(N.st[:, t, :], x[:, t, :]))

    def norm_variance(self, dve, N, b):
        N.stats.wait(dve, b)
        dve.memset(N.carrier[:, :], 0.0)
        for t in range(self.T):
            N.moments.on(dve.bn_aggr(N.mv[:, t, :], N.st[:, t, :]))
        N.moments.wait(dve, b)
        N.variance.on(dve.tensor_scalar(N.var_eps[:, :], N.mv[:, :, 1], 1e-5, None, ALU.add))

    def norm_power(self, pool, N, b):
        N.variance.wait(pool, b)
        N.normed.wait(pool, b - 1)
        N.rstd.on(pool.tensor_tensor(N.scale[:, :], N.var_eps[:, :], self.minus_half[:, 0:self.T], ALU.pow))

    def norm_apply(self, dve, N, b, x, scale, scale_event, out=None, tiles=None):
        scale_event.wait(dve, b)
        for t in tiles or range(self.T):
            N.normed.on(dve.tensor_scalar((out or x)[:, t, :], x[:, t, :], N.mv[:, t, 0:1], scale[:, t:t + 1],
                                          ALU.subtract, ALU.mult))

    def turn(self, pe, bank, src, c):
        for t in range(self.T):
            mm = pe.transpose(bank[:, t * P:(t + 1) * P], src[:, t, c * P:(c + 1) * P], self.ident[:, :])
        return mm

    def token_rows(self, dram, b):
        return dram[b, :, :].rearrange("(t p) d -> p t d", p=P)

    def constants(self, ctx):
        nc = self.nc
        self.ident = self.sb(ctx, "ident", [P, P])
        self.minus_half = self.sb(ctx, "minus_half", [P, 4])
        with Scope(self.nc) as c:
            zero = Event(c, nc, "ident_zero")
            block = c.enter_context(nc.Block())

            @block.gpsimd
            def _(pool):
                pool.memset(self.minus_half[:, :], -0.5)
                zero.on(pool.memset(self.ident[:, :], 0.0))
                zero.wait(pool, 0)
                pool.affine_select(out=self.ident[:, :], in_=self.ident[:, :], compare_op=ALU.not_equal,
                                   fill=1.0, base=0, pattern=[[-1, P]], channel_multiplier=1)

    def phase_a(self):
        nc, io, B, C, T, D, S = self.nc, self.io, self.B, self.C, self.T, self.D, self.S
        HEADS = 16
        HD = D // HEADS
        HC = P // HD
        KVW = P + HEADS
        with Scope(self.nc) as ctx:
            w = {n: self.split(ctx, f"a_{n}", [P, C, D]) for n in ("Wq", "Wk", "Wv", "Wp")}
            sb = lambda n, s, d=F32: self.sb(ctx, f"a_{n}", s, d)
            ev = lambda n, per=1, unit=1: Event(ctx, nc, f"a_{n}", per, unit)
            x = sb("x", [P, T, D])
            xT = self.split(ctx, "a_xT", [P, C, S])
            k = sb("k", [P, T, D])
            v1 = sb("v1", [P, T, C, P + 2])
            q = [self.split(ctx, f"a_q{i}", [P, C, S]) for i in range(2)]
            local = [sb(f"local{i}", [P, C, S]) for i in range(2)]
            kv = [self.split(ctx, f"a_kv{i}", [P, C * KVW + P - HEADS]) for i in range(2)]
            z = self.split(ctx, "a_z", [P, C, S])
            res = sb("res", [P, T, D])
            elu = sb("elu", [P, 2, D])
            kv_f = elu[:, :, :].rearrange("p a d -> p (a d)")[:, 0:C * KVW].rearrange("p (c e) -> p c e", c=C)
            rden = sb("rden", [HEADS, S])
            rden_s = self.split(ctx, "a_rdens", [HEADS, S])
            att = [sb(f"att{i}", [P, S]) for i in range(2)]
            head_rows = sb("head_rows", [HEADS, C, P], F32R)
            kv_mask = sb("kv_mask", [P, 2, P])
            head_mask = sb("head_mask", [P, C, HEADS])
            bp = sb("bp", [P, D])
            conv_w = sb("conv_w", [P, C, 3])
            conv_b = sb("conv_b", [P, C])
            N = self.norm_events(ctx, "a_ln")
            params = ev("params", 3, 16)
            built = ev("built", 11)
            xT_ps, xT_hi, xT_lo = ev("xT_ps", C), ev("xT_hi", C), ev("xT_lo", C)
            tap1, tap0, tap2 = ev("tap1", C), ev("tap0", C), ev("tap2", C)
            kq_ps, v_ps = ev("kq_ps", T + C), ev("v_ps", T)
            elu_neg, elu_exp, elu_out = ev("elu_neg", T + C), ev("elu_exp", T + C), ev("elu_out", T + C)
            q_hi, q_lo, v_sb = ev("q_hi", C), ev("q_lo", C), ev("v_sb", T)
            kv_ps, kv_part, kv_hi, kv_lo = ev("kv_ps", 2), ev("kv_part", 6), ev("kv_hi"), ev("kv_lo")
            den_ps, den_max, rden_f, rden_hi, rden_lo = ev("den_ps"), ev("den_max"), ev("rden_f"), ev("rden_hi"), ev("rden_lo")
            spread_ps, spread_sb, att_ps, att_sb = ev("spread_ps", C), ev("spread_sb", C), ev("att_ps", C), ev("att_sb", C)
            z_f, z_hi, z_lo = ev("z_f", C), ev("z_hi", C), ev("z_lo", C)
            out_ps, res_bp, x1_sb = ev("out_ps", T), ev("res_bp", T), ev("x1_sb", T)
            res_in, stored = ev("res_in", 1, 16), ev("stored", 1, 16)
            def load(sp, b):
                xT_ps.wait(sp, b - 1)
                N.loaded.on(sp.dma_start(x[:, :, :], self.token_rows(io["x"], b)))

            def first_loads(sp):
                load(sp, 0)
                with nc.allow_non_contiguous_dma(reason="small parameters, once"):
                    params.on(sp.dma_start(conv_w[:, :, :], io["L0_attn_conv_w"].rearrange("(c p) k -> p c k", p=P)))
                    params.on(sp.dma_start(conv_b[:, :], io["L0_attn_conv_b"].rearrange("(c p) -> p c", p=P)))
                    params.on(sp.dma_start(bp[:, :], io["L0_attn_bp"].rearrange("(a n) -> a n", a=1).to_broadcast([P, D])))

            def first_masks(pool):
                keep = lambda ap, base, pattern, mult: pool.affine_select(
                    out=ap, in_=ap, compare_op=ALU.is_ge, fill=0.0, base=base, pattern=pattern, channel_multiplier=mult)
                built.on(pool.memset(kv_mask[:, :, :], 1.0))
                built.on(pool.memset(head_mask[:, :, :], 1.0))
                built.on(pool.memset(head_rows[:, :, :].bitcast(F32), 1.0))
                built.on(pool.memset(v1[:, :, :, :], 1.0))
                for i in range(2):
                    pool.memset(kv[i].high[:, :].bitcast(F32), 0.0)
                    last = pool.memset(kv[i].low[:, :].bitcast(F32), 0.0)
                built.on(last)
                built.wait(pool, 0, 4)
                km = kv_mask[:, :, :].rearrange("p a (h e) -> p a h e", h=HC)
                built.on(keep(km, 0, [[0, 2], [-HD, HC], [0, HD]], 1))
                built.on(keep(head_mask[:, :, :], 0, [[HC * HD, C], [-HD, HEADS]], 1))
                hr = head_rows[:, :, :].rearrange("h c (a e) -> h c a e", a=HC)
                built.on(keep(hr, 0, [[-HC, C], [-1, HC], [0, HD]], 1))
                built.wait(pool, 0, 7)
                built.on(keep(km, HD - 1, [[0, 2], [HD, HC], [0, HD]], -1))
                built.on(keep(head_mask[:, :, :], HD - 1, [[-HC * HD, C], [HD, HEADS]], -1))
                built.on(keep(hr, 0, [[HC, C], [1, HC], [0, HD]], -1))
                self.norm_power(pool, N, 0)

            def first_norm(dve):
                self.norm_stats(dve, N, 0, x)
                self.norm_apply(dve, N, 0, x, N.scale, N.rstd)
            self.load_weights("aw", [("turn", io[f"L0_attn_{n}"], D, w[n]) for n in w], (k, res, *local),
                              {"sp": first_loads, "pool": first_masks, "dve": first_norm})
            first = Ring(self.banks(ctx, "a_p", 3),
                         [(den_max, 0, 1)] + [(elu_out, t) for t in range(T)]
                         + [(v_sb, t) for t in range(T)] + [(elu_out, T + c) for c in range(C)]
                         + [(kv_part, 2), (kv_part, 5)], B)
            K, V, Q, KV = 1, 1 + T, 1 + 2 * T, 1 + 2 * T + C
            kq_bank = lambda u: first.banks[(K + u if u < T else Q + u - T) % 3]
            second = Ring(self.banks(ctx, "a_r", 4),
                          [(tap2, c) for c in range(C)] + [e for c in range(C) for e in ((spread_sb, c, 1), (att_sb, c, 1))]
                          + [(x1_sb, t, 1) for t in range(T)], B)
            SPREAD, OUT = C, 3 * C
            block = ctx.enter_context(nc.Block())

            @block.sync
            def _(sp):
                def step(new, old):
                    if old:
                        stored.wait(sp, old.b - 1)
                        res_in.on(sp.dma_start(res[:, :, :], self.token_rows(io["x"], old.b)))
                    if following(new, B):
                        load(sp, new.b + 1)
                    if old:
                        x1_sb.wait(sp, old.b)
                        stored.on(sp.dma_start(self.token_rows(self.x1, old.b), res[:, :, :]))
                pipeline(sp, B, step)
                stored.wait(sp, B - 1)

            @block.gpsimd
            def _(pool):
                params.wait(pool, 0)

                def step(new, old):
                    if old:
                        res_in.wait(pool, old.b)
                        for t in range(T):
                            res_bp.on(pool.tensor_tensor(res[:, t, :], res[:, t, :], bp[:, :], ALU.add))
                        for c in range(C):
                            att_sb.wait(pool, old.b, c)
                            z_f.on(pool.tensor_tensor(att[c % 2][:, :], att[c % 2][:, :], local[old.par][:, c, :], ALU.add))
                    if following(new, B):
                        self.norm_power(pool, N, new.b + 1)
                    if new:
                        for c in range(C):
                            q_hi.wait(pool, new.b, c)
                            q_lo.on(pool.tensor_tensor(q[new.par].low[:, c, :], elu[:, c % 2, :],
                                                       q[new.par][:, c, :].high_f32(), ALU.subtract))
                pipeline(pool, B, step)

            @block.scalar
            def _(act):
                params.wait(act, 0)
                built.wait(act, 0)

                def step(new, old):
                    def elu_front(u):
                        kq_ps.wait(act, new.b, u)
                        if u < 2:
                            kv_lo.wait(act, new.b - 1)
                        elif u - 2 < T:
                            elu_out.wait(act, new.b, u - 2)
                        else:
                            q_lo.wait(act, new.b, u - 2 - T)
                        bank = kq_bank(u)
                        elu_neg.on(act.activation(elu[:, u % 2, :], bank[:, :], ACT.Relu, scale=-1.0))
                        elu_neg.wait(act, new.b, u)
                        elu_exp.on(act.activation(elu[:, u % 2, :], elu[:, u % 2, :], ACT.Exp, scale=-1.0))

                    def q_high(c):
                        elu_out.wait(act, new.b, T + c)
                        q_hi.on(act.activation(q[new.par].high[:, c, :], elu[:, c % 2, :], ACT.Copy))

                    def spread_copy(c):
                        spread_ps.wait(act, old.b, c)
                        z_lo.wait(act, old.b if c >= 2 else old.b - 1, c - 2 if c >= 2 else C + c - 2)
                        spread_sb.on(act.activation(att[c % 2][:, :], second.banks[(SPREAD + 2 * c) % 4][:, :], ACT.Copy))

                    def z_high(c):
                        z_f.wait(act, old.b, c)
                        if c == 0:
                            out_ps.wait(act, old.b - 1)
                        z_hi.on(act.activation(z.high[:, c, :], att[c % 2][:, :], ACT.Copy))

                    if new:
                        for c in range(C):
                            xT_ps.wait(act, new.b, c)
                            if c == 0:
                                kq_ps.wait(act, new.b - 1)
                            bank = second.banks[c % 4]
                            xT_hi.on(act.activation(xT.high[:, c, :], bank[:, :], ACT.Copy))
                            tap1.on(act.activation(local[new.par][:, c, :], bank[:, :], ACT.Identity,
                                                   bias=conv_b[:, c:c + 1], scale=conv_w[:, c, 1:2]))
                        elu_front(0)
                        elu_front(1)
                    if old:
                        rden_f.wait(act, old.b)
                        spread_ps.wait(act, old.b - 1)
                        rden_hi.on(act.activation(rden_s.high[:, :], rden[:, :], ACT.Copy))
                    if new:
                        elu_front(2)
                        elu_front(3)
                    if old:
                        for c in range(C):
                            spread_copy(c)
                            if c >= 1:
                                z_high(c - 1)
                        z_high(C - 1)
                    if new:
                        for t in range(T):
                            v_ps.wait(act, new.b, t)
                            if t == 0:
                                kv_ps.wait(act, new.b - 1)
                            v_sb.on(act.activation(v1[:, t, :, 0:P],
                                                   first.banks[(V + t) % 3][:, :].rearrange("p (c e) -> p c e", c=C), ACT.Copy))
                        for c in range(C):
                            elu_front(T + c)
                            if c >= 1:
                                q_high(c - 1)
                        q_high(C - 1)
                        for g in range(2):
                            kv_part.wait(act, new.b, 3 * g + 2)
                        kv_hi.on(act.activation(kv[new.par].high[:, 0:C * KVW].rearrange("p (c e) -> p c e", c=C),
                                                kv_f, ACT.Copy))
                pipeline(act, B, step)

            @block.vector
            def _(dve):
                params.wait(dve, 0)
                built.wait(dve, 0)

                def step(new, old):
                    def elu_back(u):
                        elu_exp.wait(dve, new.b, u)
                        bank = kq_bank(u)
                        if u < T:
                            if u == 0:
                                kv_ps.wait(dve, new.b - 1)
                            dst = k[:, u, :]
                        else:
                            c = u - T
                            dst = elu[:, c % 2, :]
                        elu_out.on(dve.scalar_tensor_tensor(out=dst, in0=bank[:, :], scalar=0.0, in1=elu[:, u % 2, :],
                                                            op0=ALU.max, op1=ALU.add))

                    def taps(c):
                        bank, loc = second.banks[c % 4], local[new.par]
                        tap0.on(dve.scalar_tensor_tensor(out=loc[:, c, 1:S], in0=bank[:, 0:S - 1], scalar=conv_w[:, c, 0:1],
                                                         in1=loc[:, c, 1:S], op0=ALU.mult, op1=ALU.add))
                        tap0.wait(dve, new.b, c)
                        tap2.on(dve.scalar_tensor_tensor(out=loc[:, c, 0:S - 1], in0=bank[:, 1:S], scalar=conv_w[:, c, 2:3],
                                                         in1=loc[:, c, 0:S - 1], op0=ALU.mult, op1=ALU.add))

                    if new:
                        for c in range(C):
                            tap1.wait(dve, new.b, c)
                            xT_lo.on(dve.tensor_tensor(xT.low[:, c, :], second.banks[c % 4][:, :], xT[:, c, :].high_f32(), ALU.subtract))
                    if old:
                        den_ps.wait(dve, old.b)
                        den_max.on(dve.tensor_scalar(rden[:, :], first.banks[0][0:HEADS, :], 1e-6, None, ALU.max))
                    if new:
                        taps(0)
                        elu_back(0)
                    if old:
                        den_max.wait(dve, old.b)
                        rden_f.on(dve.reciprocal(rden[:, :], rden[:, :]))
                    if new:
                        taps(1)
                        elu_back(1)
                    if old:
                        rden_hi.wait(dve, old.b)
                        rden_lo.on(dve.tensor_tensor(rden_s.low[:, :], rden[:, :], rden_s[:, :].high_f32(), ALU.subtract))
                    if new:
                        taps(2)
                        taps(3)
                        elu_back(2)
                        elu_back(3)
                    if old:
                        def z_low(c):
                            z_hi.wait(dve, old.b, c)
                            z_lo.on(dve.tensor_tensor(z.low[:, c, :], att[c % 2][:, :], z[:, c, :].high_f32(), ALU.subtract))
                        for c in range(C):
                            spread_sb.wait(dve, old.b, c)
                            att_ps.wait(dve, old.b, c)
                            att_sb.on(dve.tensor_tensor(att[c % 2][:, :], second.banks[(SPREAD + 2 * c + 1) % 4][:, :], att[c % 2][:, :], ALU.mult))
                            if c >= 1:
                                z_low(c - 1)
                        z_low(C - 1)
                    if following(new, B):
                        self.norm_stats(dve, N, new.b + 1, x)
                        self.norm_apply(dve, N, new.b + 1, x, N.scale, N.rstd)
                    if new:
                        for c in range(C):
                            elu_back(T + c)
                    if new:
                        q_lo.wait(dve, new.b)
                        for g in range(2):
                            kv_ps.wait(dve, new.b, g)
                            bank = first.banks[(KV + g) % 3][:, 0:2 * (P + 2)].rearrange("p (c e) -> p c e", c=2)
                            kv_part.on(dve.tensor_tensor(kv_f[:, 2 * g:2 * g + 2, 0:P], bank[:, :, 0:P], kv_mask[:, :, :], ALU.mult))
                            for i in range(2):
                                kv_part.on(dve.tensor_scalar(kv_f[:, 2 * g + i, P:KVW], head_mask[:, 2 * g + i, :],
                                                             bank[:, i, P:P + 1], None, ALU.mult))
                        kv_hi.wait(dve, new.b)
                        kv_part.wait(dve, new.b)
                        both = lambda ap: ap[:, 0:C * KVW].rearrange("p (c e) -> p c e", c=C)
                        kv_lo.on(dve.tensor_tensor(both(kv[new.par].low), kv_f, both(kv[new.par].high).bitcast(F32), ALU.subtract))
                    if old:
                        for t in range(T):
                            res_bp.wait(dve, old.b, t)
                            out_ps.wait(dve, old.b, t)
                            x1_sb.on(dve.tensor_tensor(res[:, t, :], second.banks[(OUT + t) % 4][:, :], res[:, t, :], ALU.add))
                pipeline(dve, B, step)

            @block.tensor
            def _(pe):
                built.wait(pe, 0)

                def step(new, old):
                    s = new.b if new else old.b + 1
                    if new:
                        for c in range(C):
                            bank = second.take(pe, s, c)
                            if c == 0:
                                N.normed.wait(pe, new.b)
                            xT_ps.on(self.turn(pe, bank, x, c))
                    if old:
                        den_bank = first.take(pe, s, 0)
                        kv_lo.wait(pe, old.b)
                        for c in range(C):
                            q_lo.wait(pe, old.b, c)
                            mm = product(pe, den_bank[:, :], kv[old.par][:, c * KVW + P:c * KVW + 2 * P],
                                         q[old.par][:, c, :], c == 0, c == C - 1)
                        den_ps.on(mm)
                    if new:
                        for t in range(T):
                            bank = first.take(pe, s, K + t)
                            for c in range(C):
                                if t == 0:
                                    xT_lo.wait(pe, new.b, c)
                                mm = product(pe, bank[:, :], xT[:, c, t * P:(t + 1) * P], w["Wk"][:, c, :], c == 0, c == C - 1)
                            kq_ps.on(mm)
                    if old:
                        rden_lo.wait(pe, old.b)
                        for c in range(C):
                            bank = second.take(pe, s, SPREAD + 2 * c)
                            pe.matmul(bank[:, :], head_rows[:, c, :], rden_s.high[:, :], start=True, stop=False)
                            spread_ps.on(pe.matmul(bank[:, :], head_rows[:, c, :], rden_s.low[:, :], start=False, stop=True))
                            bank = second.take(pe, s, SPREAD + 2 * c + 1)
                            att_ps.on(product(pe, bank[:, :], kv[old.par][:, c * KVW:c * KVW + P], q[old.par][:, c, :], True, True))
                    if new:
                        for t in range(T):
                            bank = first.take(pe, s, V + t)
                            for c in range(C):
                                mm = product(pe, bank[:, :], xT[:, c, t * P:(t + 1) * P], w["Wv"][:, c, :], c == 0, c == C - 1)
                            v_ps.on(mm)
                    if new:
                        for o in range(C):
                            bank = first.take(pe, s, Q + o)
                            for c in range(C):
                                mm = product(pe, bank[:, :], w["Wq"][:, c, o * P:(o + 1) * P], xT[:, c, :], c == 0, c == C - 1)
                            kq_ps.on(mm)
                    if new:
                        v_sb.wait(pe, new.b)
                        elu_out.wait(pe, new.b, T - 1)
                        for g in range(2):
                            bank = first.take(pe, s, KV + g)
                            for i in range(2):
                                c = 2 * g + i
                                for t in range(T):
                                    mm = pe.matmul(bank[:, i * (P + 2):(i + 1) * (P + 2)], k[:, t, c * P:(c + 1) * P],
                                                   v1[:, t, c, :], start=(t == 0), stop=(t == T - 1))
                            kv_ps.on(mm)
                    if old:
                        for t in range(T):
                            bank = second.take(pe, s, OUT + t)
                            for c in range(C):
                                if t == 0:
                                    z_lo.wait(pe, old.b, c)
                                mm = product(pe, bank[:, :], z[:, c, t * P:(t + 1) * P], w["Wp"][:, c, :], c == 0, c == C - 1)
                            out_ps.on(mm)
                pipeline(pe, B, step)

    def phase_b(self):
        nc, io, B, C, T, D, S = self.nc, self.io, self.B, self.C, self.T, self.D, self.S
        H, _, HD = io["L0_xattn_q_w"].shape
        BIG = 2.0 ** 100
        with Scope(self.nc) as ctx:
            qw = self.split(ctx, "b_qw", [P, C, H * HD])
            kvw = self.split(ctx, "b_kvw", [P, C, 2 * HD])
            ow = self.split(ctx, "b_ow", [P, H, D])
            sb = lambda n, s, d=F32: self.sb(ctx, f"b_{n}", s, d)
            ev = lambda n, per=1, unit=1: Event(ctx, nc, f"b_{n}", per, unit)
            x = sb("x", [P, T, D])
            mem = sb("mem", [P, T, D])
            nT = self.split(ctx, "b_nT", [P, C, S])
            q = self.split(ctx, "b_q", [P, H, S])
            k = [self.split(ctx, f"b_k{i}", [P, S]) for i in range(2)]
            v = [self.split(ctx, f"b_v{i}", [P, T, HD]) for i in range(2)]
            p_f = sb("p_f", [P, T, S])
            p = self.split(ctx, "b_p", [P, T, S])
            psum = sb("psum", [P, S])
            enc_f = sb("enc_f", [P, H, S])
            enc = self.split(ctx, "b_enc", [P, H, S])
            res = sb("res", [P, T, D])
            cos_q, sin_q = sb("cos_q", [P, S]), sb("sin_q", [P, S])
            cos_k, sin_k = sb("cos_k", [P, T, HD]), sb("sin_k", [P, T, HD])
            rope_f = [sb(f"rope{i}", [P, S]) for i in range(2)]
            rope_swap = sb("rope_swap", [P, S])
            k_f = sb("k_f", [P, T, HD])
            mask_u8 = sb("mask_u8", [P, S], U8)
            mask_row = sb("mask_row", [P, S])
            unused = [sb(f"unused{i}", [P, S], mybir.dt.bfloat16) for i in range(4)]
            carrier = sb("carrier", [P, 4])
            unused_sq = [sb(f"unused_sq{i}", [P, D], mybir.dt.bfloat16) for i in range(2)]
            mask_any = sb("mask_any", [P, 1])
            p_scale, p_bias = sb("p_scale", [P, T]), sb("p_bias", [P, T])
            top = sb("top", [P, T, H])
            top_row = sb("top_row", [H, S], F32R)
            rsum = sb("rsum", [P, T, H])
            rsum_s = self.split(ctx, "b_rsums", [H, S])
            head_row = sb("head_row", [H, H, P], F32R)
            minus_row = sb("minus_row", [H, H, P], F32R)
            ones = sb("ones", [P, 1])
            sumsq, mem_ms, mem_scale = sb("sumsq", [P, T]), sb("mem_ms", [P, T]), sb("mem_scale", [P, T])
            one_in_d, rms_eps = sb("one_in_d", [P, T]), sb("rms_eps", [P, T])
            n_sq, n_rms, n_scale = sb("n_sq", [P, T]), sb("n_rms", [P, T]), sb("n_scale", [P, T])
            N = self.norm_events(ctx, "b_ln")
            params, built = ev("params", 4, 16), ev("built", 5)
            mem_in, sq, ms, mscale, mem_n = ev("mem_in", 1, 16), ev("sq", T), ev("ms", 2), ev("mscale"), ev("mem_n", T)
            nsteps, nscale = ev("nsteps", 4), ev("nscale")
            memT_ps, memT_hi, memT_lo = ev("memT_ps", C), ev("memT_hi", C), ev("memT_lo", C)
            kv_ps, v_hi, v_lo = ev("kv_ps", 2), ev("v_hi", 2), ev("v_lo", 2)
            k_cos, k_swap, k_rope = ev("k_cos", 2), ev("k_swap", 4), ev("k_rope", 2)
            kT_ps, k_hi, k_lo = ev("kT_ps"), ev("k_hi"), ev("k_lo")
            xT_ps, xT_hi, xT_lo = ev("xT_ps", C), ev("xT_hi", C), ev("xT_lo", C)
            q_ps, q_cos, q_swap, q_rope = ev("q_ps", H), ev("q_cos", H), ev("q_swap", 2 * H), ev("q_rope", H)
            q_hi, q_lo = ev("q_hi", H), ev("q_lo", H)
            mask_in, mask_f, mask_max, mask_ps, mask_sb = ev("mask_in", 1, 16), ev("mask_f"), ev("mask_max"), ev("mask_ps"), ev("mask_sb", 2)
            top_ps, top_sb, row_ps, row_sb = ev("top_ps", T * H), ev("top_sb", T * H), ev("row_ps"), ev("row_sb")
            st_ps, p_exp, p_hi, p_lo = ev("st_ps", H * T), ev("p_exp", H * T), ev("p_hi", H * T), ev("p_lo", H * T)
            add = ev("add", 3 * H)
            enc_ps, enc_sb, sum_ps = ev("enc_ps", H * T), ev("enc_sb", H), ev("sum_ps", H)
            rsum_f, rrow_ps, rsum_hi, rsum_lo = ev("rsum_f"), ev("rrow_ps"), ev("rsum_hi"), ev("rsum_lo")
            spread_ps, enc_n, enc_hi, enc_lo = ev("spread_ps", H), ev("enc_n", H), ev("enc_hi", H), ev("enc_lo", H)
            out_ps, x2_sb = ev("out_ps", T), ev("x2_sb", T)
            res_in, stored = ev("res_in", 1, 16), ev("stored", 1, 16)
            def load_mem(sp, b):
                memT_ps.wait(sp, b - 1)
                mem_in.on(sp.dma_start(mem[:, :, :], self.token_rows(io["ctx_1024"], b)))

            def load_x(sp, b):
                xT_ps.wait(sp, b - 1)
                N.loaded.on(sp.dma_start(x[:, :, :], self.token_rows(self.x1, b)))
            def mem_power(pool, b):
                sq.wait(pool, b)
                ms.on(pool.tensor_tensor(mem_ms[:, :], sumsq[:, :], one_in_d[:, :], ALU.mult))
                ms.wait(pool, b, 0)
                ms.on(pool.tensor_tensor(mem_ms[:, :], mem_ms[:, :], rms_eps[:, :], ALU.add))
                ms.wait(pool, b, 1)
                mem_n.wait(pool, b - 1)
                mscale.on(pool.tensor_tensor(mem_scale[:, :], mem_ms[:, :], self.minus_half[:, 0:T], ALU.pow))

            def x_power(pool, b):
                self.norm_power(pool, N, b)
                own = lambda i, ins: (nsteps.on(ins), nsteps.wait(pool, b, i))
                N.rstd.wait(pool, b)
                own(0, pool.tensor_tensor(n_sq[:, :], N.scale[:, :], N.scale[:, :], ALU.mult))
                own(1, pool.tensor_tensor(n_rms[:, :], n_sq[:, :], N.mv[:, :, 1], ALU.mult))
                own(2, pool.tensor_tensor(n_sq[:, :], n_rms[:, :], rms_eps[:, :], ALU.add))
                own(3, pool.tensor_tensor(n_rms[:, :], n_sq[:, :], self.minus_half[:, 0:T], ALU.pow))
                nscale.on(pool.tensor_tensor(n_scale[:, :], n_rms[:, :], N.scale[:, :], ALU.mult))

            def squares(act, b):
                mem_in.wait(act, b)
                ms.wait(act, b - 1)
                for t in range(T):
                    sq.wait(act, b if t >= 2 else b - 1, (t - 2) % T)
                    sq.on(act.activation(unused_sq[t % 2][:, :], mem[:, t, :], ACT.Square, accum_out=sumsq[:, t:t + 1]))
            def mem_apply(act, b):
                mscale.wait(act, b)
                sq.wait(act, b)
                for t in range(T):
                    mem_n.on(act.activation(mem[:, t, :], mem[:, t, :], ACT.Copy, scale=mem_scale[:, t:t + 1]))

            def load_mask(act, b):
                mask_f.wait(act, b - 1)
                mask_in.on(act.dma_start(mask_u8[:, :], io["mask_BxS2_bk0"][b, :].rearrange("(a s) -> a s", a=1).to_broadcast([P, S])))

            def first_loads(sp):
                load_mem(sp, 0)
                load_x(sp, 0)

            def first_constants(pool):
                built.on(pool.memset(head_row[:, :, :].bitcast(F32), 0.0))
                built.on(pool.memset(minus_row[:, :, :].bitcast(F32), 0.0))
                pool.memset(one_in_d[:, :], 1.0 / D)
                pool.memset(rms_eps[:, :], 1e-6)
                built.on(pool.memset(ones[:, :], 1.0))
                built.wait(pool, 0, 2)
                for tile, value in ((head_row, 1.0), (minus_row, -1.0)):
                    built.on(pool.affine_select(out=tile[:, :, :], in_=tile[:, :, :], compare_op=ALU.not_equal, fill=value,
                                                base=0, pattern=[[-1, H], [0, P]], channel_multiplier=1))
                mem_power(pool, 0)
                x_power(pool, 0)

            def first_memory(act):
                load_mask(act, 0)
                squares(act, 0)
                mem_apply(act, 0)

            def first_norm(dve):
                self.norm_stats(dve, N, 0, x)
                self.norm_apply(dve, N, 0, x, n_scale, nscale)
            columns = lambda dram, n: [(dram[i, :, :].rearrange("(c p) h -> p c h", p=P), i * HD) for i in range(n)]
            self.load_weights("bw", [
                ("scale", columns(io["L0_xattn_q_w"], H), H * HD, qw),
                ("scale", columns(io["L0_xattn_kv_w"].rearrange("a k d h -> (a k) d h"), 2), 2 * HD, kvw),
                ("keep", [(io["L0_xattn_out_w"].rearrange("n h d -> h n d"), 0)], D, ow)],
                (res, p_f, enc_f), {"sp": first_loads, "pool": first_constants, "act": first_memory, "dve": first_norm}, io["L0_xattn_rms_scale"])
            KV, XT, KT, Q = C, C + 2, 2 * C + 2, 2 * C + 3
            first = Ring(self.banks(ctx, "b_p", 3),
                         [(memT_lo, c) for c in range(C)] + [(k_swap, 1), (k_swap, 3)] + [(xT_lo, c) for c in range(C)]
                         + [(k_lo, 0)] + [(q_swap, 2 * h + 1) for h in range(H)], B)
            order = [("st", i) for i in range(2 * T)]
            maxima = {h: [(), (), (0, 1), (2, 3)] if h == 1 else [(0,), (1,), (2,), (3,)] for h in range(1, H)}
            for h in range(1, H):
                for i in range(T):
                    order += [("st", (h + 1) * T + i)] if h < H - 1 else []
                    order += [("top", (h - 1) * T + t) for t in maxima[h][i]]
                    order += [("rrow", 0)] if (h, i) == (H - 1, 1) else []
            order += [("spread", h) for h in range(H)] + [("out", 0), ("out", 1), ("top", (H - 1) * T), ("out", 2)]
            order += [("top", (H - 1) * T + i) for i in (1, 2)] + [("out", 3), ("top", (H - 1) * T + 3), ("row", 0)]
            reader = {"top": (top_sb, 0), "row": (row_sb, 0), "st": (p_exp, 1), "rrow": (rsum_lo, 1), "spread": (enc_n, 1), "out": (x2_sb, 1)}
            second = Ring(self.banks(ctx, "b_r", 3), [(reader[kind][0], i, reader[kind][1]) for kind, i in order], B)
            job = {o: n for n, o in enumerate(order)}
            bank_of = lambda kind, i: second.banks[job[kind, i] % 3]
            enc_bank = self.banks(ctx, "b_enc", 1)[0]
            aux = self.banks(ctx, "b_aux", 1)[0]
            MASK = T * H
            block = ctx.enter_context(nc.Block())

            @block.sync
            def _(sp):
                for tile, name in ((cos_q[:, :], "cos_q"), (sin_q[:, :], "sin_q"), (cos_k[:, :, :], "cos_k"), (sin_k[:, :, :], "sin_k")):
                    view = io[name] if name.endswith("q") else io[name].rearrange("(t p) h -> p t h", p=P)
                    params.on(sp.dma_start(tile, view))

                def step(new, old):
                    if old:
                        stored.wait(sp, old.b - 1)
                        res_in.on(sp.dma_start(res[:, :, :], self.token_rows(self.x1, old.b)))
                    if following(new, B):
                        load_mem(sp, new.b + 1)
                        load_x(sp, new.b + 1)
                    if old:
                        x2_sb.wait(sp, old.b)
                        stored.on(sp.dma_start(self.token_rows(self.x2, old.b), res[:, :, :]))
                pipeline(sp, B, step)
                stored.wait(sp, B - 1)

            @block.gpsimd
            def _(pool):
                def step(new, old):
                    def adds(h):
                        sum_ps.wait(pool, old.b if h else old.b - 1, (h - 1) % H)
                        for i in range(1, T):
                            p_exp.wait(pool, old.b, h * T + i)
                            add.on(pool.tensor_tensor(psum[:, :], p_f[:, 0, :] if i == 1 else psum[:, :], p_f[:, i, :], ALU.add))
                            if i < T - 1:
                                add.wait(pool, old.b, 3 * h + i - 1)

                    def query_low(h):
                        q_hi.wait(pool, new.b, h)
                        q_lo.on(pool.tensor_tensor(q.low[:, h, :], rope_f[h % 2][:, :], q[:, h, :].high_f32(), ALU.subtract))

                    if old:
                        adds(0)
                        adds(1)
                    if new:
                        query_low(0)
                    if old:
                        adds(2)
                    if new:
                        query_low(1)
                    if old:
                        adds(3)
                    if following(new, B):
                        mem_power(pool, new.b + 1)
                    if new:
                        query_low(2)
                    if following(new, B):
                        x_power(pool, new.b + 1)
                    if new:
                        query_low(3)
                pipeline(pool, B, step)

            @block.scalar
            def _(act):
                built.wait(act, 0)

                def step(new, old):
                    def turned(ps, hi, c, bank, free):
                        ps.wait(act, new.b, c)
                        if c == 0:
                            free(act)
                        hi.on(act.activation(nT.high[:, c, :], bank[:, :], ACT.Copy))

                    def exp(j):
                        h, i = divmod(j, T)
                        st_ps.wait(act, old.b, j)
                        if h:
                            p_lo.wait(act, old.b, j - T)
                            add.wait(act, old.b, 3 * (h - 1) + max(i, 1) - 1)
                        else:
                            p_lo.wait(act, old.b - 1, j + (H - 1) * T)
                            add.wait(act, old.b - 1, 3 * (H - 1) + max(i, 1) - 1)
                        p_exp.on(act.activation(p_f[:, i, :], bank_of("st", j)[:, :], ACT.Exp,
                                                bias=p_bias[:, i:i + 1], scale=p_scale[:, i:i + 1]))

                    def p_high(j):
                        h, i = divmod(j, T)
                        enc_ps.wait(act, old.b if h else old.b - 1, (h - 1) % H * T + i)
                        p_exp.wait(act, old.b, j)
                        p_hi.on(act.activation(p.high[:, i, :], p_f[:, i, :], ACT.Copy))

                    def enc_copy(h):
                        enc_ps.wait(act, old.b, h * T + T - 1)
                        enc_sb.on(act.activation(enc_f[:, h, :], enc_bank[:, :], ACT.Copy))

                    def query_high(h):
                        if old:
                            st_ps.wait(act, old.b, h * T + T - 1)
                        q_rope.wait(act, new.b, h)
                        q_hi.on(act.activation(q.high[:, h, :], rope_f[h % 2][:, :], ACT.Copy))

                    def memory_high(c):
                        turned(memT_ps, memT_hi, c, first.banks[c % 3], lambda e: q_ps.wait(e, new.b - 1))

                    if old:
                        mask_sb.wait(act, old.b)
                    if new:
                        memory_high(0)
                        memory_high(1)
                    for i in range(T):
                        if old:
                            exp(i)
                        if new and i < 2:
                            memory_high(i + 2)
                        if old:
                            p_high(i)
                    if new:
                        for g in range(2):
                            kv_ps.wait(act, new.b, g)
                            v_hi.on(act.activation(v[new.par].high[:, 2 * g:2 * g + 2, :],
                                                   first.banks[(KV + g) % 3][:, :].rearrange("p (t n) -> p t n", t=2)[:, :, HD:2 * HD],
                                                   ACT.Copy))
                    for i in range(T):
                        if old:
                            exp(T + i)
                            p_high(T + i)
                        if new:
                            turned(xT_ps, xT_hi, i, first.banks[(XT + i) % 3], lambda e: kv_ps.wait(e, new.b))
                    if old:
                        enc_copy(0)
                    if new:
                        kT_ps.wait(act, new.b)
                        k_hi.on(act.activation(k[new.par].high[:, :], first.banks[KT % 3][:, :], ACT.Copy))
                    if following(new, B):
                        load_mask(act, new.b + 1)
                    for h in range(1, H):
                        for i in range(T):
                            if old and h < H - 1:
                                exp((h + 1) * T + i)
                            if new and h < H - 1 and i == T - 1:
                                query_high(h)
                            if old and h < H - 1 and i == T - 1:
                                enc_copy(h)
                            if old and h < H - 1:
                                p_high((h + 1) * T + i)
                            if new and h == 1 and i == 1:
                                query_high(0)
                    if following(new, B):
                        squares(act, new.b + 1)
                    if old:
                        rrow_ps.wait(act, old.b)
                        spread_ps.wait(act, old.b - 1)
                        rsum_hi.on(act.activation(rsum_s.high[:, :], bank_of("rrow", 0)[0:H, :], ACT.Copy))
                        enc_copy(H - 1)
                        for h in range(H):
                            enc_n.wait(act, old.b, h)
                            if h == 0:
                                out_ps.wait(act, old.b - 1)
                            enc_hi.on(act.activation(enc.high[:, h, :], enc_f[:, h, :], ACT.Copy))
                    if following(new, B):
                        mem_apply(act, new.b + 1)
                    if new:
                        query_high(H - 1)
                pipeline(act, B, step)

            @block.vector
            def _(dve):
                built.wait(dve, 0)

                def step(new, old):
                    def turned(hi, lo, c, bank):
                        hi.wait(dve, new.b, c)
                        lo.on(dve.tensor_tensor(nT.low[:, c, :], bank[:, :], nT[:, c, :].high_f32(), ALU.subtract))

                    def top_logits(h, tiles):
                        if not tiles:
                            return
                        j = h * T + tiles[0]
                        n = len(tiles)
                        earlier = j + n - 5
                        top_sb.wait(dve, new.b if earlier >= 0 else new.b - 1, earlier % (T * H))
                        top_ps.wait(dve, new.b, j + n - 1)
                        dve.memset(carrier[:, j % 4:j % 4 + 1], 0.0)
                        for i in range(j, j + n):
                            top_sb.on(dve.tensor_tensor_reduce(out=unused[i % 4][:, :], in0=bank_of("top", i)[:, :], in1=mask_row[:, :],
                                                               scale=1.0, scalar=-3e38, op0=ALU.add, op1=ALU.max,
                                                               accum_out=top[:, i % T, h:h + 1]))

                    def keys(g):
                        v_hi.wait(dve, new.b, g)
                        if isinstance(new.b, int) and new.b == 0 and g == 0:
                            params.wait(dve, 0)
                        bank = first.banks[(KV + g) % 3][:, :].rearrange("p (t n) -> p t n", t=2)
                        tiles, half = slice(2 * g, 2 * g + 2), HD // 2
                        v_lo.on(dve.tensor_tensor(v[new.par].low[:, tiles, :], bank[:, :, HD:2 * HD], v[new.par][:, tiles, :].high_f32(), ALU.subtract))
                        swap = rope_swap[:, g * 2 * HD:(g + 1) * 2 * HD].rearrange("p (t n) -> p t n", t=2)
                        k_cos.on(dve.tensor_tensor(k_f[:, tiles, :], bank[:, :, 0:HD], cos_k[:, tiles, :], ALU.mult))
                        q_rope.wait(dve, new.b - 1)
                        k_swap.on(dve.tensor_tensor(swap[:, :, 0:half], bank[:, :, half:HD], sin_k[:, tiles, 0:half], ALU.mult))
                        k_swap.on(dve.tensor_tensor(swap[:, :, half:HD], bank[:, :, 0:half], sin_k[:, tiles, half:HD], ALU.mult))
                        k_cos.wait(dve, new.b, g)
                        k_swap.wait(dve, new.b, 2 * g + 1)
                        k_rope.on(dve.tensor_tensor(k_f[:, tiles, :], k_f[:, tiles, :], swap, ALU.add))

                    def p_low(j):
                        h, i = divmod(j, T)
                        p_hi.wait(dve, old.b, j)
                        p_lo.on(dve.tensor_tensor(p.low[:, i, :], p_f[:, i, :], p[:, i, :].high_f32(), ALU.subtract))

                    def query(h):
                        q_ps.wait(dve, new.b, h)
                        bank, half = first.banks[(Q + h) % 3], HD // 2
                        q_lo.wait(dve, new.b if h >= 2 else new.b - 1, (h - 2) % H)
                        q_cos.on(dve.tensor_tensor(rope_f[h % 2][:, :], bank[:, :], cos_q[:, :], ALU.mult))
                        if h:
                            q_rope.wait(dve, new.b, h - 1)
                        else:
                            k_rope.wait(dve, new.b)
                        q_swap.on(dve.tensor_tensor(rope_swap[0:half, :], bank[half:P, :], sin_q[half:P, :], ALU.mult))
                        q_swap.on(dve.tensor_tensor(rope_swap[half:P, :], bank[0:half, :], sin_q[0:half, :], ALU.mult))
                        q_cos.wait(dve, new.b, h)
                        q_swap.wait(dve, new.b, 2 * h + 1)
                        q_rope.on(dve.tensor_tensor(rope_f[h % 2][:, :], rope_f[h % 2][:, :], rope_swap[:, :], ALU.add))

                    def enc_low(h):
                        enc_hi.wait(dve, old.b, h)
                        enc_lo.on(dve.tensor_tensor(enc.low[:, h, :], enc_f[:, h, :], enc[:, h, :].high_f32(), ALU.subtract))

                    def memory_low(c):
                        turned(memT_hi, memT_lo, c, first.banks[c % 3])

                    def enc_norm(h):
                        spread_ps.wait(dve, old.b, h)
                        enc_sb.wait(dve, old.b, h)
                        enc_n.on(dve.tensor_tensor(enc_f[:, h, :], bank_of("spread", h)[:, :], enc_f[:, h, :], ALU.mult))

                    def residual(t):
                        out_ps.wait(dve, old.b, t)
                        x2_sb.on(dve.tensor_tensor(res[:, t, :], bank_of("out", t)[:, :], res[:, t, :], ALU.add))

                    if new:
                        memory_low(0)
                        memory_low(1)
                    for i in range(T):
                        if new and i < 2:
                            memory_low(i + 2)
                        if old:
                            p_low(i)
                    if new:
                        for g in range(2):
                            keys(g)
                    for i in range(T):
                        if old:
                            p_low(T + i)
                        if new:
                            turned(xT_hi, xT_lo, i, first.banks[(XT + i) % 3])
                    if new:
                        k_hi.wait(dve, new.b)
                        k_lo.on(dve.tensor_tensor(k[new.par].low[:, :], first.banks[KT % 3][:, :], k[new.par][:, :].high_f32(), ALU.subtract))
                        mask_in.wait(dve, new.b)
                        top_sb.wait(dve, new.b - 1)
                        mask_max.wait(dve, new.b - 1)
                        mask_ps.wait(dve, new.b - 1)
                        mask_f.on(dve.tensor_scalar(mask_row[:, :], mask_u8[:, :], -1.0, BIG, ALU.add, ALU.mult))
                        mask_f.wait(dve, new.b)
                        mask_sb.wait(dve, new.b - 1)
                        mask_max.on(dve.tensor_reduce(mask_any[:, :], mask_row[:, :], mybir.AxisListType.X, ALU.max))
                        query(0)
                    for h in range(1, H):
                        for i in range(T):
                            if new and i >= 2 and h < H - 1:
                                top_logits(h - 1, maxima[h][i])
                            if old and h < H - 1:
                                p_low((h + 1) * T + i)
                            if old and h == H - 1 and i == 1:
                                sum_ps.wait(dve, old.b)
                                if new:
                                    mask_ps.wait(dve, new.b)
                                rsum_f.on(dve.reciprocal(rsum[:, :, :], aux[:, 0:T * H].rearrange("p (t h) -> p t h", t=T)))
                            if new and h == H - 1 and i == 1:
                                mask_ps.wait(dve, new.b)
                                mask_max.wait(dve, new.b)
                                if old:
                                    p_exp.wait(dve, old.b)
                                mask_sb.on(dve.tensor_scalar(p_scale[:, :], aux[:, MASK:MASK + T], 1.0 / BIG, 1.0, ALU.mult, ALU.add))
                                mask_sb.on(dve.tensor_scalar(p_bias[:, :], aux[:, MASK:MASK + T], mask_any[:, 0:1], None, ALU.subtract))
                            if old and h == H - 1 and i == 2:
                                rsum_hi.wait(dve, old.b)
                                rsum_lo.on(dve.tensor_tensor(rsum_s.low[:, :], bank_of("rrow", 0)[0:H, :], rsum_s[:, :].high_f32(), ALU.subtract))
                            if new and (i < 2 or h == H - 1):
                                top_logits(h - 1, maxima[h][i])
                            if following(new, B) and h == 2 and i < 2:
                                self.norm_tile(dve, N, new.b + 1, x, i)
                            if following(new, B) and h == 3 and i == 1:
                                self.norm_tile(dve, N, new.b + 1, x, 2)
                                self.norm_tile(dve, N, new.b + 1, x, 3)
                                self.norm_variance(dve, N, new.b + 1)
                            if new and h < H - 1 and i == 1:
                                query(h)
                    if old:
                        enc_norm(0)
                        for h in range(1, H):
                            enc_norm(h)
                            enc_low(h - 1)
                        enc_low(H - 1)
                        res_in.wait(dve, old.b)
                    if new:
                        query(H - 1)
                    if old:
                        residual(0)
                    if following(new, B):
                        self.norm_apply(dve, N, new.b + 1, x, n_scale, nscale, tiles=(0, 1))
                    if old:
                        residual(1)
                    if new:
                        top_logits(H - 1, (0,))
                    if following(new, B):
                        self.norm_apply(dve, N, new.b + 1, x, n_scale, nscale, tiles=(2, 3))
                    if old:
                        residual(2)
                    if new:
                        top_logits(H - 1, (1, 2))
                        top_logits(H - 1, (3,))
                        row_ps.wait(dve, new.b)
                        row_sb.on(dve.tensor_copy(top_row[:, :], bank_of("row", 0)[0:H, :]))
                    if old:
                        residual(3)
                pipeline(dve, B, step)

            @block.tensor
            def _(pe):
                built.wait(pe, 0)

                def step(new, old):
                    s = new.b if new else old.b + 1
                    take = lambda kind, i: second.take(pe, s, job[kind, i])

                    def turn_memory(c):
                        bank = first.take(pe, s, c)
                        if c == 0:
                            mem_n.wait(pe, new.b)
                        memT_ps.on(self.turn(pe, bank, mem, c))

                    def turn_x(c):
                        bank = first.take(pe, s, XT + c)
                        if c == 0:
                            N.normed.wait(pe, new.b)
                        xT_ps.on(self.turn(pe, bank, x, c))

                    def keys_values(g):
                        bank = first.take(pe, s, KV + g)
                        for i in range(2):
                            t = 2 * g + i
                            for c in range(C):
                                if t == 0:
                                    memT_lo.wait(pe, new.b, c)
                                mm = product(pe, bank[:, i * 2 * HD:(i + 1) * 2 * HD], nT[:, c, t * P:(t + 1) * P], kvw[:, c, :], c == 0, c == C - 1)
                        kv_ps.on(mm)

                    def turn_keys():
                        bank = first.take(pe, s, KT)
                        k_rope.wait(pe, new.b)
                        for t in range(T):
                            mm = pe.transpose(bank[:, t * P:(t + 1) * P], k_f[:, t, :], self.ident[:, :])
                        kT_ps.on(mm)

                    def queries(h):
                        bank = first.take(pe, s, Q + h)
                        for c in range(C):
                            if h == 0:
                                xT_lo.wait(pe, new.b, c)
                            mm = product(pe, bank[:, :], qw[:, c, h * HD:(h + 1) * HD], nT[:, c, :], c == 0, c == C - 1)
                        q_ps.on(mm)

                    def top_logits(h, tiles):
                        for t in tiles:
                            bank = take("top", h * T + t)
                            q_hi.wait(pe, new.b, h)
                            k_hi.wait(pe, new.b)
                            top_ps.on(pe.matmul(bank[:, :], q.high[:, h, t * P:(t + 1) * P], k[new.par].high[:, :], start=True, stop=True))

                    def logits(h, i):
                        j = h * T + i
                        bank = take("st", j)
                        if j == 0:
                            row_sb.wait(pe, old.b)
                            k_lo.wait(pe, old.b)
                        if i == 0:
                            q_lo.wait(pe, old.b, h)
                        pe.matmul(bank[:, :], minus_row[:, h, :], top_row[:, :], start=True, stop=False)
                        st_ps.on(product(pe, bank[:, :], k[old.par][:, i * P:(i + 1) * P], q[:, h, :], False, True))

                    def encode(h, i):
                        if i == 0:
                            enc_sb.wait(pe, old.b if h else old.b - 1, (h - 1) % H)
                            v_lo.wait(pe, old.b)
                        p_lo.wait(pe, old.b, h * T + i)
                        enc_ps.on(product(pe, enc_bank[:, :], v[old.par][:, i, :], p[:, i, :], i == 0, i == T - 1))

                    def total(h):
                        if h == 0:
                            rsum_f.wait(pe, old.b - 1)
                            mask_sb.wait(pe, old.b)
                        add.wait(pe, old.b, 3 * h + 2)
                        for t in range(T):
                            mm = pe.matmul(aux[:, t * H + h:t * H + h + 1], psum[:, t * P:(t + 1) * P], ones[:, :], start=True, stop=True)
                        sum_ps.on(mm)

                    def spread(h):
                        bank = take("spread", h)
                        if h == 0:
                            rsum_lo.wait(pe, old.b)
                        pe.matmul(bank[:, :], head_row[:, h, :], rsum_s.high[:, :], start=True, stop=False)
                        spread_ps.on(pe.matmul(bank[:, :], head_row[:, h, :], rsum_s.low[:, :], start=False, stop=True))

                    def out(t, between=lambda h: None):
                        bank = take("out", t)
                        for h in range(H):
                            between(h)
                            if t == 0:
                                enc_lo.wait(pe, old.b, h)
                            mm = product(pe, bank[:, :], enc[:, h, t * P:(t + 1) * P], ow[:, h, :], h == 0, h == H - 1)
                        out_ps.on(mm)

                    def mask_columns():
                        mask_f.wait(pe, new.b)
                        mask_sb.wait(pe, new.b - 1)
                        for i in range(T):
                            mm = pe.matmul(aux[:, MASK + i:MASK + i + 1], mask_row[0:1, i * P:(i + 1) * P], ones[0:1, :], start=True, stop=True)
                        mask_ps.on(mm)

                    def top_rows():
                        bank = take("row", 0)
                        top_sb.wait(pe, new.b)
                        for t in range(T):
                            mm = pe.matmul(bank[0:H, t * P:(t + 1) * P], top[:, t, :], self.ident[:, :], start=True, stop=True)
                        row_ps.on(mm)

                    def sum_rows():
                        bank = take("rrow", 0)
                        rsum_f.wait(pe, old.b)
                        for t in range(T):
                            mm = pe.matmul(bank[0:H, t * P:(t + 1) * P], rsum[:, t, :], self.ident[:, :], start=True, stop=True)
                        rrow_ps.on(mm)

                    if new:
                        turn_memory(0)
                        turn_memory(1)
                    for i in range(T):
                        if old:
                            logits(0, i)
                        if new and i < 2:
                            turn_memory(i + 2)
                    if new:
                        keys_values(0)
                        keys_values(1)
                    for i in range(T):
                        if old:
                            logits(1, i)
                            encode(0, i)
                            if i == 1:
                                total(0)
                        if new:
                            turn_x(i)
                    if new:
                        turn_keys()
                        queries(0)
                    for h in range(1, H):
                        last = h == H - 1
                        for i in range(T):
                            if last and new and i == 0:
                                mask_columns()
                            if last and new and i != 1:
                                top_logits(h - 1, maxima[h][i])
                            if last and new and i == 1:
                                top_logits(h - 1, maxima[h][1])
                            if last and old and i == 1:
                                total(h)
                            if old and not last:
                                logits(h + 1, i)
                            if old:
                                encode(h, i)
                            if new and not last:
                                top_logits(h - 1, maxima[h][i])
                            if i == 1 and not last:
                                if old:
                                    total(h)
                                if new:
                                    queries(h)
                            if i == 1 and last and old:
                                sum_rows()
                    if old:
                        for h in range(H):
                            spread(h)
                    if new:
                        queries(H - 1)
                    if old:
                        out(0)
                        out(1)
                    if new:
                        top_logits(H - 1, (0,))
                    if old:
                        out(2)
                    if new:
                        top_logits(H - 1, (1, 2))

                    def last_maxima(h):
                        if new and h == 1:
                            top_logits(H - 1, (3,))
                        if new and h == H - 1:
                            top_rows()
                    if old:
                        out(3, last_maxima)
                    else:
                        last_maxima(1)
                        last_maxima(H - 1)
                pipeline(pe, B, step)

    def phase_c(self, state):
        nc, io, B, C, T, D, S = self.nc, self.io, self.B, self.C, self.T, self.D, self.S
        GATES = "icf"
        with Scope(self.nc) as ctx:
            w = {g: self.split(ctx, f"c_w{g}", [P, C, D]) for g in GATES}
            u = {g: self.split(ctx, f"c_u{g}", [P, C, D]) for g in GATES}
            sb = lambda n, s, d=F32: self.sb(ctx, f"c_{n}", s, d)
            ev = lambda n, per=1, unit=1: Event(ctx, nc, f"c_{n}", per, unit)
            x = sb("x", [P, T, D])
            nT = [self.split(ctx, f"c_nT{i}", [P, C, S]) for i in range(2)]
            c_f = sb("c_f", [P, C, S])
            gate = sb("gate", [P, 2, 3, S])
            bias = sb("bias", [P, 3, C])
            c_in = sb("c_in", [P, C])
            N = self.norm_events(ctx, "c_ln")
            params, zero, start_f, start_hi, start = ev("params", 4, 16), ev("zero"), ev("start_f", C), ev("start_hi"), ev("start")
            xT_ps, xT_hi, xT_lo = ev("xT_ps", C), ev("xT_hi", C), ev("xT_lo", C)
            gate_ps, gate_sb = ev("gate_ps", 3 * C), ev("gate_sb", 3 * C)
            ig, fc, c_new, c_hi, c_lo = ev("ig", C), ev("fc", C), ev("c_new", C), ev("c_hi", C), ev("c_lo", C)

            def load(sp, b):
                xT_ps.wait(sp, b - 1)
                N.loaded.on(sp.dma_start(x[:, :, :], self.token_rows(self.x2, b)))

            def norm(dve, b):
                self.norm_stats(dve, N, b, x)
                self.norm_apply(dve, N, b, x, N.scale, N.rstd)

            def first_loads(sp):
                load(sp, 0)
                with nc.allow_non_contiguous_dma(reason="small parameters, once"):
                    for i, g in enumerate(GATES):
                        params.on(sp.dma_start(bias[:, i, :], io[f"L0_ffn_b{g}"].rearrange("(c p) -> p c", p=P)))
                    params.on(sp.dma_start(c_in[:, :], io["L0_ffn_in_c"].rearrange("(c p) -> p c", p=P)))

            def first_high(act):
                start_f.wait(act, 0)
                start_hi.on(act.activation(state[1].high[:, :, :], c_f[:, :, :], ACT.Copy))

            def first_state(dve):
                zero.on(dve.memset(c_f[:, :, :], 0.0))
                norm(dve, 0)
                zero.wait(dve, 0)
                params.wait(dve, 0)
                for c in range(C):
                    start_f.on(dve.tensor_scalar(c_f[:, c, :], c_f[:, c, :], c_in[:, c:c + 1], None, ALU.add))
                start_hi.wait(dve, 0)
                start.on(dve.tensor_tensor(state[1].low[:, :, :], c_f[:, :, :], state[1][:, :, :].high_f32(), ALU.subtract))
            stage = [sb("stage0", [P, C, D]), sb("stage1", [P, C, D]), gate[:, :, :, :].rearrange("p a g s -> p (a g) s")[:, 0:C, :]]
            self.load_weights("cw", [("turn", io[f"L0_ffn_{k}{g}"], D, t[g]) for g in GATES for k, t in (("w", w), ("u", u))], stage,
                              {"sp": first_loads, "pool": lambda pool: self.norm_power(pool, N, 0), "act": first_high, "dve": first_state})
            turning = Ring(self.banks(ctx, "c_t", 2), [(xT_lo, c) for c in range(C)], self.B)
            gating = Ring(self.banks(ctx, "c_g", 6), [(gate_sb, n) for n in range(3 * C)], self.B)
            block = ctx.enter_context(nc.Block())

            @block.sync
            def _(sp):
                def step(new, old):
                    if following(new, B):
                        load(sp, new.b + 1)
                pipeline(sp, B, step)

            @block.gpsimd
            def _(pool):
                def step(new, old):
                    if following(new, B):
                        self.norm_power(pool, N, new.b + 1)
                pipeline(pool, B, step)

            @block.scalar
            def _(act):
                params.wait(act, 0)

                def step(new, old):
                    def split_new(j):
                        c_new.wait(act, old.b, j)
                        c_hi.on(act.activation(state[old.par].high[:, j, :], c_f[:, j, :], ACT.Copy))
                    if new:
                        for c in range(C):
                            xT_ps.wait(act, new.b, c)
                            xT_hi.on(act.activation(nT[new.par].high[:, c, :], turning.banks[c % 2][:, :], ACT.Copy))
                    if old:
                        for j in range(C):
                            for i, g in enumerate(GATES):
                                gate_ps.wait(act, old.b, 3 * j + i)
                                if i == 0:
                                    c_new.wait(act, old.b if j >= 2 else old.b - 1, (j - 2) % C)
                                gate_sb.on(act.activation(gate[:, j % 2, i, :], gating.banks[(3 * j + i) % 6][:, :],
                                                          ACT.Tanh if g == "c" else ACT.Sigmoid, bias=bias[:, i, j:j + 1]))
                                if j and i == 0:
                                    split_new(j - 1)
                        split_new(C - 1)
                pipeline(act, B, step)

            @block.vector
            def _(dve):
                def step(new, old):
                    if new:
                        for c in range(C):
                            xT_hi.wait(dve, new.b, c)
                            xT_lo.on(dve.tensor_tensor(nT[new.par].low[:, c, :], turning.banks[c % 2][:, :],
                                                       nT[new.par][:, c, :].high_f32(), ALU.subtract))

                    def update(j):
                        slot = gate[:, j % 2, :, :]
                        gate_sb.wait(dve, old.b, 3 * j + 1)
                        ig.on(dve.tensor_tensor(slot[:, 0, :], slot[:, 0, :], slot[:, 1, :], ALU.mult))
                        gate_sb.wait(dve, old.b, 3 * j + 2)
                        fc.on(dve.tensor_tensor(slot[:, 2, :], slot[:, 2, :], c_f[:, j, :], ALU.mult))
                        ig.wait(dve, old.b, j)
                        fc.wait(dve, old.b, j)
                        c_new.on(dve.tensor_tensor(c_f[:, j, :], slot[:, 0, :], slot[:, 2, :], ALU.add))

                    def split_new(j):
                        c_hi.wait(dve, old.b, j)
                        c_lo.on(dve.tensor_tensor(state[old.par].low[:, j, :], c_f[:, j, :], state[old.par][:, j, :].high_f32(), ALU.subtract))
                    if old:
                        update(0)
                        update(1)
                        split_new(0)
                    if following(new, B):
                        norm(dve, new.b + 1)
                    if old:
                        for j in range(2, C):
                            update(j)
                            split_new(j - 1)
                        split_new(C - 1)
                pipeline(dve, B, step)

            @block.tensor
            def _(pe):
                start.wait(pe, 0)

                def step(new, old):
                    def turn_x(c):
                        if c == 0:
                            N.normed.wait(pe, new.b)
                        xT_ps.on(self.turn(pe, turning.take(pe, new.b, c), x, c))

                    def part(j, weights, source, first):
                        for i, g in enumerate(GATES):
                            n = 3 * j + i
                            bank = gating.take(pe, old.b, n) if first else gating.banks[n % 6]
                            for c in range(C):
                                mm = product(pe, bank[:, :], weights[g][:, c, j * P:(j + 1) * P], source[:, c, :],
                                             first and c == 0, not first and c == C - 1)
                            if not first:
                                gate_ps.on(mm)
                            if new and first and j == 0 and i < 2:
                                turn_x(2 * i)
                                turn_x(2 * i + 1)
                    if old:
                        xT_lo.wait(pe, old.b)
                        part(0, w, nT[old.par], True)
                    else:
                        for c in range(C):
                            turn_x(c)
                    if old:
                        c_lo.wait(pe, old.b - 1)
                        part(0, u, state[1 - old.par], False)
                        for j in range(1, C):
                            part(j, w, nT[old.par], True)
                            part(j, u, state[1 - old.par], False)
                pipeline(pe, B, step)

    def phase_d(self, c_last):
        nc, io, B, C, T, D, S = self.nc, self.io, self.B, self.C, self.T, self.D, self.S
        X = 4
        with Scope(self.nc) as ctx:
            wo, uo = (self.split(ctx, f"d_{n}", [P, C, D]) for n in ("wo", "uo"))
            sb = lambda n, s, d=F32: self.sb(ctx, f"d_{n}", s, d)
            ev = lambda n, per=1, unit=1: Event(ctx, nc, f"d_{n}", per, unit)
            x = [sb(f"x{i}", [P, T, D]) for i in range(X)]
            n = sb("n", [P, T, D])
            nT = [self.split(ctx, f"d_nT{i}", [P, C, S]) for i in range(2)]
            base = sb("base", [P, T, D])
            bo = sb("bo", [P, D])
            y = sb("y", [P, 2, D])
            N = self.norm_events(ctx, "d_ln")
            stored = ev("stored", 1, 16)
            bo_in, base_ps, base_sb = ev("bo_in", 1, 16), ev("base_ps", T), ev("base_sb", T)
            xT_ps, xT_hi, xT_lo = ev("xT_ps", C), ev("xT_hi", C), ev("xT_lo", C)
            y_ps, y_sb, y_tanh, out_sb = ev("y_ps", T), ev("y_sb", T), ev("y_tanh", T), ev("out_sb", T)

            def load(sp, b, tile):
                N.loaded.wait(sp, b - 1)
                N.loaded.on(sp.dma_start(tile[:, :, :], self.token_rows(self.x2, b)))

            def first_loads(sp):
                load(sp, 0, x[0])
                bo_in.on(sp.dma_start(bo[:, :], io["L0_ffn_bo"].rearrange("(a n) -> a n", a=1).to_broadcast([P, D])))

            def apply(dve, b, tile):
                xT_ps.wait(dve, b - 1)
                self.norm_apply(dve, N, b, tile, N.scale, N.rstd, n)

            def first_norm(dve):
                self.norm_stats(dve, N, 0, x[0])
                apply(dve, 0, x[0])
            self.load_weights("dw", [("turn", io[f"L0_ffn_{n}"], D, t) for n, t in (("uo", uo), ("wo", wo))], (x[1], x[2]),
                              {"sp": first_loads, "pool": lambda pool: self.norm_power(pool, N, 0), "dve": first_norm})
            turning = Ring(self.banks(ctx, "d_t", 4), [(xT_lo, c) for c in range(C)], self.B)
            output = Ring(self.banks(ctx, "d_y", 4), [(y_sb, t) for t in range(T)], self.B)
            block = ctx.enter_context(nc.Block())

            @block.sync
            def _(sp):
                load(sp, 1, x[1])

                def step(new, old):
                    if following(new, B, 2):
                        stored.wait(sp, new.b - 2)
                        load(sp, new.b + 2, x[(new.par + 2) % X])
                    if old:
                        out_sb.wait(sp, old.b)
                        stored.on(sp.dma_start(self.token_rows(self.out, old.b), x[old.par][:, :, :]))
                pipeline(sp, B, step, X, ahead=2)
                stored.wait(sp, B - 1)

            @block.gpsimd
            def _(pool):
                def step(new, old):
                    if following(new, B):
                        self.norm_power(pool, N, new.b + 1)
                    if old:
                        for t in range(T):
                            y_tanh.wait(pool, old.b, t)
                            out_sb.on(pool.tensor_tensor(x[old.par][:, t, :], x[old.par][:, t, :], y[:, t % 2, :], ALU.add))
                pipeline(pool, B, step, X)

            @block.scalar
            def _(act):
                def step(new, old):
                    for c in range(C):
                        if new:
                            xT_ps.wait(act, new.b, c)
                            xT_hi.on(act.activation(nT[new.par % 2].high[:, c, :], turning.banks[c][:, :], ACT.Copy))
                    for t in range(T):
                        if old:
                            y_sb.wait(act, old.b, t)
                            y_tanh.on(act.activation(y[:, t % 2, :], y[:, t % 2, :], ACT.Tanh))
                pipeline(act, B, step, X)

            @block.vector
            def _(dve):
                bo_in.wait(dve, 0)
                for t in range(T):
                    base_ps.wait(dve, 0, t)
                    base_sb.on(dve.tensor_tensor(base[:, t, :], output.banks[t][:, :], bo[:, :], ALU.add))
                base_sb.wait(dve, 0)

                def step(new, old):
                    if new:
                        for c in range(C):
                            xT_hi.wait(dve, new.b, c)
                            xT_lo.on(dve.tensor_tensor(nT[new.par % 2].low[:, c, :], turning.banks[c][:, :],
                                                       nT[new.par % 2][:, c, :].high_f32(), ALU.subtract))
                    if following(new, B):
                        self.norm_stats(dve, N, new.b + 1, x[(new.par + 1) % X])
                    for t in range(T):
                        if old:
                            y_ps.wait(dve, old.b, t)
                            out_sb.wait(dve, old.b if t >= 2 else old.b - 1, (t - 2) % T)
                            y_sb.on(dve.tensor_tensor(y[:, t % 2, :], output.banks[t][:, :], base[:, t, :], ALU.add))
                        if following(new, B) and t == 0:
                            apply(dve, new.b + 1, x[(new.par + 1) % X])
                pipeline(dve, B, step, X)

            @block.tensor
            def _(pe):
                for t in range(T):
                    for c in range(C):
                        mm = product(pe, output.banks[t][:, :], c_last[:, c, t * P:(t + 1) * P], uo[:, c, :], c == 0, c == C - 1)
                    base_ps.on(mm)

                def step(new, old):
                    if new:
                        N.normed.wait(pe, new.b)
                        for c in range(C):
                            xT_ps.on(self.turn(pe, turning.take(pe, new.b, c), n, c))
                    if old:
                        for t in range(T):
                            if isinstance(old.b, int) and old.b == 0:
                                base_sb.wait(pe, 0, t)
                            bank = output.take(pe, old.b, t)
                            for c in range(C):
                                if t == 0:
                                    xT_lo.wait(pe, old.b, c)
                                mm = product(pe, bank[:, :], nT[old.par % 2][:, c, t * P:(t + 1) * P], wo[:, c, :], c == 0, c == C - 1)
                            y_ps.on(mm)
                pipeline(pe, B, step, X)

    def run(self):
        with Scope(self.nc) as ctx:
            self.constants(ctx)
            self.phase_a()
            self.phase_b()
            self.phase_cd(ctx)

    def phase_cd(self, ctx):
        state = [self.split(ctx, f"state{i}", [P, self.C, self.S]) for i in range(2)]
        self.phase_c(state)
        self.phase_d(state[(self.B - 1) % 2])


def tables(T, S, H):
    f32 = np.float32
    timescale = f32(10000.0) ** (f32(2.0 / H) * np.arange(H // 2, dtype=f32))
    angle = lambda start, n: (np.arange(start, start + n, dtype=f32)[:, None] / timescale).astype(f32)
    aq, ak, scale = angle(S, T).T, angle(0, S), f32(H ** -0.5)
    two = np.concatenate
    return {"cos_q": two([np.cos(aq), np.cos(aq)]) * scale, "sin_q": two([np.sin(aq), -np.sin(aq)]) * scale,
            "cos_k": two([np.cos(ak), np.cos(ak)], 1), "sin_k": two([-np.sin(ak), np.sin(ak)], 1)}


_INS = ["x", "ctx_1024", "mask_BxS2_bk0", "L0_attn_Wq", "L0_attn_Wk", "L0_attn_Wv", "L0_attn_Wp", "L0_attn_bp",
        "L0_attn_conv_w", "L0_attn_conv_b", "L0_xattn_rms_scale", "L0_xattn_q_w", "L0_xattn_kv_w", "L0_xattn_out_w",
        "L0_ffn_wf", "L0_ffn_uf", "L0_ffn_bf", "L0_ffn_wi", "L0_ffn_ui", "L0_ffn_bi", "L0_ffn_wc", "L0_ffn_uc",
        "L0_ffn_bc", "L0_ffn_wo", "L0_ffn_uo", "L0_ffn_bo", "L0_ffn_in_c"]


def kernel(**inputs):
    import concourse.bacc as bacc
    from concourse.bass_utils import run_bass_kernel_spmd

    nc = bacc.Bacc("TRN2", target_bir_lowering=False, num_devices=1)
    arrays = {f"in_{n}": np.ascontiguousarray(inputs[n]) for n in _INS}
    B, S, D = inputs["x"].shape
    arrays.update({f"in_{n}": np.ascontiguousarray(t, np.float32)
                   for n, t in tables(S, inputs["ctx_1024"].shape[1], inputs["L0_xattn_q_w"].shape[2]).items()})
    io = {n[3:]: nc.dram_tensor(n, a.shape, mybir.dt.from_np(a.dtype), kind="ExternalInput").ap() for n, a in arrays.items()}
    out = nc.dram_tensor("out", (B, S, D), F32, kind="ExternalOutput").ap()
    x1, x2 = (nc.dram_tensor(n, (B, S, D), F32, kind="Internal").ap() for n in ("x1", "x2"))
    Kernel(nc, io, out, x1, x2).run()
    return run_bass_kernel_spmd(nc, [arrays], core_ids=[0]).results[0]["out"]
```
